# Optimizing a Trainium2 kernel written in Bass

```python
import numpy as np
import jax
import jax.numpy as jnp

def _softmax(x, axis=-1):
    return jax.nn.softmax(x, axis=axis)

def _gelu(x):
    return jax.nn.gelu(x, approximate=True)

def _silu(x):
    return jax.nn.silu(x)

def _sigmoid(x):
    return jax.nn.sigmoid(x)

def _layernorm(x, axis=-1, eps=1e-05):
    m = jnp.mean(x, axis=axis, keepdims=True)
    v = jnp.var(x, axis=axis, keepdims=True)
    return (x - m) / jnp.sqrt(v + eps)

def _scatter_add(tgt, idx, src, axis=0):
    return tgt.at[idx].add(src)

def _segment_sum(src, seg, n):
    return jax.ops.segment_sum(src, seg, n)
kernel_name = 'mk_decoder_postln_d1_seqx_r8_16c136'

def setup_inputs(seed: int=0):
    np.random.seed(seed)
    _w = jnp.asarray

    def _rec_inputs():
        import jax
        import jax.numpy as jnp
        _rk = jax.random.key(seed)
        x = -0.0002928 + 1 * jax.random.normal(jax.random.fold_in(_rk, 1), (16, 128, 128), jnp.float32)
        _lenS = 128 - jax.random.randint(jax.random.fold_in(_rk, 7), (16,), 0, max(1, 128 // 4) + 1, jnp.int32)
        _lenS2 = 128 - jax.random.randint(jax.random.fold_in(_rk, 8), (16,), 0, max(1, 128 // 4) + 1, jnp.int32)
        _ctx_1024P = jax.random.normal(jax.random.fold_in(_rk, 11), (16, 16, 128), jnp.float32)
        _ctx_1024c = jax.random.dirichlet(jax.random.fold_in(_rk, 511), 0.3 * jnp.ones((16,), jnp.float32), (16, 128))
        _ctx_1024t = jnp.einsum('bsk,bkd->bsd', _ctx_1024c, _ctx_1024P)
        _ctx_1024t = _ctx_1024t * jax.lax.rsqrt(jnp.mean(jnp.square(_ctx_1024t)) + 1e-12) * 0.953939
        ctx_1024 = -1.39393e-06 + 0.999914 * (_ctx_1024t + 0.3 * jax.random.normal(jax.random.fold_in(_rk, 611), (16, 128, 128), jnp.float32))
        _validS = jnp.arange(128)[None, :] < _lenS[:, None]
        _validS2 = jnp.arange(128)[None, :] < _lenS2[:, None]
        _causal = jnp.tril(jnp.ones((128, 128), dtype=bool))
        mask_BxS2_bk0 = jnp.logical_not(jnp.broadcast_to(_validS2[:, :], (16, 128)))
        return (x, ctx_1024, mask_BxS2_bk0)
    x, ctx_1024, mask_BxS2_bk0 = _rec_inputs()

    def _L0_attn_setup():
        import jax, jax.numpy as jnp
        import numpy as np
        D_MODEL = 128

        def dw_causal_conv(x, w, b):
            K = w.shape[1]
            out = jax.lax.conv_general_dilated(x, w[:, None, :], window_strides=(1,), padding=[(K - 1, 0)], feature_group_count=x.shape[1], dimension_numbers=('NCH', 'OIH', 'NCH'))
            return out + b[None, :, None]
        key = jax.random.key(seed)
        ks = jax.random.split(key, 9)
        B, L, D = (2, 1024, D_MODEL)
        s = 0.02
        return {'u': jax.random.normal(ks[0], (B, L, D), jnp.float32), 'W_in': jax.random.normal(ks[1], (D, 3 * D), jnp.float32) * s, 'b_in': jax.random.normal(ks[2], (3 * D,), jnp.float32) * s, 'short_w': jax.random.normal(ks[3], (3 * D, 3), jnp.float32) * s, 'short_b': jax.random.normal(ks[4], (3 * D,), jnp.float32) * s, 'inner_w': jax.random.normal(ks[5], (D, 4), jnp.float32) * s, 'inner_b': jax.random.normal(ks[6], (D,), jnp.float32) * s, 'W_out': jax.random.normal(ks[7], (D, D), jnp.float32) * s, 'b_out': jax.random.normal(ks[8], (D,), jnp.float32) * s}
    _L0_attn_all = _L0_attn_setup()
    _L0_attn_in = {k: v for k, v in _L0_attn_all.items() if k in ('W_in', 'b_in', 'short_w', 'short_b', 'inner_w', 'inner_b', 'W_out', 'b_out')}
    del _L0_attn_all

    def _L0_xattn_setup():
        import jax, jax.numpy as jnp
        import numpy as np
        B, S, D = (2, 256, 128)
        H, DH = (16, 64)
        INNER = H * DH
        FF = 512
        SCALE = DH ** (-0.5)
        EPS = 1e-05

        def layernorm(x, g, b):
            m = jnp.mean(x, axis=-1, keepdims=True)
            v = jnp.var(x, axis=-1, keepdims=True)
            return (x - m) * jax.lax.rsqrt(v + EPS) * g + b

        def attention(x, ctx, mask, wq, wk, wv, wo, bo):
            b, n, _ = x.shape
            j = ctx.shape[1]
            q = (x @ wq).reshape(b, n, H, DH).transpose(0, 2, 1, 3)
            k = (ctx @ wk).reshape(b, j, H, DH).transpose(0, 2, 1, 3)
            v = (ctx @ wv).reshape(b, j, H, DH).transpose(0, 2, 1, 3)
            sim = jnp.einsum('bhid,bhjd->bhij', q, k) * SCALE
            if mask is not None:
                neg = -jnp.finfo(sim.dtype).max
                sim = jnp.where(mask[:, None, None, :], neg, sim)
            attn = jax.nn.softmax(sim, axis=-1)
            out = jnp.einsum('bhij,bhjd->bhid', attn, v)
            out = out.transpose(0, 2, 1, 3).reshape(b, n, INNER)
            return out @ wo + bo
        key = jax.random.key(seed)
        ks = jax.random.split(key, 26)
        w = lambda k, shp, fan: (jax.random.normal(k, shp, jnp.float32) / np.sqrt(fan)).astype(jnp.float32)
        return {'x': jax.random.normal(ks[0], (B, S, D), jnp.float32), 'enc_output': jax.random.normal(ks[1], (B, S, D), jnp.float32), 'sa_wq': w(ks[2], (D, INNER), D), 'sa_wk': w(ks[3], (D, INNER), D), 'sa_wv': w(ks[4], (D, INNER), D), 'sa_wo': w(ks[5], (INNER, D), INNER), 'sa_bo': jnp.zeros((D,), jnp.float32), 'ca_wq': w(ks[6], (D, INNER), D), 'ca_wk': w(ks[7], (D, INNER), D), 'ca_wv': w(ks[8], (D, INNER), D), 'ca_wo': w(ks[9], (INNER, D), INNER), 'ca_bo': jnp.zeros((D,), jnp.float32), 'ln1_g': jnp.ones((D,), jnp.float32), 'ln1_b': jnp.zeros((D,), jnp.float32), 'ln2_g': jnp.ones((D,), jnp.float32), 'ln2_b': jnp.zeros((D,), jnp.float32), 'ln3_g': jnp.ones((D,), jnp.float32), 'ln3_b': jnp.zeros((D,), jnp.float32), 'fc1_w': w(ks[10], (D, FF), D), 'fc1_b': jnp.zeros((FF,), jnp.float32), 'fc2_w': w(ks[11], (FF, D), FF), 'fc2_b': jnp.zeros((D,), jnp.float32), 'tgt_mask': jax.random.bernoulli(ks[12], 0.1, (B, S)), 'src_mask': jax.random.bernoulli(ks[13], 0.1, (B, S))}
    _L0_xattn_all = _L0_xattn_setup()
    _L0_xattn_in = {k: v for k, v in _L0_xattn_all.items() if k in ('sa_wq', 'sa_wk', 'sa_wv', 'sa_wo', 'sa_bo', 'ca_wq', 'ca_wk', 'ca_wv', 'ca_wo', 'ca_bo', 'ln1_g', 'ln1_b', 'ln2_g', 'ln2_b', 'ln3_g', 'ln3_b', 'fc1_w', 'fc1_b', 'fc2_w', 'fc2_b')}
    del _L0_xattn_all

    def _L0_ffn_setup():
        import jax, jax.numpy as jnp
        import numpy as np
        EPS = 1e-05
        NUM = 16

        def _layernorm(x, gamma, beta):
            mu = jnp.mean(x, axis=-1, keepdims=True)
            var = jnp.var(x, axis=-1, keepdims=True)
            return (x - mu) * jax.lax.rsqrt(var + EPS) * gamma + beta
        key = jax.random.key(seed)
        ks = jax.random.split(key, 6)
        B, P, D = (256, 32, 128)
        s = 1.0 / np.sqrt(D)
        return {'x': jax.random.normal(ks[0], (B, P, D), dtype=jnp.float32), 'g_e': jnp.ones((NUM, D), jnp.float32), 'b_e': jnp.zeros((NUM, D), jnp.float32), 'W1_e': jax.random.normal(ks[1], (NUM, D, D), jnp.float32) * s, 'b1_e': jnp.zeros((NUM, D), jnp.float32), 'W2_e': jax.random.normal(ks[2], (NUM, D, D), jnp.float32) * s, 'b2_e': jnp.zeros((NUM, D), jnp.float32), 'g_s': jnp.ones((D,), jnp.float32), 'b_s': jnp.zeros((D,), jnp.float32), 'W1_s': jax.random.normal(ks[3], (D, D), jnp.float32) * s, 'b1_s': jnp.zeros((D,), jnp.float32), 'W2_s': jax.random.normal(ks[4], (D, D), jnp.float32) * s, 'b2_s': jnp.zeros((D,), jnp.float32)}
    _L0_ffn_all = _L0_ffn_setup()
    _L0_ffn_in = {k: v for k, v in _L0_ffn_all.items() if k in ('g_e', 'b_e', 'W1_e', 'b1_e', 'W2_e', 'b2_e', 'g_s', 'b_s', 'W1_s', 'b1_s', 'W2_s', 'b2_s')}
    del _L0_ffn_all
    return {'x': x, 'ctx_1024': ctx_1024, 'mask_BxS2_bk0': mask_BxS2_bk0, 'L0_attn_W_in': _L0_attn_in['W_in'], 'L0_attn_b_in': _L0_attn_in['b_in'], 'L0_attn_short_w': _L0_attn_in['short_w'], 'L0_attn_short_b': _L0_attn_in['short_b'], 'L0_attn_inner_w': _L0_attn_in['inner_w'], 'L0_attn_inner_b': _L0_attn_in['inner_b'], 'L0_attn_W_out': _L0_attn_in['W_out'], 'L0_attn_b_out': _L0_attn_in['b_out'], 'L0_xattn_sa_wq': _L0_xattn_in['sa_wq'], 'L0_xattn_sa_wk': _L0_xattn_in['sa_wk'], 'L0_xattn_sa_wv': _L0_xattn_in['sa_wv'], 'L0_xattn_sa_wo': _L0_xattn_in['sa_wo'], 'L0_xattn_sa_bo': _L0_xattn_in['sa_bo'], 'L0_xattn_ca_wq': _L0_xattn_in['ca_wq'], 'L0_xattn_ca_wk': _L0_xattn_in['ca_wk'], 'L0_xattn_ca_wv': _L0_xattn_in['ca_wv'], 'L0_xattn_ca_wo': _L0_xattn_in['ca_wo'], 'L0_xattn_ca_bo': _L0_xattn_in['ca_bo'], 'L0_xattn_ln1_g': _L0_xattn_in['ln1_g'], 'L0_xattn_ln1_b': _L0_xattn_in['ln1_b'], 'L0_xattn_ln2_g': _L0_xattn_in['ln2_g'], 'L0_xattn_ln2_b': _L0_xattn_in['ln2_b'], 'L0_xattn_ln3_g': _L0_xattn_in['ln3_g'], 'L0_xattn_ln3_b': _L0_xattn_in['ln3_b'], 'L0_xattn_fc1_w': _L0_xattn_in['fc1_w'], 'L0_xattn_fc1_b': _L0_xattn_in['fc1_b'], 'L0_xattn_fc2_w': _L0_xattn_in['fc2_w'], 'L0_xattn_fc2_b': _L0_xattn_in['fc2_b'], 'L0_ffn_g_e': _L0_ffn_in['g_e'], 'L0_ffn_b_e': _L0_ffn_in['b_e'], 'L0_ffn_W1_e': _L0_ffn_in['W1_e'], 'L0_ffn_b1_e': _L0_ffn_in['b1_e'], 'L0_ffn_W2_e': _L0_ffn_in['W2_e'], 'L0_ffn_b2_e': _L0_ffn_in['b2_e'], 'L0_ffn_g_s': _L0_ffn_in['g_s'], 'L0_ffn_b_s': _L0_ffn_in['b_s'], 'L0_ffn_W1_s': _L0_ffn_in['W1_s'], 'L0_ffn_b1_s': _L0_ffn_in['b1_s'], 'L0_ffn_W2_s': _L0_ffn_in['W2_s'], 'L0_ffn_b2_s': _L0_ffn_in['b2_s']}

def reference(x, ctx_1024, mask_BxS2_bk0, L0_attn_W_in, L0_attn_b_in, L0_attn_short_w, L0_attn_short_b, L0_attn_inner_w, L0_attn_inner_b, L0_attn_W_out, L0_attn_b_out, L0_xattn_sa_wq, L0_xattn_sa_wk, L0_xattn_sa_wv, L0_xattn_sa_wo, L0_xattn_sa_bo, L0_xattn_ca_wq, L0_xattn_ca_wk, L0_xattn_ca_wv, L0_xattn_ca_wo, L0_xattn_ca_bo, L0_xattn_ln1_g, L0_xattn_ln1_b, L0_xattn_ln2_g, L0_xattn_ln2_b, L0_xattn_ln3_g, L0_xattn_ln3_b, L0_xattn_fc1_w, L0_xattn_fc1_b, L0_xattn_fc2_w, L0_xattn_fc2_b, L0_ffn_g_e, L0_ffn_b_e, L0_ffn_W1_e, L0_ffn_b1_e, L0_ffn_W2_e, L0_ffn_b2_e, L0_ffn_g_s, L0_ffn_b_s, L0_ffn_W1_s, L0_ffn_b1_s, L0_ffn_W2_s, L0_ffn_b2_s):
    import jax
    import jax.numpy as jnp

    def _L0_attn_ref(u, W_in, b_in, short_w, short_b, inner_w, inner_b, W_out, b_out):
        import jax, jax.numpy as jnp
        import numpy as np
        D_MODEL = 128

        def dw_causal_conv(x, w, b):
            K = w.shape[1]
            out = jax.lax.conv_general_dilated(x, w[:, None, :], window_strides=(1,), padding=[(K - 1, 0)], feature_group_count=x.shape[1], dimension_numbers=('NCH', 'OIH', 'NCH'))
            return out + b[None, :, None]
        D = D_MODEL
        x = jnp.einsum('bld,de->ble', u, W_in) + b_in
        x = jnp.swapaxes(x, 1, 2)
        uc = dw_causal_conv(x, short_w, short_b)
        q, k, v = (uc[:, :D], uc[:, D:2 * D], uc[:, 2 * D:])
        v = k * v
        v = dw_causal_conv(v, inner_w, inner_b)
        y = q * v
        y = jnp.swapaxes(y, 1, 2)
        return jnp.einsum('bld,de->ble', y, W_out) + b_out

    def _L0_xattn_ref(x, enc_output, sa_wq, sa_wk, sa_wv, sa_wo, sa_bo, ca_wq, ca_wk, ca_wv, ca_wo, ca_bo, ln1_g, ln1_b, ln2_g, ln2_b, ln3_g, ln3_b, fc1_w, fc1_b, fc2_w, fc2_b, tgt_mask, src_mask):
        import jax, jax.numpy as jnp
        import numpy as np
        B, S, D = (2, 256, 128)
        H, DH = (16, 64)
        INNER = H * DH
        FF = 512
        SCALE = DH ** (-0.5)
        EPS = 1e-05

        def layernorm(x, g, b):
            m = jnp.mean(x, axis=-1, keepdims=True)
            v = jnp.var(x, axis=-1, keepdims=True)
            return (x - m) * jax.lax.rsqrt(v + EPS) * g + b

        def attention(x, ctx, mask, wq, wk, wv, wo, bo):
            b, n, _ = x.shape
            j = ctx.shape[1]
            q = (x @ wq).reshape(b, n, H, DH).transpose(0, 2, 1, 3)
            k = (ctx @ wk).reshape(b, j, H, DH).transpose(0, 2, 1, 3)
            v = (ctx @ wv).reshape(b, j, H, DH).transpose(0, 2, 1, 3)
            sim = jnp.einsum('bhid,bhjd->bhij', q, k) * SCALE
            if mask is not None:
                neg = -jnp.finfo(sim.dtype).max
                sim = jnp.where(mask[:, None, None, :], neg, sim)
            attn = jax.nn.softmax(sim, axis=-1)
            out = jnp.einsum('bhij,bhjd->bhid', attn, v)
            out = out.transpose(0, 2, 1, 3).reshape(b, n, INNER)
            return out @ wo + bo
        a = attention(x, x, tgt_mask, sa_wq, sa_wk, sa_wv, sa_wo, sa_bo)
        x = layernorm(x + a, ln1_g, ln1_b)
        a = attention(x, enc_output, src_mask, ca_wq, ca_wk, ca_wv, ca_wo, ca_bo)
        x = layernorm(x + a, ln2_g, ln2_b)
        h = jax.nn.gelu(x @ fc1_w + fc1_b, approximate=False)
        ff = h @ fc2_w + fc2_b
        x = layernorm(x + ff, ln3_g, ln3_b)
        return x

    def _L0_ffn_ref(x, g_e, b_e, W1_e, b1_e, W2_e, b2_e, g_s, b_s, W1_s, b1_s, W2_s, b2_s):
        import jax, jax.numpy as jnp
        import numpy as np
        EPS = 1e-05
        NUM = 16

        def _layernorm(x, gamma, beta):
            mu = jnp.mean(x, axis=-1, keepdims=True)
            var = jnp.var(x, axis=-1, keepdims=True)
            return (x - mu) * jax.lax.rsqrt(var + EPS) * gamma + beta
        xe = x[:, :NUM, :]
        y = _layernorm(xe, g_e, b_e)
        h = jnp.einsum('bnd,ndh->bnh', y, W1_e) + b1_e
        h = jax.nn.gelu(h, approximate=False)
        out_e = jnp.einsum('bnh,nhk->bnk', h, W2_e) + b2_e
        xr = x[:, NUM:, :]
        yr = _layernorm(xr, g_s, b_s)
        hr = jax.nn.gelu(yr @ W1_s + b1_s, approximate=False)
        out_s = hr @ W2_s + b2_s
        return jnp.concatenate([out_e, out_s], axis=1)
    x = _layernorm(x + _L0_attn_ref(x, L0_attn_W_in, L0_attn_b_in, L0_attn_short_w, L0_attn_short_b, L0_attn_inner_w, L0_attn_inner_b, L0_attn_W_out, L0_attn_b_out), axis=-1)
    x = _layernorm(x + _L0_xattn_ref(x, ctx_1024, L0_xattn_sa_wq, L0_xattn_sa_wk, L0_xattn_sa_wv, L0_xattn_sa_wo, L0_xattn_sa_bo, L0_xattn_ca_wq, L0_xattn_ca_wk, L0_xattn_ca_wv, L0_xattn_ca_wo, L0_xattn_ca_bo, L0_xattn_ln1_g, L0_xattn_ln1_b, L0_xattn_ln2_g, L0_xattn_ln2_b, L0_xattn_ln3_g, L0_xattn_ln3_b, L0_xattn_fc1_w, L0_xattn_fc1_b, L0_xattn_fc2_w, L0_xattn_fc2_b, mask_BxS2_bk0, mask_BxS2_bk0), axis=-1)
    x = _layernorm(x + _L0_ffn_ref(x, L0_ffn_g_e, L0_ffn_b_e, L0_ffn_W1_e, L0_ffn_b1_e, L0_ffn_W2_e, L0_ffn_b2_e, L0_ffn_g_s, L0_ffn_b_s, L0_ffn_W1_s, L0_ffn_b1_s, L0_ffn_W2_s, L0_ffn_b2_s), axis=-1)
    return x

_drawn_inputs = setup_inputs


def setup_inputs(seed=0):
    import zlib

    import numpy as np

    out = dict(_drawn_inputs(seed))
    spreads = {'L0_xattn_sa_bo': (0.0, 0.1),
     'L0_xattn_ca_bo': (0.0, 0.1),
     'L0_xattn_ln1_g': (1.0, 0.2),
     'L0_xattn_ln1_b': (0.0, 0.1),
     'L0_xattn_ln2_g': (1.0, 0.2),
     'L0_xattn_ln2_b': (0.0, 0.1),
     'L0_xattn_ln3_g': (1.0, 0.2),
     'L0_xattn_ln3_b': (0.0, 0.1),
     'L0_xattn_fc1_b': (0.0, 0.1),
     'L0_xattn_fc2_b': (0.0, 0.1),
     'L0_ffn_g_e': (1.0, 0.2),
     'L0_ffn_b_e': (0.0, 0.405),
     'L0_ffn_b1_e': (0.0, 0.401),
     'L0_ffn_b2_e': (0.0, 0.274),
     'L0_ffn_g_s': (1.0, 0.2),
     'L0_ffn_b_s': (0.0, 0.1),
     'L0_ffn_b1_s': (0.0, 0.1),
     'L0_ffn_b2_s': (0.0, 0.1)}
    factors = {'L0_attn_W_in': 8.0,
     'L0_attn_b_in': 25.401,
     'L0_attn_short_w': 8.0,
     'L0_attn_short_b': 8.0,
     'L0_attn_inner_w': 8.0,
     'L0_attn_inner_b': 8.0,
     'L0_attn_W_out': 8.0}
    for name, (base, spread) in spreads.items():
        noise = np.random.default_rng([zlib.crc32(name.encode()), seed]).standard_normal(out[name].shape)
        drawn = base * np.exp(spread * noise) if base else spread * noise
        out[name] = jnp.asarray(drawn.astype(out[name].dtype))
    for name, factor in factors.items():
        out[name] = (out[name] * factor).astype(out[name].dtype)
    return out
```

```python
from contextlib import ExitStack

import numpy as np

import concourse.bass as bass
from concourse import mybir

F32 = mybir.dt.float32
F32R = mybir.dt.float32r
BF16 = mybir.dt.bfloat16
U8 = mybir.dt.uint8
ALU = mybir.AluOpType
ACT = mybir.ActivationFunctionType
AX_X = mybir.AxisListType.X

NSEQ, L, D = 16, 128, 128
H, DH = 16, 64
INNER = H * DH
FF = 512
NEXP = 16
EPS = 1e-5
SCALE = DH ** -0.5
MASKED = -(2.0 ** 100)
T = NSEQ * L
PAIR = 2
NPAIR = NSEQ // PAIR
PCOLS = PAIR * L
HQ = 4
QUADS = PAIR * H // HQ
UNITS = H // 2
GRP = 4
NGRP = NSEQ // GRP
GCOLS = GRP * L
Y_AHEAD, T_LAG, PV_LAG = 4, 2, 3
P_RING = 4


def wait(engine, sem, value):
    if isinstance(value, int) and value <= 0:
        return
    engine.wait_ge(sem, value)


def wait_apart(engine, sem, value, spare):
    wait(engine, sem, value)
    engine.sem_inc(spare, 1)


def f32(ap):
    return ap.bitcast(F32)


def looped(engine, count, body):
    body(0)
    with engine.Fori(1, count - 1) as t:
        body(t)
    body(count - 1)


class Split:

    def __init__(self, hi, lo):
        self.hi, self.lo = hi, lo


def mm_split(nc, out, w, wsel, x, xsel, first=True):
    nc.tensor.matmul(out, w.hi[wsel], x.hi[xsel], start=first, stop=False)
    nc.tensor.matmul(out, w.hi[wsel], x.lo[xsel], start=False, stop=False)
    return nc.tensor.matmul(out, w.lo[wsel], x.hi[xsel], start=False, stop=True)


class Kernel:
    def __init__(self, nc, io):
        self.nc, self.io = nc, io

    def sb(self, ctx, name, shape, dt=F32):
        return ctx.enter_context(self.nc.sbuf_tensor(name, shape, dt))

    def split(self, ctx, name, shape):
        return Split(self.sb(ctx, name + "_hi", shape, F32R), self.sb(ctx, name + "_lo", shape, F32R))

    def banks(self, ctx, tag):
        return [ctx.enter_context(self.nc.psum_tensor(f"{tag}_bank{i}", [128, 512], F32)) for i in range(8)]

    def sems(self, ctx, tag, names):
        return [ctx.enter_context(self.nc.semaphore(f"{tag}_{n}")) for n in names.split()]


def allocate(k, ctx):
    sb, split = k.sb, k.split
    k.ident = sb(ctx, "ident", [128, 128])
    k.half_neg = sb(ctx, "half_neg", [128, NSEQ])
    k.eps = sb(ctx, "eps", [128, NSEQ])
    k.one = sb(ctx, "one", [128, 1])
    k.rows = {n: sb(ctx, "row_" + n, [128, 128]) for n in
              "sa_bo ca_bo ln1_g ln1_b ln2_g ln2_b fc2_b".split()}
    k.x1 = sb(ctx, "x1", [128, NSEQ, 128])
    k.xres = sb(ctx, "xres", [128, NSEQ, 128])
    k.x1T = split(ctx, "x1T", [128, T])


def allocate_attention(k, ctx):
    sb, split = k.sb, k.split
    k.ones_row0 = sb(ctx, "ones_row0", [128, 128], BF16)
    k.maskb = sb(ctx, "maskb", [128, T], BF16)
    k.m_sa = split(ctx, "m_sa", [128, H, 128])
    k.m_ca = split(ctx, "m_ca", [128, H, 128])
    k.wv_sa = split(ctx, "wv_sa", [128, INNER])
    k.wv_ca = split(ctx, "wv_ca", [128, INNER])
    k.wo_sa = sb(ctx, "wo_sa", [128, H // 2, 128])
    k.wo_ca = sb(ctx, "wo_ca", [128, H // 2, 128])
    k.x2T = split(ctx, "x2T", [128, T])
    k.ctxT = split(ctx, "ctxT", [128, T])


def row_broadcast(nc, engine, dst, src_row):
    return engine.dma_start(dst, src_row.partition_broadcast(dst.shape[0]))


def setup_and_mixer(k):
    nc, io = k.nc, k.io
    with ExitStack() as ctx:
        x_tok = k.sb(ctx, "x_tok", [128, NSEQ, 128])
        xT_in = k.sb(ctx, "xT_in", [128, T])
        c_in = k.sb(ctx, "c_in", [128, T])
        xT = k.x2T
        w_in_raw = k.sb(ctx, "w_in_raw", [128, 3 * D])
        w_in = k.split(ctx, "w_in", [128, 3 * D])
        w_out = k.sb(ctx, "w_out", [128, D])
        wv_raw = k.sb(ctx, "wv_raw", [128, INNER])
        qkT = k.sb(ctx, "qkT", [DH, 2, H, 128])
        mask_raw = k.sb(ctx, "mask_raw", [1, T], U8)
        taps = k.sb(ctx, "taps", [128, 3, 3])
        short_b = k.sb(ctx, "short_b", [128, 3])
        b_in = k.sb(ctx, "b_in", [128, 3])
        inner = k.sb(ctx, "inner", [128, 4])
        inner_b = k.sb(ctx, "inner_b", [128, 1])
        b_out = k.sb(ctx, "b_out", [128, 128])
        U = k.sb(ctx, "U", [128, 3, GRP, L + 2])
        C = k.sb(ctx, "C", [128, 3, GRP, L])
        KV = k.sb(ctx, "KV", [128, GRP, L + 3])
        G = k.sb(ctx, "G", [128, GRP, L])
        yT = k.sb(ctx, "yT", [128, GRP, L])
        R = k.sb(ctx, "R", [128, GRP, 128])
        N1 = k.sb(ctx, "N1", [128, GRP, 128])
        stats = k.sb(ctx, "stats", [128, GRP, 6])
        mv = k.sb(ctx, "mv", [128, GRP, 2])
        rstd = k.sb(ctx, "rstd", [128, GRP])
        banks = k.banks(ctx, "mix")
        (ld_x, ld_win, ld_small, ld_qk, ld_wv, ld_keep, ld_ctx, ident0, ident_ok, consts_ok, pads_ok,
         xhi, xlo, whi, wlo, chi, clo, mm_m, m_hi, m_lo, wv_hi, wv_lo, mask_ok,
         u_mm, u_ev, dve, kv_ok, y_ok, o_mm, r_ok, stat_ok, eps_ok, rstd_ok, n_ok, xT_mm, x1hi, x1lo,
         xb_ok, res_ok, spare) = k.sems(ctx, "mix", """ld_x ld_win ld_small ld_qk ld_wv ld_keep ld_ctx ident0
            ident_ok consts_ok pads_ok xhi xlo whi wlo chi clo mm_m m_hi m_lo wv_hi wv_lo mask_ok
            u_mm u_ev dve kv_ok y_ok o_mm r_ok stat_ok eps_ok rstd_ok n_ok xT_mm x1hi x1lo xb_ok
            res_ok spare""")
        block = ctx.enter_context(nc.Block())
        KEPT = 2 + len(k.rows)

        @block.sync
        def _(sp):
            sp.dma_start(xT_in[:], io["xT"]).then_inc(ld_x, 16)
            sp.dma_start(w_in_raw[:], io["W_in"]).then_inc(ld_win, 16)
            sp.dma_start(taps[:], io["short_w"].rearrange("(c p) j -> p c j", p=128)).then_inc(ld_small, 16)
            sp.dma_start(short_b[:], io["short_bT"]).then_inc(ld_small, 16)
            sp.dma_start(b_in[:], io["b_inT"]).then_inc(ld_small, 16)
            sp.dma_start(inner[:], io["inner_w"]).then_inc(ld_small, 16)
            sp.dma_start(inner_b[:], io["inner_b"].rearrange("(p o) -> p o", o=1)).then_inc(ld_small, 16)
            sp.dma_start(x_tok[:], io["x"].rearrange("b p d -> p b d")).then_inc(ld_small, 16)
            row_broadcast(nc, sp, b_out[:], io["b_out"]).then_inc(ld_small, 16)
            sp.dma_start(w_out[:], io["W_out"]).then_inc(ld_small, 16)
            for n, tile in k.rows.items():
                row_broadcast(nc, sp, tile[:], io[n]).then_inc(ld_keep, 16)
            sp.dma_start(k.wo_sa[:], io["sa_wo"].rearrange("(c p) n -> p c n", p=128)).then_inc(ld_keep, 16)
            sp.dma_start(k.wo_ca[:], io["ca_wo"].rearrange("(c p) n -> p c n", p=128)).then_inc(ld_keep, 16)
            sp.wait_ge(ld_keep, 16 * KEPT)

        @block.scalar
        def _(act):
            act.dma_start(qkT[:, 0], io["sa_wqT"].rearrange("(h j) d -> j h d", j=DH)).then_inc(ld_qk, 16)
            act.dma_start(qkT[:, 1], io["sa_wkT"].rearrange("(h j) d -> j h d", j=DH)).then_inc(ld_qk, 16)
            act.dma_start(wv_raw[:], io["sa_wv"]).then_inc(ld_wv, 16)
            act.dma_start(c_in[:], io["ctxT"]).then_inc(ld_ctx, 16)
            act.dma_start(mask_raw[:], io["mask"].rearrange("(o b) p -> o (b p)", o=1)).then_inc(ld_ctx, 16)
            act.wait_ge(ld_x, 16)
            nc.scalar.activation(xT.hi[:], xT_in[:], ACT.Copy).then_inc(xhi, 1)
            act.wait_ge(ld_win, 16)
            nc.scalar.activation(w_in.hi[:], w_in_raw[:], ACT.Copy).then_inc(whi, 1)
            act.wait_ge(ld_small, 16 * 8)
            act.wait_ge(pads_ok, 2)

            def mixer(t):
                for c in range(3):
                    wait(act, u_mm, 3 * t + c + 1)
                    if c == 0:
                        wait(act, kv_ok, t)
                    nc.scalar.activation(U[:, c, :, 2:], banks[c][:].rearrange("p (b l) -> p b l", b=GRP),
                                         ACT.Identity, bias=b_in[:, c:c + 1]).then_inc(u_ev, 1)
                wait(act, xT_mm, t + 1)
                nc.scalar.activation(k.x1T.hi[:, bass.ds(t * GCOLS, GCOLS)], banks[4][:],
                                     ACT.Copy).then_inc(x1hi, 1)

            looped(act, NGRP, mixer)
            act.wait_ge(ld_ctx, 32)
            nc.scalar.activation(k.ctxT.hi[:], c_in[:], ACT.Copy).then_inc(chi, 1)
            for a, (m, wv) in enumerate(((k.m_sa, k.wv_sa), (k.m_ca, k.wv_ca))):
                for q in range(H // HQ):
                    i = a * H // HQ + q
                    act.wait_ge(mm_m, i + 1)
                    nc.scalar.activation(m.hi[:, q * HQ:(q + 1) * HQ, :],
                                         banks[5 + i % 2][:].rearrange("p (h d) -> p h d", h=HQ),
                                         ACT.Copy, scale=SCALE).then_inc(m_hi, 1)
                if a == 0:
                    act.wait_ge(mm_m, H // HQ)
                    act.dma_start(qkT[:, 0], io["ca_wqT"].rearrange("(h j) d -> j h d", j=DH)).then_inc(ld_qk, 16)
                    act.dma_start(qkT[:, 1], io["ca_wkT"].rearrange("(h j) d -> j h d", j=DH)).then_inc(ld_qk, 16)
                act.wait_ge(ld_wv, 16 * (a + 1))
                nc.scalar.activation(wv.hi[:], wv_raw[:], ACT.Copy).then_inc(wv_hi, 1)
                if a == 0:
                    act.wait_ge(wv_lo, 1)
                    act.dma_start(wv_raw[:], io["ca_wv"]).then_inc(ld_wv, 16)

        @block.gpsimd
        def _(pool):
            nc.gpsimd.memset(k.ident[:], 0.0).then_inc(ident0, 1)
            pool.wait_ge(ident0, 1)
            nc.gpsimd.affine_select(out=k.ident[:], in_=k.ident[:], compare_op=ALU.not_equal, fill=1.0, base=0,
                                    pattern=[[-1, 128]], channel_multiplier=1).then_inc(ident_ok, 1)
            nc.gpsimd.memset(U[:], 0.0).then_inc(pads_ok, 1)
            nc.gpsimd.memset(KV[:], 0.0).then_inc(pads_ok, 1)
            nc.gpsimd.memset(k.half_neg[:], -0.5).then_inc(consts_ok, 1)
            nc.gpsimd.memset(k.eps[:], EPS).then_inc(consts_ok, 1)
            nc.gpsimd.memset(k.one[:], 1.0).then_inc(consts_ok, 1)
            nc.gpsimd.memset(k.maskb[:], 0.0).then_inc(consts_ok, 1)
            nc.gpsimd.memset(k.ones_row0[:], 0.0).then_inc(consts_ok, 1)
            pool.wait_ge(consts_ok, 5)
            nc.gpsimd.memset(k.ones_row0[0:1, :], 1.0).then_inc(consts_ok, 1)
            pool.wait_ge(ld_small, 16 * 8)
            nc.gpsimd.tensor_tensor(x_tok[:], x_tok[:], b_out[:].unsqueeze(1).to_broadcast([128, NSEQ, 128]),
                                    ALU.add).then_inc(xb_ok, 1)
            pool.wait_ge(ld_keep, 16 * KEPT)

            def mixer(t):
                wait(pool, stat_ok, t + 1)
                nc.gpsimd.tensor_tensor(rstd[:], mv[:, :, 1], k.eps[:, 0:GRP], ALU.add).then_inc(eps_ok, 1)
                wait(pool, eps_ok, t + 1)
                nc.gpsimd.tensor_tensor(rstd[:], rstd[:], k.half_neg[:, 0:GRP], ALU.pow).then_inc(rstd_ok, 1)
                wait_apart(pool, n_ok, GRP * (t + 1), spare)
                nc.gpsimd.tensor_tensor(k.xres[:, bass.ds(t * GRP, GRP), :], N1[:],
                                        k.rows["sa_bo"][:].unsqueeze(1).to_broadcast([128, GRP, 128]),
                                        ALU.add).then_inc(res_ok, 1)
                nc.gpsimd.tensor_tensor(k.x1[:, bass.ds(t * GRP, GRP), :], N1[:],
                                        k.one[:].unsqueeze(1).to_broadcast([128, GRP, 128]),
                                        ALU.mult).then_inc(res_ok, 1)

            looped(pool, NGRP, mixer)

        @block.vector
        def _(vec):
            vec.wait_ge(xhi, 1)
            nc.vector.tensor_tensor(xT.lo[:], xT_in[:], f32(xT.hi[:]), ALU.subtract).then_inc(xlo, 1)
            vec.wait_ge(whi, 1)
            nc.vector.tensor_tensor(w_in.lo[:], w_in_raw[:], f32(w_in.hi[:]), ALU.subtract).then_inc(wlo, 1)
            vec.wait_ge(ld_small, 16 * 8)
            vec.wait_ge(pads_ok, 2)
            CH = 3 + 2 + 4 + 2

            def mixer(t):
                link = [0]

                def then(ins):
                    link[0] += 1
                    ins.then_inc(dve, 1)
                    wait(vec, dve, CH * t + link[0])

                for c in range(3):
                    wait(vec, u_ev, 3 * t + c + 1)
                    nc.vector.tensor_scalar(C[:, c], U[:, c, :, 2:2 + L], taps[:, c, 2:3], short_b[:, c:c + 1],
                                            ALU.mult, ALU.add).then_inc(dve, 1)
                    link[0] += 1
                for j in range(2):
                    for c in range(3):
                        if c == 0:
                            wait(vec, dve, CH * t + link[0])
                        last = nc.vector.scalar_tensor_tensor(C[:, c], U[:, c, :, j:j + L], taps[:, c, j:j + 1],
                                                              C[:, c], ALU.mult, ALU.add)
                    last.then_inc(dve, 1)
                    link[0] += 1
                wait(vec, dve, CH * t + link[0])
                last = nc.vector.tensor_tensor(KV[:, :, 3:], C[:, 1], C[:, 2], ALU.mult)
                last.then_inc(kv_ok, 1)
                wait(vec, kv_ok, t + 1)
                then(nc.vector.tensor_scalar(G[:], KV[:, :, 3:3 + L], inner[:, 3:4], inner_b[:, 0:1],
                                             ALU.mult, ALU.add))
                for j in range(3):
                    then(nc.vector.scalar_tensor_tensor(G[:], KV[:, :, j:j + L], inner[:, j:j + 1], G[:],
                                                        ALU.mult, ALU.add))
                wait(vec, o_mm, t)
                nc.vector.tensor_tensor(yT[:], C[:, 0], G[:], ALU.mult).then_inc(y_ok, 1)
                wait(vec, o_mm, t + 1)
                if isinstance(t, int) and t == 0:
                    vec.wait_ge(xb_ok, 1)
                then(nc.vector.tensor_tensor(R[:], banks[3][:].rearrange("p (b d) -> p b d", b=GRP),
                                             x_tok[:, bass.ds(t * GRP, GRP), :], ALU.add))
                for b in range(GRP):
                    last = nc.vector.bn_stats(stats[:, b], R[:, b])
                then(last)
                vec.sem_inc(spare, 1)
                for b in range(GRP):
                    last = nc.vector.bn_aggr(mv[:, b], stats[:, b])
                last.then_inc(stat_ok, 1)
                wait(vec, rstd_ok, t + 1)
                wait(vec, xT_mm, t)
                wait(vec, res_ok, 2 * t)
                for b in range(GRP):
                    nc.vector.tensor_scalar(N1[:, b], R[:, b], mv[:, b, 0:1], rstd[:, b:b + 1],
                                            ALU.subtract, ALU.mult).then_inc(n_ok, 1)
                wait(vec, x1hi, t + 1)
                last = nc.vector.tensor_tensor(k.x1T.lo[:, bass.ds(t * GCOLS, GCOLS)], banks[4][:],
                                               f32(k.x1T.hi[:, bass.ds(t * GCOLS, GCOLS)]), ALU.subtract)
                last.then_inc(x1lo, 1)
                assert link[0] == CH

            looped(vec, NGRP, mixer)
            vec.wait_ge(ld_ctx, 32)
            vec.wait_ge(consts_ok, 6)
            nc.vector.tensor_scalar(k.maskb[0:1, :], mask_raw[:], MASKED, None, ALU.mult).then_inc(mask_ok, 1)
            vec.wait_ge(chi, 1)
            nc.vector.tensor_tensor(k.ctxT.lo[:], c_in[:], f32(k.ctxT.hi[:]), ALU.subtract).then_inc(clo, 1)
            for a, (m, wv) in enumerate(((k.m_sa, k.wv_sa), (k.m_ca, k.wv_ca))):
                for q in range(H // HQ):
                    i = a * H // HQ + q
                    vec.wait_ge(m_hi, i + 1)
                    sl = m.hi[:, q * HQ:(q + 1) * HQ, :]
                    nc.vector.scalar_tensor_tensor(m.lo[:, q * HQ:(q + 1) * HQ, :],
                                                   banks[5 + i % 2][:].rearrange("p (h d) -> p h d", h=HQ), SCALE,
                                                   f32(sl), ALU.mult, ALU.subtract).then_inc(m_lo, 1)
                vec.wait_ge(wv_hi, a + 1)
                nc.vector.tensor_tensor(wv.lo[:], wv_raw[:], f32(wv.hi[:]), ALU.subtract).then_inc(wv_lo, 1)

        @block.tensor
        def _(pe):
            pe.wait_ge(xlo, 1)
            pe.wait_ge(wlo, 1)
            pe.wait_ge(ident_ok, 1)
            pe.wait_ge(ld_small, 16 * 8)

            def mixer(t):
                for c in range(3):
                    wait(pe, u_ev, 3 * t + c - 2)
                    mm_split(nc, banks[c][:], w_in, np.s_[:, c * D:(c + 1) * D], xT,
                             np.s_[:, bass.ds(t * GCOLS, GCOLS)]).then_inc(u_mm, 1)
                wait(pe, y_ok, t + 1)
                for b in range(GRP):
                    last = nc.tensor.matmul(banks[3][:, b * 128:(b + 1) * 128], yT[:, b, :], w_out[:],
                                            start=True, stop=True)
                last.then_inc(o_mm, 1)
                wait(pe, n_ok, GRP * (t + 1))
                wait(pe, x1lo, t)
                for b in range(GRP):
                    last = nc.tensor.transpose(banks[4][:, b * 128:(b + 1) * 128], N1[:, b, :], k.ident[:])
                last.then_inc(xT_mm, 1)

            looped(pe, NGRP, mixer)
            for a in range(2):
                pe.wait_ge(ld_qk, 32 * (a + 1))
                for q in range(H // HQ):
                    i = a * H // HQ + q
                    wait(pe, m_lo, i - 1)
                    for h in range(HQ):
                        last = nc.tensor.matmul(banks[5 + i % 2][:, h * 128:(h + 1) * 128], qkT[:, 1, q * HQ + h, :],
                                                qkT[:, 0, q * HQ + h, :], start=True, stop=True)
                    last.then_inc(mm_m, 1)


def attention(k, tag, qT, kvT, m, wv, wo, g_row, b_row, next_bias, outT):
    nc = k.nc
    with ExitStack() as ctx:
        xq = k.split(ctx, tag + "xq", [128, PAIR, 128])
        xv = k.split(ctx, tag + "xv", [128, PAIR, 128])
        y = k.split(ctx, tag + "y", [128, PAIR, H, 128])
        V = k.sb(ctx, tag + "V", [128, PAIR, INNER])
        P = k.sb(ctx, tag + "P", [128, P_RING, HQ, 128])
        PT = k.sb(ctx, tag + "PT", [128, 2, HQ * 128])
        OT = k.sb(ctx, tag + "OT", [128, PAIR, H // 2, 128])
        negmax = k.sb(ctx, tag + "negmax", [128, 2, HQ])
        total = k.sb(ctx, tag + "total", [128, 2, HQ])
        inv = k.sb(ctx, tag + "inv", [128, 2, HQ])
        R = k.sb(ctx, tag + "R", [128, PAIR, 128])
        N = k.sb(ctx, tag + "N", [128, PAIR, 128])
        X = k.sb(ctx, tag + "X", [128, PAIR, 128])
        stats = k.sb(ctx, tag + "stats", [128, PAIR, 6])
        mv = k.sb(ctx, tag + "mv", [128, PAIR, 2])
        rstd = k.sb(ctx, tag + "rstd", [128, PAIR])
        banks = k.banks(ctx, tag)
        Y_BANK, S_BANK, PT_BANK, O_BANK, V_BANK, W_BANK = (0, 1), (2, 3), 4, 5, 6, 7
        (y_mm, y_hi, y_lo, s_mm, max_ok, exp_ok, inv_ok, norm_ok, t_mm, pt_ok, pv_mm, o_ok, v_mm, v_ok,
         xq_ok, xv_ok, wo_mm, r_ok, st_ok, mv_ok, eps_ok, rstd_ok, n_ok, gain_ok, x_ok, res_ok, xT_mm, xT_hi,
         xT_lo, spare) = k.sems(ctx, tag, """y_mm y_hi y_lo s_mm max_ok exp_ok inv_ok norm_ok t_mm pt_ok pv_mm o_ok
             v_mm v_ok xq_ok xv_ok wo_mm r_ok st_ok mv_ok eps_ok rstd_ok n_ok gain_ok x_ok res_ok xT_mm xT_hi
             xT_lo spare""")
        block = ctx.enter_context(nc.Block())
        V1_STEPS = (3, 4)
        V0_STEPS = (6, 7)
        XV_STEP = 5
        WO_STEP, XT_STEP = 3, 6

        def cols(t, n=PCOLS, off=0):
            return bass.ds(t * PCOLS + off, n)

        def exists(t):
            return not isinstance(t, int) or 0 <= t < NPAIR

        @block.tensor
        def _(pe):
            def y_unit(t, u):
                n = UNITS * t + u
                wait(pe, y_lo, n - 1)
                for j in range(2):
                    last = mm_split(nc, banks[Y_BANK[u % 2]][:, j * PCOLS:(j + 1) * PCOLS], m,
                                    np.s_[:, 2 * u + j, :], kvT, np.s_[:, cols(t)])
                last.then_inc(y_mm, 1)

            def scores(t, g):
                n, b, hq = QUADS * t + g, g % PAIR, g // PAIR
                wait(pe, y_lo, UNITS * t + 2 * hq + 2)
                if hq == 0:
                    wait(pe, xq_ok, PAIR * t + b + 1)
                wait(pe, exp_ok, n - 1)
                out = banks[S_BANK[g % 2]][:]
                nc.tensor.matmul(out, k.ones_row0[:],
                                 k.maskb[:, cols(t, 128, b * 128)].unsqueeze(1).to_broadcast([128, HQ, 128]),
                                 start=True, stop=False)
                mm_split(nc, out, xq, np.s_[:, b, :], y, np.s_[:, b, HQ * hq:HQ * (hq + 1), :],
                         first=False).then_inc(s_mm, 1)

            def transposes(n, g):
                wait(pe, norm_ok, n + 1)
                wait(pe, pt_ok, n)
                for h in range(HQ):
                    last = nc.tensor.transpose(banks[PT_BANK][:, h * 128:(h + 1) * 128], P[:, g % P_RING, h, :],
                                               k.ident[:])
                last.then_inc(t_mm, 1)

            def p_v(t, n, g):
                b, hq = g % PAIR, g // PAIR
                wait(pe, pt_ok, n + 1)
                wait(pe, v_ok, 4 * t + (2 if hq < 2 else 4))
                wait(pe, o_ok, n)
                for h in range(HQ):
                    part = 64 * (h % 2)
                    last = nc.tensor.matmul(banks[O_BANK][part:part + 64, (h // 2) * 128:(h // 2 + 1) * 128],
                                            V[:, b, (HQ * hq + h) * DH:(HQ * hq + h + 1) * DH],
                                            PT[:, g % 2, h * 128:(h + 1) * 128], start=True, stop=True)
                last.then_inc(pv_mm, 1)

            def v_half(i, t, b, half):
                wait(pe, xv_ok, t + 1)
                wait(pe, v_ok, i)
                mm_split(nc, banks[V_BANK][:], xv, np.s_[:, b, :], wv,
                         np.s_[:, half * 512:(half + 1) * 512]).then_inc(v_mm, 1)

            def out_proj(t):
                wait(pe, o_ok, QUADS * (t + 1))
                wait(pe, xT_lo, t)
                for b in range(PAIR):
                    for c in range(H // 2):
                        last = nc.tensor.matmul(banks[W_BANK][:, b * 128:(b + 1) * 128], OT[:, b, c, :], wo[:, c, :],
                                                start=(c == 0), stop=(c == H // 2 - 1))
                last.then_inc(wo_mm, 1)

            def x_transposes(t):
                wait(pe, x_ok, t + 1)
                for b in range(PAIR):
                    last = nc.tensor.transpose(banks[W_BANK][:, b * 128:(b + 1) * 128], X[:, b, :], k.ident[:])
                last.then_inc(xT_mm, 1)

            def pair(t):
                for g in range(QUADS):
                    n = QUADS * t + g
                    scores(t, g)
                    if g + Y_AHEAD < UNITS:
                        y_unit(t, g + Y_AHEAD)
                    elif exists(t + 1):
                        y_unit(t + 1, g + Y_AHEAD - UNITS)
                    back = 1 if g < T_LAG else 0
                    if exists(t - back):
                        transposes(n - T_LAG, (g - T_LAG) % QUADS)
                    if g == WO_STEP and exists(t - 1):
                        out_proj(t - 1)
                    back = 1 if g < PV_LAG else 0
                    if exists(t - back):
                        p_v(t - back, n - PV_LAG, (g - PV_LAG) % QUADS)
                    if g in V1_STEPS:
                        b = V1_STEPS.index(g)
                        v_half(4 * t + 2 + b, t, b, 1)
                    if g in V0_STEPS and exists(t + 1):
                        b = V0_STEPS.index(g)
                        v_half(4 * t + 4 + b, t + 1, b, 0)
                    if g == XT_STEP and exists(t - 1):
                        x_transposes(t - 1)

            for u in range(Y_AHEAD):
                y_unit(0, u)
            for b in range(PAIR):
                v_half(b, 0, b, 0)
            looped(pe, NPAIR, pair)
            N_ALL = QUADS * NPAIR
            for n in range(N_ALL, N_ALL + PV_LAG):
                if n - T_LAG < N_ALL:
                    transposes(n - T_LAG, (n - T_LAG) % QUADS)
                p_v(NPAIR - 1, n - PV_LAG, (n - PV_LAG) % QUADS)
            out_proj(NPAIR - 1)
            x_transposes(NPAIR - 1)

        @block.scalar
        def _(act):
            def exps(n, g):
                wait(act, max_ok, n + 1)
                for h in range(HQ):
                    last = nc.scalar.activation(P[:, g % P_RING, h, :], banks[S_BANK[g % 2]][:, h * 128:(h + 1) * 128],
                                                ACT.Exp, bias=negmax[:, g % 2, h:h + 1],
                                                accum_out=total[:, g % 2, h:h + 1])
                last.then_inc(exp_ok, 1)

            def y_high(t, u):
                n = UNITS * t + u
                wait(act, y_mm, n + 1)
                wait(act, s_mm, QUADS * (t - 1) + 2 * (u // 2) + 2)
                for b in range(PAIR):
                    last = nc.scalar.activation(
                        y.hi[:, b, 2 * u:2 * u + 2, :],
                        banks[Y_BANK[u % 2]][:].rearrange("p (h b l) -> p b h l", h=2, b=PAIR)[:, b], ACT.Copy)
                last.then_inc(y_hi, 1)

            def v_out(i, t, b, half):
                wait(act, v_mm, i + 1)
                wait(act, pv_mm, QUADS * (t - 1) + (4 if half == 0 else 8))
                nc.scalar.activation(V[:, b, half * 512:(half + 1) * 512], banks[V_BANK][:], ACT.Copy).then_inc(v_ok, 1)

            def xT_high(t):
                wait(act, xT_mm, t + 1)
                nc.scalar.activation(outT.hi[:, cols(t)], banks[W_BANK][:, 0:PCOLS], ACT.Copy).then_inc(xT_hi, 1)

            def pair(t):
                for g in range(QUADS):
                    n = QUADS * t + g
                    exps(n, g)
                    if g + Y_AHEAD < UNITS:
                        y_high(t, g + Y_AHEAD)
                    elif exists(t + 1):
                        y_high(t + 1, g + Y_AHEAD - UNITS)
                    back = 1 if g < PV_LAG else 0
                    if exists(t - back):
                        if g == PV_LAG and exists(t - 1):
                            wait(act, wo_mm, t)
                        o_out(n - PV_LAG, (g - PV_LAG) % QUADS)
                    if g in V1_STEPS:
                        b = V1_STEPS.index(g)
                        v_out(4 * t + 2 + b, t, b, 1)
                    if g in V0_STEPS and exists(t + 1):
                        b = V0_STEPS.index(g)
                        v_out(4 * t + 4 + b, t + 1, b, 0)
                    if g == XT_STEP and exists(t - 1):
                        xT_high(t - 1)

            def o_out(n, g):
                b, hq = g % PAIR, g // PAIR
                wait(act, pv_mm, n + 1)
                nc.scalar.activation(OT[:, b, 2 * hq:2 * hq + 2, :],
                                     banks[O_BANK][:, 0:256].rearrange("p (c l) -> p c l", c=2),
                                     ACT.Copy).then_inc(o_ok, 1)

            for u in range(Y_AHEAD):
                y_high(0, u)
            for b in range(PAIR):
                v_out(b, 0, b, 0)
            looped(act, NPAIR, pair)
            N_ALL = QUADS * NPAIR
            for n in range(N_ALL - PV_LAG, N_ALL):
                o_out(n, n % QUADS)
            xT_high(NPAIR - 1)

        @block.vector
        def _(vec):
            def reciprocals(n, g):
                wait(vec, exp_ok, n + 1)
                nc.vector.reciprocal(inv[:, g % 2], total[:, g % 2]).then_inc(inv_ok, 1)

            def y_low(t, u):
                n = UNITS * t + u
                wait(vec, y_hi, n + 1)
                for b in range(PAIR):
                    last = nc.vector.tensor_tensor(
                        y.lo[:, b, 2 * u:2 * u + 2, :],
                        banks[Y_BANK[u % 2]][:].rearrange("p (h b l) -> p b h l", h=2, b=PAIR)[:, b],
                        f32(y.hi[:, b, 2 * u:2 * u + 2, :]), ALU.subtract)
                last.then_inc(y_lo, 1)

            def maxima(n, g):
                wait(vec, s_mm, n + 1)
                nc.vector.tensor_reduce(negmax[:, g % 2], banks[S_BANK[g % 2]][:].rearrange("p (h l) -> p h l", h=HQ),
                                        AX_X, ALU.max, negate=True).then_inc(max_ok, 1)

            def pt_out(n, g):
                wait(vec, t_mm, n + 1)
                wait(vec, pv_mm, n - 1)
                nc.vector.tensor_copy(PT[:, g % 2], banks[PT_BANK][:]).then_inc(pt_ok, 1)

            def residual(t):
                wait(vec, wo_mm, t + 1)
                nc.vector.tensor_tensor(R[:], banks[W_BANK][:, 0:PCOLS].rearrange("p (b d) -> p b d", b=PAIR),
                                        k.xres[:, bass.ds(t * PAIR, PAIR), :], ALU.add).then_inc(r_ok, 1)
                wait(vec, r_ok, t + 1)
                for b in range(PAIR):
                    last = nc.vector.bn_stats(stats[:, b], R[:, b])
                last.then_inc(st_ok, 1)
                wait_apart(vec, st_ok, t + 1, spare)
                for b in range(PAIR):
                    last = nc.vector.bn_aggr(mv[:, b], stats[:, b])
                last.then_inc(mv_ok, 1)

            def normalise(t):
                wait(vec, rstd_ok, t + 1)
                for b in range(PAIR):
                    last = nc.vector.tensor_scalar(N[:, b], R[:, b], mv[:, b, 0:1], rstd[:, b:b + 1],
                                                   ALU.subtract, ALU.mult)
                last.then_inc(n_ok, 1)

            def xT_low(t):
                wait(vec, xT_hi, t + 1)
                nc.vector.tensor_tensor(outT.lo[:, cols(t)], banks[W_BANK][:, 0:PCOLS], f32(outT.hi[:, cols(t)]),
                                        ALU.subtract).then_inc(xT_lo, 1)

            def pair(t):
                for g in range(QUADS):
                    n = QUADS * t + g
                    if exists(t - (g < 1)):
                        reciprocals(n - 1, (g - 1) % QUADS)
                    u = g - 1 + Y_AHEAD
                    if u < UNITS and (g > 0 or exists(t - 1)):
                        y_low(t, u)
                    elif u >= UNITS and exists(t + 1):
                        y_low(t + 1, u - UNITS)
                    maxima(n, g)
                    if exists(t - (g < T_LAG)):
                        pt_out(n - T_LAG, (g - T_LAG) % QUADS)
                    if g == WO_STEP and exists(t - 1):
                        residual(t - 1)
                    if g == WO_STEP + 1 and exists(t - 1):
                        normalise(t - 1)
                    if g == XT_STEP and exists(t - 1):
                        xT_low(t - 1)

            for u in range(Y_AHEAD):
                y_low(0, u)
            looped(vec, NPAIR, pair)
            N_ALL = QUADS * NPAIR
            reciprocals(N_ALL - 1, (N_ALL - 1) % QUADS)
            for n in range(N_ALL - T_LAG, N_ALL):
                pt_out(n, n % QUADS)
            residual(NPAIR - 1)
            normalise(NPAIR - 1)
            xT_low(NPAIR - 1)

        @block.gpsimd
        def _(pool):
            def copy(dst, src):
                return nc.gpsimd.tensor_tensor(dst, f32(src), k.one[:].to_broadcast([128, src.shape[1]]), ALU.mult)

            def queries(t, b):
                wait_apart(pool, s_mm, QUADS * (t - 1) + QUADS - PAIR + b + 1, spare)
                copy(xq.hi[:, b], qT.hi[:, cols(t, 128, b * 128)])
                copy(xq.lo[:, b], qT.lo[:, cols(t, 128, b * 128)]).then_inc(xq_ok, 1)

            def keys(t):
                wait_apart(pool, v_mm, 4 * t, spare)
                copy(xv.hi[:].rearrange("p b l -> p (b l)"), kvT.hi[:, cols(t)])
                copy(xv.lo[:].rearrange("p b l -> p (b l)"), kvT.lo[:, cols(t)]).then_inc(xv_ok, 1)

            def normalise(n, g):
                wait(pool, inv_ok, n + 1)
                tile = P[:, g % P_RING]
                nc.gpsimd.tensor_tensor(tile, tile, inv[:, g % 2].unsqueeze(2).to_broadcast([128, HQ, 128]),
                                        ALU.mult).then_inc(norm_ok, 1)

            def inverse_deviation(t):
                wait(pool, mv_ok, t + 1)
                nc.gpsimd.tensor_tensor(rstd[:], mv[:, :, 1], k.eps[:, 0:PAIR], ALU.add).then_inc(eps_ok, 1)
                wait(pool, eps_ok, t + 1)
                nc.gpsimd.tensor_tensor(rstd[:], rstd[:], k.half_neg[:, 0:PAIR], ALU.pow).then_inc(rstd_ok, 1)

            def affine(t):
                wait(pool, n_ok, t + 1)

                def row(r):
                    return r[:].unsqueeze(1).to_broadcast([128, PAIR, 128])

                nc.gpsimd.tensor_tensor(N[:], N[:], row(g_row), ALU.mult).then_inc(gain_ok, 1)
                wait(pool, gain_ok, t + 1)
                wait(pool, xT_mm, t)
                nc.gpsimd.tensor_tensor(X[:], N[:], row(b_row), ALU.add).then_inc(x_ok, 1)
                wait_apart(pool, x_ok, t + 1, spare)
                nc.gpsimd.tensor_tensor(k.xres[:, bass.ds(t * PAIR, PAIR), :], X[:], row(next_bias),
                                        ALU.add).then_inc(res_ok, 1)

            def pair(t):
                for g in range(QUADS):
                    n = QUADS * t + g
                    if g == QUADS - 1 and exists(t + 1):
                        queries(t + 1, 0)
                    if g == 0 and exists(t - 1):
                        queries(t, 1)
                    if g == XV_STEP and exists(t + 1):
                        keys(t + 1)
                    if exists(t - (g < 1)):
                        normalise(n - 1, (g - 1) % QUADS)
                    if g == WO_STEP and exists(t - 1):
                        inverse_deviation(t - 1)
                    if g == WO_STEP + 1 and exists(t - 1):
                        affine(t - 1)

            queries(0, 0)
            queries(0, 1)
            keys(0)
            looped(pool, NPAIR, pair)
            normalise(QUADS * NPAIR - 1, QUADS - 1)
            inverse_deviation(NPAIR - 1)
            affine(NPAIR - 1)


def feed_forward(k):
    nc, io = k.nc, k.io
    with ExitStack() as ctx:
        sb = k.sb
        fc1_raw = sb(ctx, "fc1_raw", [128, FF])
        fc1 = k.split(ctx, "fc1", [128, FF])
        fc1_b = sb(ctx, "fc1_b", [128, FF // 128])
        fc2 = sb(ctx, "fc2", [128, FF // 128, 128])
        w1_raw = sb(ctx, "w1_raw", [128, 128])
        w1 = k.split(ctx, "w1s", [128, 128])
        b1 = sb(ctx, "b1", [128, 1])
        w2 = sb(ctx, "w2", [128, 128])
        w1e = sb(ctx, "w1e", [128, NEXP, 128])
        w2e = sb(ctx, "w2e", [128, NEXP, 128])
        b1e = sb(ctx, "b1e", [128, NEXP])
        rows3 = {n: sb(ctx, "row_" + n, [128, 128]) for n in ("ln3_g", "ln3_b")}
        gain = sb(ctx, "gain", [128, 128])
        shift = sb(ctx, "shift", [128, 128])
        bias2 = sb(ctx, "bias2", [128, 128])
        hT = sb(ctx, "hT", [128, FF // 128, GRP, 128])
        R = sb(ctx, "ffR", [128, GRP, 128])
        N3 = sb(ctx, "N3", [128, GRP, 128])
        X4 = sb(ctx, "X4", [128, GRP, 128])
        N5 = sb(ctx, "N5", [128, GRP, 128])
        zT = k.split(ctx, "zT", [128, GRP, 128])
        zE = sb(ctx, "zE", [128, NSEQ, NEXP])
        gT = sb(ctx, "gT", [128, GRP, 128])
        res = sb(ctx, "res", [128, NSEQ, 128])
        hE = sb(ctx, "hE", [128, NEXP, NSEQ])
        oE = sb(ctx, "oE", [NSEQ, NEXP, 128])
        oE_pos = sb(ctx, "oE_pos", [NEXP, NSEQ, 128])
        stats = sb(ctx, "ffstats", [128, 3, GRP, 6])
        mv = sb(ctx, "ffmv", [128, 3, GRP, 2])
        rstd = sb(ctx, "ffrstd", [128, 3, GRP])
        stats_o = sb(ctx, "stats_o", [128, NSEQ, 6])
        mv_o = sb(ctx, "mv_o", [128, NSEQ, 2])
        rstd_o = sb(ctx, "rstd_o", [128, NSEQ])
        outt = sb(ctx, "outt", [128, NSEQ, 128])
        banks = k.banks(ctx, "ff")
        (ld, ld_w, ld_e, f1hi, w1hi, wlo, fc1_mm, h_ok, fc2_mm, r_ok, st, mvs, eps_ok, rstd_ok, nrm, g3, b3, x4a,
         x4_ok, g5, z_ok, zT_mm, z_hi, z_lo, ze_ok, w1_mm, g_ok, w2_mm, x4b, res_ok, e1_mm, e1_b, e1_g, e2_mm, e2_ok,
         e_moved, e_added, so, mo, eo, ro, no, stored, spare,
         zeroed) = k.sems(ctx, "ff", """ld ld_w ld_e f1hi w1hi wlo fc1_mm
            h_ok fc2_mm r_ok st mvs eps_ok rstd_ok nrm g3 b3 x4a x4_ok g5 z_ok zT_mm z_hi z_lo ze_ok w1_mm g_ok w2_mm
            x4b res_ok e1_mm e1_b e1_g e2_mm e2_ok e_moved e_added so mo eo ro no stored spare zeroed""")
        block = ctx.enter_context(nc.Block())
        NLD = 12

        def quarter(bank):
            return banks[bank][:].rearrange("p (b d) -> p b d", b=GRP)

        @block.sync
        def _(sp):
            sp.dma_start(fc1_raw[:], io["fc1_w"]).then_inc(ld_w, 16)
            sp.dma_start(w1_raw[:], io["W1_s"]).then_inc(ld_w, 16)
            sp.dma_start(fc1_b[:], io["fc1_bT"]).then_inc(ld, 16)
            sp.dma_start(fc2[:], io["fc2_w"].rearrange("(c p) n -> p c n", p=128)).then_inc(ld, 16)
            for n, tile in rows3.items():
                row_broadcast(nc, sp, tile[:], io[n]).then_inc(ld, 16)
            sp.dma_start(b1[:], io["b1_s"].rearrange("(p o) -> p o", o=1)).then_inc(ld, 16)
            sp.dma_start(w2[:], io["W2_s"]).then_inc(ld, 16)
            for tile, name in ((gain, "g"), (shift, "b"), (bias2, "b2")):
                sp.dma_start(tile[0:NEXP, :], io[name + "_e"]).then_inc(ld, 16)
                row_broadcast(nc, sp, tile[NEXP:128, :], io[name + "_s"]).then_inc(ld, 16)
            sp.dma_start(w1e[:], io["W1_e"].rearrange("n d h -> d n h")).then_inc(ld_e, 16)
            sp.dma_start(w2e[:], io["W2_e"].rearrange("n d h -> d n h")).then_inc(ld_e, 16)
            sp.dma_start(b1e[:], io["b1_eT"]).then_inc(ld_e, 16)
            sp.wait_ge(e2_ok, 4)
            sp.dma_start(io["scratch"], oE[:]).then_inc(e_moved, 16)
            sp.wait_ge(e_moved, 16)
            sp.dma_start(oE_pos[:], io["scratch"].rearrange("b n d -> n b d")).then_inc(e_moved, 16)
            for q in range(NGRP):
                sp.wait_ge(no, q + 1)
                sp.dma_start(io["out"].rearrange("b p d -> p b d")[:, q * GRP:(q + 1) * GRP, :],
                             outt[:, q * GRP:(q + 1) * GRP, :]).then_inc(stored, 16)
            sp.wait_ge(stored, 16 * NGRP)

        @block.tensor
        def _(pe):
            pe.wait_ge(wlo, 2)
            pe.wait_ge(ld, 16 * NLD)

            def group(t):
                for c in range(FF // 128):
                    wait(pe, h_ok, 4 * t + c - 3)
                    mm_split(nc, banks[c][:], fc1, np.s_[:, c * 128:(c + 1) * 128], k.x1T,
                             np.s_[:, bass.ds(t * GCOLS, GCOLS)]).then_inc(fc1_mm, 1)
                wait(pe, h_ok, 4 * (t + 1))
                wait(pe, r_ok, t)
                for b in range(GRP):
                    for c in range(FF // 128):
                        last = nc.tensor.matmul(banks[4][:, b * 128:(b + 1) * 128], hT[:, c, b, :], fc2[:, c, :],
                                                start=(c == 0), stop=(c == FF // 128 - 1))
                last.then_inc(fc2_mm, 1)
                wait(pe, z_ok, t + 1)
                wait(pe, ze_ok, t)
                for b in range(GRP):
                    last = nc.tensor.transpose(banks[5][:, b * 128:(b + 1) * 128], N5[:, b, :], k.ident[:])
                last.then_inc(zT_mm, 1)
                wait(pe, z_lo, t + 1)
                wait(pe, g_ok, t)
                mm_split(nc, banks[6][:], w1, np.s_[:, :], zT, np.s_[:, :, :]).then_inc(w1_mm, 1)
                wait(pe, g_ok, t + 1)
                wait(pe, res_ok, t)
                for b in range(GRP):
                    last = nc.tensor.matmul(banks[7][:, b * 128:(b + 1) * 128], gT[:, b, :], w2[:], start=True,
                                            stop=True)
                last.then_inc(w2_mm, 1)

            looped(pe, NGRP, group)
            pe.wait_ge(ld_e, 48)
            pe.wait_ge(ze_ok, NGRP)
            for e in range(NEXP):
                last = nc.tensor.matmul(banks[0][:, e * NSEQ:(e + 1) * NSEQ], w1e[:, e, :], zE[:, :, e],
                                        start=True, stop=True)
            last.then_inc(e1_mm, 1)
            pe.wait_ge(e1_g, 1)
            for q in range(4):
                for e in range(4):
                    last = nc.tensor.matmul(banks[1 + q][0:NSEQ, e * 128:(e + 1) * 128], hE[:, 4 * q + e, :],
                                            w2e[:, 4 * q + e, :], start=True, stop=True)
                last.then_inc(e2_mm, 1)

        @block.scalar
        def _(act):
            act.wait_ge(ld_w, 32)
            nc.scalar.activation(fc1.hi[:], fc1_raw[:], ACT.Copy).then_inc(f1hi, 1)
            nc.scalar.activation(w1.hi[:], w1_raw[:], ACT.Copy).then_inc(f1hi, 1)
            act.wait_ge(ld, 16 * NLD)
            act.wait_ge(zeroed, 1)

            def group(t):
                for c in range(FF // 128):
                    wait(act, fc1_mm, 4 * t + c + 1)
                    if c == 0:
                        wait(act, fc2_mm, t)
                    nc.scalar.activation(hT[:, c], quarter(c), ACT.Gelu, bias=fc1_b[:, c:c + 1]).then_inc(h_ok, 1)
                wait(act, zT_mm, t + 1)
                nc.scalar.activation(zT.hi[:], quarter(5), ACT.Copy).then_inc(z_hi, 1)
                wait(act, w1_mm, t + 1)
                nc.scalar.activation(gT[:, :, NEXP:], quarter(6)[:, :, NEXP:], ACT.Gelu, bias=b1[:, 0:1]).then_inc(g_ok, 1)

            looped(act, NGRP, group)
            act.wait_ge(e1_b, 1)
            nc.scalar.activation(hE[:], hE[:], ACT.Gelu).then_inc(e1_g, 1)
            for q in range(4):
                act.wait_ge(e2_mm, q + 1)
                nc.scalar.activation(oE[:, 4 * q:4 * q + 4, :],
                                     banks[1 + q][0:NSEQ, :].rearrange("p (e d) -> p e d", e=4),
                                     ACT.Copy).then_inc(e2_ok, 1)

        @block.vector
        def _(vec):
            vec.wait_ge(f1hi, 2)
            nc.vector.tensor_tensor(fc1.lo[:], fc1_raw[:], f32(fc1.hi[:]), ALU.subtract).then_inc(wlo, 1)
            nc.vector.tensor_tensor(w1.lo[:], w1_raw[:], f32(w1.hi[:]), ALU.subtract).then_inc(wlo, 1)
            vec.wait_ge(ld, 16 * NLD)

            def statistics(t, i, src):
                for b in range(GRP):
                    last = nc.vector.bn_stats(stats[:, i, b], src[:, b])
                last.then_inc(st, 1)
                wait_apart(vec, st, 3 * t + i + 1, spare)
                for b in range(GRP):
                    last = nc.vector.bn_aggr(mv[:, i, b], stats[:, i, b])
                last.then_inc(mvs, 1)

            def normalise(t, i, dst, src):
                wait(vec, rstd_ok, 3 * t + i + 1)
                for b in range(GRP):
                    last = nc.vector.tensor_scalar(dst[:, b], src[:, b], mv[:, i, b, 0:1], rstd[:, i, b:b + 1],
                                                   ALU.subtract, ALU.mult)
                last.then_inc(nrm, 1)

            def group(t):
                seqs = bass.ds(t * GRP, GRP)
                wait(vec, fc2_mm, t + 1)
                nc.vector.tensor_tensor(R[:], quarter(4), k.xres[:, seqs, :], ALU.add).then_inc(r_ok, 1)
                wait(vec, r_ok, t + 1)
                statistics(t, 0, R)
                wait(vec, x4a, t)
                normalise(t, 0, N3, R)
                wait(vec, x4a, t + 1)
                statistics(t, 1, N3)
                wait(vec, x4b, t)
                normalise(t, 1, X4, N3)
                wait(vec, nrm, 3 * t + 2)
                statistics(t, 2, X4)
                wait(vec, zT_mm, t)
                normalise(t, 2, N5, X4)
                wait(vec, z_hi, t + 1)
                nc.vector.tensor_tensor(zT.lo[:], quarter(5), f32(zT.hi[:]), ALU.subtract).then_inc(z_lo, 1)
                nc.vector.tensor_copy(zE[:, seqs, :], quarter(5)[:, :, 0:NEXP]).then_inc(ze_ok, 1)
                wait(vec, w2_mm, t + 1)
                wait(vec, x4b, t + 1)
                nc.vector.tensor_tensor(res[:, seqs, :], quarter(7), X4[:], ALU.add).then_inc(res_ok, 1)

            looped(vec, NGRP, group)
            vec.wait_ge(e1_mm, 1)
            vec.wait_ge(ld_e, 48)
            nc.vector.tensor_tensor(hE[:], banks[0][:, 0:NEXP * NSEQ].rearrange("p (e b) -> p e b", e=NEXP),
                                    b1e[:].unsqueeze(2).to_broadcast([128, NEXP, NSEQ]), ALU.add).then_inc(e1_b, 1)
            vec.wait_ge(x4a, NGRP)
            vec.wait_ge(e_added, 1)
            for b in range(NSEQ):
                last = nc.vector.bn_stats(stats_o[:, b], res[:, b])
            last.then_inc(so, 1)
            vec.wait_ge(so, 1)
            for b in range(NSEQ):
                last = nc.vector.bn_aggr(mv_o[:, b], stats_o[:, b])
            last.then_inc(mo, 1)
            vec.wait_ge(ro, 1)
            for b in range(NSEQ):
                last = nc.vector.tensor_scalar(outt[:, b], res[:, b], mv_o[:, b, 0:1], rstd_o[:, b:b + 1],
                                               ALU.subtract, ALU.mult)
                if b % GRP == GRP - 1:
                    last.then_inc(no, 1)

        @block.gpsimd
        def _(pool):
            nc.gpsimd.memset(gT[:], 0.0).then_inc(zeroed, 1)
            pool.wait_ge(ld, 16 * NLD)

            def row(r, n=GRP):
                return r[:].unsqueeze(1).to_broadcast([128, n, 128])

            def inverse_deviation(t, i):
                wait(pool, mvs, 3 * t + i + 1)
                nc.gpsimd.tensor_tensor(rstd[:, i], mv[:, i, :, 1], k.eps[:, 0:GRP], ALU.add).then_inc(eps_ok, 1)
                wait(pool, eps_ok, 3 * t + i + 1)
                nc.gpsimd.tensor_tensor(rstd[:, i], rstd[:, i], k.half_neg[:, 0:GRP], ALU.pow).then_inc(rstd_ok, 1)

            def group(t):
                seqs = bass.ds(t * GRP, GRP)
                inverse_deviation(t, 0)
                wait(pool, nrm, 3 * t + 1)
                nc.gpsimd.tensor_tensor(N3[:], N3[:], row(rows3["ln3_g"]), ALU.mult).then_inc(g3, 1)
                wait(pool, g3, t + 1)
                nc.gpsimd.tensor_tensor(N3[:], N3[:], row(rows3["ln3_b"]), ALU.add).then_inc(b3, 1)
                wait_apart(pool, b3, t + 1, spare)
                nc.gpsimd.tensor_tensor(N3[:], N3[:], k.x1[:, seqs, :], ALU.add).then_inc(x4a, 1)
                inverse_deviation(t, 1)
                inverse_deviation(t, 2)
                wait(pool, nrm, 3 * t + 3)
                nc.gpsimd.tensor_tensor(N5[:], N5[:], row(gain), ALU.mult).then_inc(g5, 1)
                wait(pool, g5, t + 1)
                nc.gpsimd.tensor_tensor(N5[:], N5[:], row(shift), ALU.add).then_inc(z_ok, 1)
                nc.gpsimd.tensor_tensor(X4[:], X4[:], row(bias2), ALU.add).then_inc(x4b, 1)

            looped(pool, NGRP, group)
            pool.wait_ge(e_moved, 32)
            pool.wait_ge(res_ok, NGRP)
            nc.gpsimd.tensor_tensor(res[0:NEXP], res[0:NEXP], oE_pos[:], ALU.add).then_inc(e_added, 1)
            pool.wait_ge(mo, 1)
            nc.gpsimd.tensor_tensor(rstd_o[:], mv_o[:, :, 1], k.eps[:], ALU.add).then_inc(eo, 1)
            pool.wait_ge(eo, 1)
            nc.gpsimd.tensor_tensor(rstd_o[:], rstd_o[:], k.half_neg[:], ALU.pow).then_inc(ro, 1)


def build(nc, io):
    k = Kernel(nc, io)
    with ExitStack() as ctx:
        allocate(k, ctx)
        with ExitStack() as inner:
            allocate_attention(k, inner)
            setup_and_mixer(k)
            attention(k, "sa", k.x1T, k.x1T, k.m_sa, k.wv_sa, k.wo_sa, k.rows["ln1_g"], k.rows["ln1_b"],
                      k.rows["ca_bo"], k.x2T)
            attention(k, "ca", k.x2T, k.ctxT, k.m_ca, k.wv_ca, k.wo_ca, k.rows["ln2_g"], k.rows["ln2_b"],
                      k.rows["fc2_b"], k.x1T)
        feed_forward(k)


def layouts(a):
    tall = {"x": a["x"], "xT": a["x"].transpose(2, 0, 1).reshape(D, T),
            "ctxT": a["ctx_1024"].transpose(2, 0, 1).reshape(D, T),
            "mask": a["mask_BxS2_bk0"],
            "short_bT": a["L0_attn_short_b"].reshape(3, D).T, "b_inT": a["L0_attn_b_in"].reshape(3, D).T,
            "fc1_bT": a["L0_xattn_fc1_b"].reshape(FF // D, D).T, "b1_eT": a["L0_ffn_b1_e"].T}
    for n in "W_in short_w inner_w inner_b W_out b_out".split():
        tall[n] = a["L0_attn_" + n]
    for s in ("sa", "ca"):
        for n in ("wq", "wk"):
            tall[f"{s}_{n}T"] = a[f"L0_xattn_{s}_{n}"].T
        for n in ("wv", "wo", "bo"):
            tall[f"{s}_{n}"] = a[f"L0_xattn_{s}_{n}"]
    for n in "ln1_g ln1_b ln2_g ln2_b ln3_g ln3_b fc1_w fc2_w fc2_b".split():
        tall[n] = a["L0_xattn_" + n]
    for n in "g_e b_e W1_e W2_e b2_e g_s b_s W1_s b1_s W2_s b2_s".split():
        tall[n] = a["L0_ffn_" + n]
    return {n: np.ascontiguousarray(v) for n, v in tall.items()}


def kernel(**inputs):
    from concourse import bacc
    from concourse.bass_utils import run_bass_kernel_spmd

    nc = bacc.Bacc("TRN2", target_bir_lowering=False, num_devices=1)
    arrays = layouts({n: np.asarray(v) for n, v in inputs.items()})
    io = {n: nc.dram_tensor("in_" + n, v.shape, mybir.dt.from_np(v.dtype), kind="ExternalInput").ap()
          for n, v in arrays.items()}
    io["scratch"] = nc.dram_tensor("experts_out", (NSEQ, NEXP, D), F32, kind="Internal").ap()
    io["out"] = nc.dram_tensor("out", (NSEQ, L, D), F32, kind="ExternalOutput").ap()
    build(nc, io)
    result = run_bass_kernel_spmd(nc, [{"in_" + n: v for n, v in arrays.items()}], core_ids=[0])
    return result.results[0]["out"]
```

```python
from contextlib import ExitStack

import numpy as np

import concourse.bass as bass
from concourse import mybir

F32 = mybir.dt.float32
F32R = mybir.dt.float32r
BF16 = mybir.dt.bfloat16
U8 = mybir.dt.uint8
ALU = mybir.AluOpType
ACT = mybir.ActivationFunctionType
AX_X = mybir.AxisListType.X

NSEQ, L, D = 16, 128, 128
H, DH = 16, 64
INNER = H * DH
FF = 512
NEXP = 16
EPS = 1e-5
SCALE = DH ** -0.5
MASKED = -(2.0 ** 100)
T = NSEQ * L
PAIR = 2
NPAIR = NSEQ // PAIR
PCOLS = PAIR * L
HQ = 4
QUADS = PAIR * H // HQ
UNITS = H // 2
GRP = 4
NGRP = NSEQ // GRP
GCOLS = GRP * L
Y_AHEAD, T_LAG, PV_LAG = 4, 2, 3
P_RING = 4


def wait(engine, sem, value):
    if isinstance(value, int) and value <= 0:
        return
    engine.wait_ge(sem, value)


def wait_apart(engine, sem, value, spare):
    wait(engine, sem, value)
    engine.sem_inc(spare, 1)


def f32(ap):
    return ap.bitcast(F32)


def looped(engine, count, body):
    body(0)
    with engine.Fori(1, count - 1) as t:
        body(t)
    body(count - 1)


class Split:

    def __init__(self, hi, lo):
        self.hi, self.lo = hi, lo


def mm_split(nc, out, w, wsel, x, xsel, first=True):
    nc.tensor.matmul(out, w.hi[wsel], x.hi[xsel], start=first, stop=False)
    nc.tensor.matmul(out, w.hi[wsel], x.lo[xsel], start=False, stop=False)
    return nc.tensor.matmul(out, w.lo[wsel], x.hi[xsel], start=False, stop=True)


class Kernel:
    def __init__(self, nc, io):
        self.nc, self.io = nc, io

    def sb(self, ctx, name, shape, dt=F32):
        return ctx.enter_context(self.nc.sbuf_tensor(name, shape, dt))

    def split(self, ctx, name, shape):
        return Split(self.sb(ctx, name + "_hi", shape, F32R), self.sb(ctx, name + "_lo", shape, F32R))

    def banks(self, ctx, tag):
        return [ctx.enter_context(self.nc.psum_tensor(f"{tag}_bank{i}", [128, 512], F32)) for i in range(8)]

    def sems(self, ctx, tag, names):
        return [ctx.enter_context(self.nc.semaphore(f"{tag}_{n}")) for n in names.split()]


def allocate(k, ctx):
    sb, split = k.sb, k.split
    k.ident = sb(ctx, "ident", [128, 128])
    k.half_neg = sb(ctx, "half_neg", [128, NSEQ])
    k.eps = sb(ctx, "eps", [128, NSEQ])
    k.one = sb(ctx, "one", [128, 1])
    k.rows = {n: sb(ctx, "row_" + n, [128, 128]) for n in
              "sa_bo ca_bo ln1_g ln1_b ln2_g ln2_b fc2_b".split()}
    k.x1 = sb(ctx, "x1", [128, NSEQ, 128])
    k.xres = sb(ctx, "xres", [128, NSEQ, 128])
    k.x1T = split(ctx, "x1T", [128, T])


def allocate_attention(k, ctx):
    sb, split = k.sb, k.split
    k.ones_row0 = sb(ctx, "ones_row0", [128, 128], BF16)
    k.maskb = sb(ctx, "maskb", [128, T], BF16)
    k.m_sa = split(ctx, "m_sa", [128, H, 128])
    k.m_ca = split(ctx, "m_ca", [128, H, 128])
    k.wv_sa = split(ctx, "wv_sa", [128, INNER])
    k.wv_ca = split(ctx, "wv_ca", [128, INNER])
    k.wo_sa = sb(ctx, "wo_sa", [128, H // 2, 128])
    k.wo_ca = sb(ctx, "wo_ca", [128, H // 2, 128])
    k.x2T = split(ctx, "x2T", [128, T])
    k.ctxT = split(ctx, "ctxT", [128, T])


def row_broadcast(nc, engine, dst, src_row):
    return engine.dma_start(dst, src_row.partition_broadcast(dst.shape[0]))


def setup_and_mixer(k):
    nc, io = k.nc, k.io
    with ExitStack() as ctx:
        x_tok = k.sb(ctx, "x_tok", [128, NSEQ, 128])
        xT_in = k.sb(ctx, "xT_in", [128, T])
        c_in = k.sb(ctx, "c_in", [128, T])
        xT = k.x2T
        w_in_raw = k.sb(ctx, "w_in_raw", [128, 3 * D])
        w_in = k.split(ctx, "w_in", [128, 3 * D])
        w_out = k.sb(ctx, "w_out", [128, D])
        wv_raw = k.sb(ctx, "wv_raw", [128, INNER])
        qkT = k.sb(ctx, "qkT", [DH, 2, H, 128])
        mask_raw = k.sb(ctx, "mask_raw", [1, T], U8)
        taps = k.sb(ctx, "taps", [128, 3, 3])
        short_b = k.sb(ctx, "short_b", [128, 3])
        b_in = k.sb(ctx, "b_in", [128, 3])
        inner = k.sb(ctx, "inner", [128, 4])
        inner_b = k.sb(ctx, "inner_b", [128, 1])
        b_out = k.sb(ctx, "b_out", [128, 128])
        U = k.sb(ctx, "U", [128, 3, GRP, L + 2])
        C = k.sb(ctx, "C", [128, 3, GRP, L])
        KV = k.sb(ctx, "KV", [128, GRP, L + 3])
        G = k.sb(ctx, "G", [128, GRP, L])
        yT = k.sb(ctx, "yT", [128, GRP, L])
        R = k.sb(ctx, "R", [128, GRP, 128])
        N1 = k.sb(ctx, "N1", [128, GRP, 128])
        stats = k.sb(ctx, "stats", [128, GRP, 6])
        mv = k.sb(ctx, "mv", [128, GRP, 2])
        rstd = k.sb(ctx, "rstd", [128, GRP])
        banks = k.banks(ctx, "mix")
        (ld_x, ld_win, ld_small, ld_qk, ld_wv, ld_keep, ld_ctx, ident0, ident_ok, consts_ok, pads_ok,
         xhi, xlo, whi, wlo, chi, clo, mm_m, m_hi, m_lo, wv_hi, wv_lo, mask_ok,
         u_mm, u_ev, dve, kv_ok, y_ok, o_mm, r_ok, stat_ok, eps_ok, rstd_ok, n_ok, xT_mm, x1hi, x1lo,
         xb_ok, res_ok, spare) = k.sems(ctx, "mix", """ld_x ld_win ld_small ld_qk ld_wv ld_keep ld_ctx ident0
            ident_ok consts_ok pads_ok xhi xlo whi wlo chi clo mm_m m_hi m_lo wv_hi wv_lo mask_ok
            u_mm u_ev dve kv_ok y_ok o_mm r_ok stat_ok eps_ok rstd_ok n_ok xT_mm x1hi x1lo xb_ok
            res_ok spare""")
        block = ctx.enter_context(nc.Block())
        KEPT = 2 + len(k.rows)

        @block.sync
        def _(sp):
            sp.dma_start(xT_in[:], io["xT"]).then_inc(ld_x, 16)
            sp.dma_start(w_in_raw[:], io["W_in"]).then_inc(ld_win, 16)
            sp.dma_start(taps[:], io["short_w"].rearrange("(c p) j -> p c j", p=128)).then_inc(ld_small, 16)
            sp.dma_start(short_b[:], io["short_bT"]).then_inc(ld_small, 16)
            sp.dma_start(b_in[:], io["b_inT"]).then_inc(ld_small, 16)
            sp.dma_start(inner[:], io["inner_w"]).then_inc(ld_small, 16)
            sp.dma_start(inner_b[:], io["inner_b"].rearrange("(p o) -> p o", o=1)).then_inc(ld_small, 16)
            sp.dma_start(x_tok[:], io["x"].rearrange("b p d -> p b d")).then_inc(ld_small, 16)
            row_broadcast(nc, sp, b_out[:], io["b_out"]).then_inc(ld_small, 16)
            sp.dma_start(w_out[:], io["W_out"]).then_inc(ld_small, 16)
            for n, tile in k.rows.items():
                row_broadcast(nc, sp, tile[:], io[n]).then_inc(ld_keep, 16)
            sp.dma_start(k.wo_sa[:], io["sa_wo"].rearrange("(c p) n -> p c n", p=128)).then_inc(ld_keep, 16)
            sp.dma_start(k.wo_ca[:], io["ca_wo"].rearrange("(c p) n -> p c n", p=128)).then_inc(ld_keep, 16)
            sp.wait_ge(ld_keep, 16 * KEPT)

        @block.scalar
        def _(act):
            act.dma_start(qkT[:, 0], io["sa_wqT"].rearrange("(h j) d -> j h d", j=DH)).then_inc(ld_qk, 16)
            act.dma_start(qkT[:, 1], io["sa_wkT"].rearrange("(h j) d -> j h d", j=DH)).then_inc(ld_qk, 16)
            act.dma_start(wv_raw[:], io["sa_wv"]).then_inc(ld_wv, 16)
            act.dma_start(c_in[:], io["ctxT"]).then_inc(ld_ctx, 16)
            act.dma_start(mask_raw[:], io["mask"].rearrange("(o b) p -> o (b p)", o=1)).then_inc(ld_ctx, 16)
            act.wait_ge(ld_x, 16)
            nc.scalar.activation(xT.hi[:], xT_in[:], ACT.Copy).then_inc(xhi, 1)
            act.wait_ge(ld_win, 16)
            nc.scalar.activation(w_in.hi[:], w_in_raw[:], ACT.Copy).then_inc(whi, 1)
            act.wait_ge(ld_small, 16 * 8)
            act.wait_ge(pads_ok, 2)

            def mixer(t):
                for c in range(3):
                    wait(act, u_mm, 3 * t + c + 1)
                    if c == 0:
                        wait(act, kv_ok, t)
                    nc.scalar.activation(U[:, c, :, 2:], banks[c][:].rearrange("p (b l) -> p b l", b=GRP),
                                         ACT.Identity, bias=b_in[:, c:c + 1]).then_inc(u_ev, 1)
                wait(act, xT_mm, t + 1)
                nc.scalar.activation(k.x1T.hi[:, bass.ds(t * GCOLS, GCOLS)], banks[4][:],
                                     ACT.Copy).then_inc(x1hi, 1)

            looped(act, NGRP, mixer)
            act.wait_ge(ld_ctx, 32)
            nc.scalar.activation(k.ctxT.hi[:], c_in[:], ACT.Copy).then_inc(chi, 1)
            for a, (m, wv) in enumerate(((k.m_sa, k.wv_sa), (k.m_ca, k.wv_ca))):
                for q in range(H // HQ):
                    i = a * H // HQ + q
                    act.wait_ge(mm_m, i + 1)
                    nc.scalar.activation(m.hi[:, q * HQ:(q + 1) * HQ, :],
                                         banks[5 + i % 2][:].rearrange("p (h d) -> p h d", h=HQ),
                                         ACT.Copy, scale=SCALE).then_inc(m_hi, 1)
                if a == 0:
                    act.wait_ge(mm_m, H // HQ)
                    act.dma_start(qkT[:, 0], io["ca_wqT"].rearrange("(h j) d -> j h d", j=DH)).then_inc(ld_qk, 16)
                    act.dma_start(qkT[:, 1], io["ca_wkT"].rearrange("(h j) d -> j h d", j=DH)).then_inc(ld_qk, 16)
                act.wait_ge(ld_wv, 16 * (a + 1))
                nc.scalar.activation(wv.hi[:], wv_raw[:], ACT.Copy).then_inc(wv_hi, 1)
                if a == 0:
                    act.wait_ge(wv_lo, 1)
                    act.dma_start(wv_raw[:], io["ca_wv"]).then_inc(ld_wv, 16)

        @block.gpsimd
        def _(pool):
            nc.gpsimd.memset(k.ident[:], 0.0).then_inc(ident0, 1)
            pool.wait_ge(ident0, 1)
            nc.gpsimd.affine_select(out=k.ident[:], in_=k.ident[:], compare_op=ALU.not_equal, fill=1.0, base=0,
                                    pattern=[[-1, 128]], channel_multiplier=1).then_inc(ident_ok, 1)
            nc.gpsimd.memset(U[:], 0.0).then_inc(pads_ok, 1)
            nc.gpsimd.memset(KV[:], 0.0).then_inc(pads_ok, 1)
            nc.gpsimd.memset(k.half_neg[:], -0.5).then_inc(consts_ok, 1)
            nc.gpsimd.memset(k.eps[:], EPS).then_inc(consts_ok, 1)
            nc.gpsimd.memset(k.one[:], 1.0).then_inc(consts_ok, 1)
            nc.gpsimd.memset(k.maskb[:], 0.0).then_inc(consts_ok, 1)
            nc.gpsimd.memset(k.ones_row0[:], 0.0).then_inc(consts_ok, 1)
            pool.wait_ge(consts_ok, 5)
            nc.gpsimd.memset(k.ones_row0[0:1, :], 1.0).then_inc(consts_ok, 1)
            pool.wait_ge(ld_small, 16 * 8)
            nc.gpsimd.tensor_tensor(x_tok[:], x_tok[:], b_out[:].unsqueeze(1).to_broadcast([128, NSEQ, 128]),
                                    ALU.add).then_inc(xb_ok, 1)
            pool.wait_ge(ld_keep, 16 * KEPT)

            def mixer(t):
                wait(pool, stat_ok, t + 1)
                nc.gpsimd.tensor_tensor(rstd[:], mv[:, :, 1], k.eps[:, 0:GRP], ALU.add).then_inc(eps_ok, 1)
                wait(pool, eps_ok, t + 1)
                nc.gpsimd.tensor_tensor(rstd[:], rstd[:], k.half_neg[:, 0:GRP], ALU.pow).then_inc(rstd_ok, 1)
                wait_apart(pool, n_ok, GRP * (t + 1), spare)
                nc.gpsimd.tensor_tensor(k.xres[:, bass.ds(t * GRP, GRP), :], N1[:],
                                        k.rows["sa_bo"][:].unsqueeze(1).to_broadcast([128, GRP, 128]),
                                        ALU.add).then_inc(res_ok, 1)
                nc.gpsimd.tensor_tensor(k.x1[:, bass.ds(t * GRP, GRP), :], N1[:],
                                        k.one[:].unsqueeze(1).to_broadcast([128, GRP, 128]),
                                        ALU.mult).then_inc(res_ok, 1)

            looped(pool, NGRP, mixer)

        @block.vector
        def _(vec):
            vec.wait_ge(xhi, 1)
            nc.vector.tensor_tensor(xT.lo[:], xT_in[:], f32(xT.hi[:]), ALU.subtract).then_inc(xlo, 1)
            vec.wait_ge(whi, 1)
            nc.vector.tensor_tensor(w_in.lo[:], w_in_raw[:], f32(w_in.hi[:]), ALU.subtract).then_inc(wlo, 1)
            vec.wait_ge(ld_small, 16 * 8)
            vec.wait_ge(pads_ok, 2)
            CH = 3 + 2 + 4 + 2

            def mixer(t):
                link = [0]

                def then(ins):
                    link[0] += 1
                    ins.then_inc(dve, 1)
                    wait(vec, dve, CH * t + link[0])

                for c in range(3):
                    wait(vec, u_ev, 3 * t + c + 1)
                    nc.vector.tensor_scalar(C[:, c], U[:, c, :, 2:2 + L], taps[:, c, 2:3], short_b[:, c:c + 1],
                                            ALU.mult, ALU.add).then_inc(dve, 1)
                    link[0] += 1
                for j in range(2):
                    for c in range(3):
                        if c == 0:
                            wait(vec, dve, CH * t + link[0])
                        last = nc.vector.scalar_tensor_tensor(C[:, c], U[:, c, :, j:j + L], taps[:, c, j:j + 1],
                                                              C[:, c], ALU.mult, ALU.add)
                    last.then_inc(dve, 1)
                    link[0] += 1
                wait(vec, dve, CH * t + link[0])
                last = nc.vector.tensor_tensor(KV[:, :, 3:], C[:, 1], C[:, 2], ALU.mult)
                last.then_inc(kv_ok, 1)
                wait(vec, kv_ok, t + 1)
                then(nc.vector.tensor_scalar(G[:], KV[:, :, 3:3 + L], inner[:, 3:4], inner_b[:, 0:1],
                                             ALU.mult, ALU.add))
                for j in range(3):
                    then(nc.vector.scalar_tensor_tensor(G[:], KV[:, :, j:j + L], inner[:, j:j + 1], G[:],
                                                        ALU.mult, ALU.add))
                wait(vec, o_mm, t)
                nc.vector.tensor_tensor(yT[:], C[:, 0], G[:], ALU.mult).then_inc(y_ok, 1)
                wait(vec, o_mm, t + 1)
                if isinstance(t, int) and t == 0:
                    vec.wait_ge(xb_ok, 1)
                then(nc.vector.tensor_tensor(R[:], banks[3][:].rearrange("p (b d) -> p b d", b=GRP),
                                             x_tok[:, bass.ds(t * GRP, GRP), :], ALU.add))
                for b in range(GRP):
                    last = nc.vector.bn_stats(stats[:, b], R[:, b])
                then(last)
                vec.sem_inc(spare, 1)
                for b in range(GRP):
                    last = nc.vector.bn_aggr(mv[:, b], stats[:, b])
                last.then_inc(stat_ok, 1)
                wait(vec, rstd_ok, t + 1)
                wait(vec, xT_mm, t)
                wait(vec, res_ok, 2 * t)
                for b in range(GRP):
                    nc.vector.tensor_scalar(N1[:, b], R[:, b], mv[:, b, 0:1], rstd[:, b:b + 1],
                                            ALU.subtract, ALU.mult).then_inc(n_ok, 1)
                wait(vec, x1hi, t + 1)
                last = nc.vector.tensor_tensor(k.x1T.lo[:, bass.ds(t * GCOLS, GCOLS)], banks[4][:],
                                               f32(k.x1T.hi[:, bass.ds(t * GCOLS, GCOLS)]), ALU.subtract)
                last.then_inc(x1lo, 1)
                assert link[0] == CH

            looped(vec, NGRP, mixer)
            vec.wait_ge(ld_ctx, 32)
            vec.wait_ge(consts_ok, 6)
            nc.vector.tensor_scalar(k.maskb[0:1, :], mask_raw[:], MASKED, None, ALU.mult).then_inc(mask_ok, 1)
            vec.wait_ge(chi, 1)
            nc.vector.tensor_tensor(k.ctxT.lo[:], c_in[:], f32(k.ctxT.hi[:]), ALU.subtract).then_inc(clo, 1)
            for a, (m, wv) in enumerate(((k.m_sa, k.wv_sa), (k.m_ca, k.wv_ca))):
                for q in range(H // HQ):
                    i = a * H // HQ + q
                    vec.wait_ge(m_hi, i + 1)
                    sl = m.hi[:, q * HQ:(q + 1) * HQ, :]
                    nc.vector.scalar_tensor_tensor(m.lo[:, q * HQ:(q + 1) * HQ, :],
                                                   banks[5 + i % 2][:].rearrange("p (h d) -> p h d", h=HQ), SCALE,
                                                   f32(sl), ALU.mult, ALU.subtract).then_inc(m_lo, 1)
                vec.wait_ge(wv_hi, a + 1)
                nc.vector.tensor_tensor(wv.lo[:], wv_raw[:], f32(wv.hi[:]), ALU.subtract).then_inc(wv_lo, 1)

        @block.tensor
        def _(pe):
            pe.wait_ge(xlo, 1)
            pe.wait_ge(wlo, 1)
            pe.wait_ge(ident_ok, 1)
            pe.wait_ge(ld_small, 16 * 8)

            def mixer(t):
                for c in range(3):
                    wait(pe, u_ev, 3 * t + c - 2)
                    mm_split(nc, banks[c][:], w_in, np.s_[:, c * D:(c + 1) * D], xT,
                             np.s_[:, bass.ds(t * GCOLS, GCOLS)]).then_inc(u_mm, 1)
                wait(pe, y_ok, t + 1)
                for b in range(GRP):
                    last = nc.tensor.matmul(banks[3][:, b * 128:(b + 1) * 128], yT[:, b, :], w_out[:],
                                            start=True, stop=True)
                last.then_inc(o_mm, 1)
                wait(pe, n_ok, GRP * (t + 1))
                wait(pe, x1lo, t)
                for b in range(GRP):
                    last = nc.tensor.transpose(banks[4][:, b * 128:(b + 1) * 128], N1[:, b, :], k.ident[:])
                last.then_inc(xT_mm, 1)

            looped(pe, NGRP, mixer)
            for a in range(2):
                pe.wait_ge(ld_qk, 32 * (a + 1))
                for q in range(H // HQ):
                    i = a * H // HQ + q
                    wait(pe, m_lo, i - 1)
                    for h in range(HQ):
                        last = nc.tensor.matmul(banks[5 + i % 2][:, h * 128:(h + 1) * 128], qkT[:, 1, q * HQ + h, :],
                                                qkT[:, 0, q * HQ + h, :], start=True, stop=True)
                    last.then_inc(mm_m, 1)


def attention(k, tag, qT, kvT, m, wv, wo, g_row, b_row, next_bias, outT):
    nc = k.nc
    with ExitStack() as ctx:
        xq = k.split(ctx, tag + "xq", [128, PAIR, 128])
        xv = k.split(ctx, tag + "xv", [128, PAIR, 128])
        y = k.split(ctx, tag + "y", [128, PAIR, H, 128])
        V = k.sb(ctx, tag + "V", [128, PAIR, INNER])
        P = k.sb(ctx, tag + "P", [128, P_RING, HQ, 128])
        PT = k.sb(ctx, tag + "PT", [128, 2, HQ * 128])
        OT = k.sb(ctx, tag + "OT", [128, PAIR, H // 2, 128])
        negmax = k.sb(ctx, tag + "negmax", [128, 2, HQ])
        total = k.sb(ctx, tag + "total", [128, 2, HQ])
        inv = k.sb(ctx, tag + "inv", [128, 2, HQ])
        R = k.sb(ctx, tag + "R", [128, PAIR, 128])
        N = k.sb(ctx, tag + "N", [128, PAIR, 128])
        X = k.sb(ctx, tag + "X", [128, PAIR, 128])
        stats = k.sb(ctx, tag + "stats", [128, PAIR, 6])
        mv = k.sb(ctx, tag + "mv", [128, PAIR, 2])
        rstd = k.sb(ctx, tag + "rstd", [128, PAIR])
        banks = k.banks(ctx, tag)
        Y_BANK, S_BANK, PT_BANK, O_BANK, V_BANK, W_BANK = (0, 1), (2, 3), 4, 5, 6, 7
        (y_mm, y_hi, y_lo, s_mm, max_ok, exp_ok, inv_ok, norm_ok, t_mm, pt_ok, pv_mm, o_ok, v_mm, v_ok,
         xq_ok, xv_ok, wo_mm, r_ok, st_ok, mv_ok, eps_ok, rstd_ok, n_ok, gain_ok, x_ok, res_ok, xT_mm, xT_hi,
         xT_lo, spare) = k.sems(ctx, tag, """y_mm y_hi y_lo s_mm max_ok exp_ok inv_ok norm_ok t_mm pt_ok pv_mm o_ok
             v_mm v_ok xq_ok xv_ok wo_mm r_ok st_ok mv_ok eps_ok rstd_ok n_ok gain_ok x_ok res_ok xT_mm xT_hi
             xT_lo spare""")
        block = ctx.enter_context(nc.Block())
        V1_STEPS = (3, 4)
        V0_STEPS = (6, 7)
        XV_STEP = 5
        WO_STEP, XT_STEP = 3, 6

        def cols(t, n=PCOLS, off=0):
            return bass.ds(t * PCOLS + off, n)

        def exists(t):
            return not isinstance(t, int) or 0 <= t < NPAIR

        @block.tensor
        def _(pe):
            def y_unit(t, u):
                n = UNITS * t + u
                wait(pe, y_lo, n - 1)
                for j in range(2):
                    last = mm_split(nc, banks[Y_BANK[u % 2]][:, j * PCOLS:(j + 1) * PCOLS], m,
                                    np.s_[:, 2 * u + j, :], kvT, np.s_[:, cols(t)])
                last.then_inc(y_mm, 1)

            def scores(t, g):
                n, b, hq = QUADS * t + g, g % PAIR, g // PAIR
                wait(pe, y_lo, UNITS * t + 2 * hq + 2)
                if hq == 0:
                    wait(pe, xq_ok, PAIR * t + b + 1)
                wait(pe, exp_ok, n - 1)
                out = banks[S_BANK[g % 2]][:]
                nc.tensor.matmul(out, k.ones_row0[:],
                                 k.maskb[:, cols(t, 128, b * 128)].unsqueeze(1).to_broadcast([128, HQ, 128]),
                                 start=True, stop=False)
                mm_split(nc, out, xq, np.s_[:, b, :], y, np.s_[:, b, HQ * hq:HQ * (hq + 1), :],
                         first=False).then_inc(s_mm, 1)

            def transposes(n, g):
                wait(pe, norm_ok, n + 1)
                wait(pe, pt_ok, n)
                for h in range(HQ):
                    last = nc.tensor.transpose(banks[PT_BANK][:, h * 128:(h + 1) * 128], P[:, g % P_RING, h, :],
                                               k.ident[:])
                last.then_inc(t_mm, 1)

            def p_v(t, n, g):
                b, hq = g % PAIR, g // PAIR
                wait(pe, pt_ok, n + 1)
                wait(pe, v_ok, 4 * t + (2 if hq < 2 else 4))
                wait(pe, o_ok, n)
                for h in range(HQ):
                    part = 64 * (h % 2)
                    last = nc.tensor.matmul(banks[O_BANK][part:part + 64, (h // 2) * 128:(h // 2 + 1) * 128],
                                            V[:, b, (HQ * hq + h) * DH:(HQ * hq + h + 1) * DH],
                                            PT[:, g % 2, h * 128:(h + 1) * 128], start=True, stop=True)
                last.then_inc(pv_mm, 1)

            def v_half(i, t, b, half):
                wait(pe, xv_ok, t + 1)
                wait(pe, v_ok, i)
                mm_split(nc, banks[V_BANK][:], xv, np.s_[:, b, :], wv,
                         np.s_[:, half * 512:(half + 1) * 512]).then_inc(v_mm, 1)

            def out_proj(t):
                wait(pe, o_ok, QUADS * (t + 1))
                wait(pe, xT_lo, t)
                for b in range(PAIR):
                    for c in range(H // 2):
                        last = nc.tensor.matmul(banks[W_BANK][:, b * 128:(b + 1) * 128], OT[:, b, c, :], wo[:, c, :],
                                                start=(c == 0), stop=(c == H // 2 - 1))
                last.then_inc(wo_mm, 1)

            def x_transposes(t):
                wait(pe, x_ok, t + 1)
                for b in range(PAIR):
                    last = nc.tensor.transpose(banks[W_BANK][:, b * 128:(b + 1) * 128], X[:, b, :], k.ident[:])
                last.then_inc(xT_mm, 1)

            def pair(t):
                for g in range(QUADS):
                    n = QUADS * t + g
                    scores(t, g)
                    if g + Y_AHEAD < UNITS:
                        y_unit(t, g + Y_AHEAD)
                    elif exists(t + 1):
                        y_unit(t + 1, g + Y_AHEAD - UNITS)
                    back = 1 if g < T_LAG else 0
                    if exists(t - back):
                        transposes(n - T_LAG, (g - T_LAG) % QUADS)
                    if g == WO_STEP and exists(t - 1):
                        out_proj(t - 1)
                    back = 1 if g < PV_LAG else 0
                    if exists(t - back):
                        p_v(t - back, n - PV_LAG, (g - PV_LAG) % QUADS)
                    if g in V1_STEPS:
                        b = V1_STEPS.index(g)
                        v_half(4 * t + 2 + b, t, b, 1)
                    if g in V0_STEPS and exists(t + 1):
                        b = V0_STEPS.index(g)
                        v_half(4 * t + 4 + b, t + 1, b, 0)
                    if g == XT_STEP and exists(t - 1):
                        x_transposes(t - 1)

            for u in range(Y_AHEAD):
                y_unit(0, u)
            for b in range(PAIR):
                v_half(b, 0, b, 0)
            looped(pe, NPAIR, pair)
            N_ALL = QUADS * NPAIR
            for n in range(N_ALL, N_ALL + PV_LAG):
                if n - T_LAG < N_ALL:
                    transposes(n - T_LAG, (n - T_LAG) % QUADS)
                p_v(NPAIR - 1, n - PV_LAG, (n - PV_LAG) % QUADS)
            out_proj(NPAIR - 1)
            x_transposes(NPAIR - 1)

        @block.scalar
        def _(act):
            def exps(n, g):
                wait(act, max_ok, n + 1)
                for h in range(HQ):
                    last = nc.scalar.activation(P[:, g % P_RING, h, :], banks[S_BANK[g % 2]][:, h * 128:(h + 1) * 128],
                                                ACT.Exp, bias=negmax[:, g % 2, h:h + 1],
                                                accum_out=total[:, g % 2, h:h + 1])
                last.then_inc(exp_ok, 1)

            def y_high(t, u):
                n = UNITS * t + u
                wait(act, y_mm, n + 1)
                wait(act, s_mm, QUADS * (t - 1) + 2 * (u // 2) + 2)
                for b in range(PAIR):
                    last = nc.scalar.activation(
                        y.hi[:, b, 2 * u:2 * u + 2, :],
                        banks[Y_BANK[u % 2]][:].rearrange("p (h b l) -> p b h l", h=2, b=PAIR)[:, b], ACT.Copy)
                last.then_inc(y_hi, 1)

            def v_out(i, t, b, half):
                wait(act, v_mm, i + 1)
                wait(act, pv_mm, QUADS * (t - 1) + (4 if half == 0 else 8))
                nc.scalar.activation(V[:, b, half * 512:(half + 1) * 512], banks[V_BANK][:], ACT.Copy).then_inc(v_ok, 1)

            def xT_high(t):
                wait(act, xT_mm, t + 1)
                nc.scalar.activation(outT.hi[:, cols(t)], banks[W_BANK][:, 0:PCOLS], ACT.Copy).then_inc(xT_hi, 1)

            def o_out(n, g):
                b, hq = g % PAIR, g // PAIR
                wait(act, pv_mm, n + 1)
                nc.scalar.activation(OT[:, b, 2 * hq:2 * hq + 2, :],
                                     banks[O_BANK][:, 0:256].rearrange("p (c l) -> p c l", c=2),
                                     ACT.Copy).then_inc(o_ok, 1)

            def behind(t, g):
                n = QUADS * t + g
                if g >= PV_LAG or exists(t - 1):
                    if g == PV_LAG:
                        wait(act, wo_mm, t)
                    o_out(n - PV_LAG, (g - PV_LAG) % QUADS)
                if g + Y_AHEAD < UNITS:
                    y_high(t, g + Y_AHEAD)
                elif exists(t + 1):
                    y_high(t + 1, g + Y_AHEAD - UNITS)
                if g in V1_STEPS:
                    b = V1_STEPS.index(g)
                    v_out(4 * t + 2 + b, t, b, 1)
                if g in V0_STEPS and exists(t + 1):
                    b = V0_STEPS.index(g)
                    v_out(4 * t + 4 + b, t + 1, b, 0)
                if g == XT_STEP and exists(t - 1):
                    xT_high(t - 1)

            def pair(t):
                for g in range(QUADS):
                    if g > 0:
                        behind(t, g - 1)
                    elif exists(t - 1):
                        behind(t - 1, QUADS - 1)
                    exps(QUADS * t + g, g)

            for u in range(Y_AHEAD):
                y_high(0, u)
            for b in range(PAIR):
                v_out(b, 0, b, 0)
            looped(act, NPAIR, pair)
            behind(NPAIR - 1, QUADS - 1)
            N_ALL = QUADS * NPAIR
            for n in range(N_ALL - PV_LAG, N_ALL):
                o_out(n, n % QUADS)
            xT_high(NPAIR - 1)

        @block.vector
        def _(vec):
            def reciprocals(n, g):
                wait(vec, exp_ok, n + 1)
                nc.vector.reciprocal(inv[:, g % 2], total[:, g % 2]).then_inc(inv_ok, 1)

            def y_low(t, u):
                n = UNITS * t + u
                wait(vec, y_hi, n + 1)
                for b in range(PAIR):
                    last = nc.vector.tensor_tensor(
                        y.lo[:, b, 2 * u:2 * u + 2, :],
                        banks[Y_BANK[u % 2]][:].rearrange("p (h b l) -> p b h l", h=2, b=PAIR)[:, b],
                        f32(y.hi[:, b, 2 * u:2 * u + 2, :]), ALU.subtract)
                last.then_inc(y_lo, 1)

            def maxima(n, g):
                wait(vec, s_mm, n + 1)
                nc.vector.tensor_reduce(negmax[:, g % 2], banks[S_BANK[g % 2]][:].rearrange("p (h l) -> p h l", h=HQ),
                                        AX_X, ALU.max, negate=True).then_inc(max_ok, 1)

            def pt_out(n, g):
                wait(vec, t_mm, n + 1)
                wait(vec, pv_mm, n - 1)
                nc.vector.tensor_copy(PT[:, g % 2], banks[PT_BANK][:]).then_inc(pt_ok, 1)

            def residual(t):
                wait(vec, wo_mm, t + 1)
                nc.vector.tensor_tensor(R[:], banks[W_BANK][:, 0:PCOLS].rearrange("p (b d) -> p b d", b=PAIR),
                                        k.xres[:, bass.ds(t * PAIR, PAIR), :], ALU.add).then_inc(r_ok, 1)
                wait(vec, r_ok, t + 1)
                for b in range(PAIR):
                    last = nc.vector.bn_stats(stats[:, b], R[:, b])
                last.then_inc(st_ok, 1)
                wait_apart(vec, st_ok, t + 1, spare)
                for b in range(PAIR):
                    last = nc.vector.bn_aggr(mv[:, b], stats[:, b])
                last.then_inc(mv_ok, 1)

            def normalise(t):
                wait(vec, rstd_ok, t + 1)
                for b in range(PAIR):
                    last = nc.vector.tensor_scalar(N[:, b], R[:, b], mv[:, b, 0:1], rstd[:, b:b + 1],
                                                   ALU.subtract, ALU.mult)
                last.then_inc(n_ok, 1)

            def xT_low(t):
                wait(vec, xT_hi, t + 1)
                nc.vector.tensor_tensor(outT.lo[:, cols(t)], banks[W_BANK][:, 0:PCOLS], f32(outT.hi[:, cols(t)]),
                                        ALU.subtract).then_inc(xT_lo, 1)

            def pair(t):
                for g in range(QUADS):
                    n = QUADS * t + g
                    if exists(t - (g < 1)):
                        reciprocals(n - 1, (g - 1) % QUADS)
                    maxima(n, g)
                    u = g - 1 + Y_AHEAD
                    if u < UNITS and (g > 0 or exists(t - 1)):
                        y_low(t, u)
                    elif u >= UNITS and exists(t + 1):
                        y_low(t + 1, u - UNITS)
                    if exists(t - (g < T_LAG)):
                        pt_out(n - T_LAG, (g - T_LAG) % QUADS)
                    if g == WO_STEP and exists(t - 1):
                        residual(t - 1)
                    if g == WO_STEP + 1 and exists(t - 1):
                        normalise(t - 1)
                    if g == XT_STEP and exists(t - 1):
                        xT_low(t - 1)

            for u in range(Y_AHEAD):
                y_low(0, u)
            looped(vec, NPAIR, pair)
            N_ALL = QUADS * NPAIR
            reciprocals(N_ALL - 1, (N_ALL - 1) % QUADS)
            for n in range(N_ALL - T_LAG, N_ALL):
                pt_out(n, n % QUADS)
            residual(NPAIR - 1)
            normalise(NPAIR - 1)
            xT_low(NPAIR - 1)

        @block.gpsimd
        def _(pool):
            def copy(dst, src):
                return nc.gpsimd.tensor_tensor(dst, f32(src), k.one[:].to_broadcast([128, src.shape[1]]), ALU.mult)

            def queries(t, b):
                wait_apart(pool, s_mm, QUADS * (t - 1) + QUADS - PAIR + b + 1, spare)
                copy(xq.hi[:, b], qT.hi[:, cols(t, 128, b * 128)])
                copy(xq.lo[:, b], qT.lo[:, cols(t, 128, b * 128)]).then_inc(xq_ok, 1)

            def keys(t):
                wait_apart(pool, v_mm, 4 * t, spare)
                copy(xv.hi[:].rearrange("p b l -> p (b l)"), kvT.hi[:, cols(t)])
                copy(xv.lo[:].rearrange("p b l -> p (b l)"), kvT.lo[:, cols(t)]).then_inc(xv_ok, 1)

            def normalise(n, g):
                wait(pool, inv_ok, n + 1)
                tile = P[:, g % P_RING]
                nc.gpsimd.tensor_tensor(tile, tile, inv[:, g % 2].unsqueeze(2).to_broadcast([128, HQ, 128]),
                                        ALU.mult).then_inc(norm_ok, 1)

            def inverse_deviation(t):
                wait(pool, mv_ok, t + 1)
                nc.gpsimd.tensor_tensor(rstd[:], mv[:, :, 1], k.eps[:, 0:PAIR], ALU.add).then_inc(eps_ok, 1)
                wait(pool, eps_ok, t + 1)
                nc.gpsimd.tensor_tensor(rstd[:], rstd[:], k.half_neg[:, 0:PAIR], ALU.pow).then_inc(rstd_ok, 1)

            def affine(t):
                wait(pool, n_ok, t + 1)

                def row(r):
                    return r[:].unsqueeze(1).to_broadcast([128, PAIR, 128])

                nc.gpsimd.tensor_tensor(N[:], N[:], row(g_row), ALU.mult).then_inc(gain_ok, 1)
                wait(pool, gain_ok, t + 1)
                wait(pool, xT_mm, t)
                nc.gpsimd.tensor_tensor(X[:], N[:], row(b_row), ALU.add).then_inc(x_ok, 1)
                wait_apart(pool, x_ok, t + 1, spare)
                nc.gpsimd.tensor_tensor(k.xres[:, bass.ds(t * PAIR, PAIR), :], X[:], row(next_bias),
                                        ALU.add).then_inc(res_ok, 1)

            def pair(t):
                for g in range(QUADS):
                    n = QUADS * t + g
                    if g == QUADS - 1 and exists(t + 1):
                        queries(t + 1, 0)
                    if g == 0 and exists(t - 1):
                        queries(t, 1)
                    if g == XV_STEP and exists(t + 1):
                        keys(t + 1)
                    if exists(t - (g < 1)):
                        normalise(n - 1, (g - 1) % QUADS)
                    if g == WO_STEP and exists(t - 1):
                        inverse_deviation(t - 1)
                    if g == WO_STEP + 1 and exists(t - 1):
                        affine(t - 1)

            queries(0, 0)
            queries(0, 1)
            keys(0)
            looped(pool, NPAIR, pair)
            normalise(QUADS * NPAIR - 1, QUADS - 1)
            inverse_deviation(NPAIR - 1)
            affine(NPAIR - 1)


def feed_forward(k):
    nc, io = k.nc, k.io
    with ExitStack() as ctx:
        sb = k.sb
        fc1_raw = sb(ctx, "fc1_raw", [128, FF])
        fc1 = k.split(ctx, "fc1", [128, FF])
        fc1_b = sb(ctx, "fc1_b", [128, FF // 128])
        fc2 = sb(ctx, "fc2", [128, FF // 128, 128])
        w1_raw = sb(ctx, "w1_raw", [128, 128])
        w1 = k.split(ctx, "w1s", [128, 128])
        b1 = sb(ctx, "b1", [128, 1])
        w2 = sb(ctx, "w2", [128, 128])
        w1e = sb(ctx, "w1e", [128, NEXP, 128])
        w2e = sb(ctx, "w2e", [128, NEXP, 128])
        b1e = sb(ctx, "b1e", [128, NEXP])
        rows3 = {n: sb(ctx, "row_" + n, [128, 128]) for n in ("ln3_g", "ln3_b")}
        gain = sb(ctx, "gain", [128, 128])
        shift = sb(ctx, "shift", [128, 128])
        bias2 = sb(ctx, "bias2", [128, 128])
        hT = sb(ctx, "hT", [128, 2, FF // 128, GRP, 128])
        R = sb(ctx, "ffR", [128, NSEQ, 128])
        N3 = sb(ctx, "N3", [128, NSEQ, 128])
        X4 = sb(ctx, "X4", [128, NSEQ, 128])
        N5 = sb(ctx, "N5", [128, NSEQ, 128])
        zT = k.split(ctx, "zT", [128, 2, GRP, 128])
        zE = sb(ctx, "zE", [128, NSEQ, NEXP])
        gT = sb(ctx, "gT", [128, 2, GRP, 128])
        res = sb(ctx, "res", [128, NSEQ, 128])
        hE = sb(ctx, "hE", [128, NEXP, NSEQ])
        xE = sb(ctx, "xE", [NSEQ, NEXP, 128])
        rE = sb(ctx, "rE", [NSEQ, NEXP, 128])
        stats = sb(ctx, "ffstats", [128, 4, NSEQ, 6])
        mv = sb(ctx, "ffmv", [128, 4, NSEQ, 2])
        rstd = sb(ctx, "ffrstd", [128, 4, NSEQ])
        stats_e = sb(ctx, "stats_e", [NSEQ, NEXP, 6])
        mv_e = sb(ctx, "mv_e", [NSEQ, NEXP, 2])
        rstd_e = sb(ctx, "rstd_e", [NSEQ, NEXP])
        banks = k.banks(ctx, "ff")
        FC2_BANK, ZT_BANK, W1_BANK, W2_BANK = 4, 5, 6, 7
        (ld, ld_w, ld_e, hi_ok, wlo, fc1_mm, h_ok, fc2_mm, r_ok, gain3, shift3, x4a, gain5, z_ok, x4b, zT_mm, z_hi,
         z_lo, ze_ok, w1_mm, g_ok, w2_mm, res_ok, parked, xe_in, e1_mm, e1_b, e1_g, e2_mm, re_ok, st_e, mv_e_ok,
         eps_e, rstd_e_ok, ne_ok, stored, zeroed) = k.sems(ctx, "ff", """ld ld_w ld_e hi_ok wlo fc1_mm h_ok fc2_mm
            r_ok gain3 shift3 x4a gain5 z_ok x4b zT_mm z_hi z_lo ze_ok w1_mm g_ok w2_mm res_ok parked xe_in e1_mm
            e1_b e1_g e2_mm re_ok st_e mv_e_ok eps_e rstd_e_ok ne_ok stored zeroed""")
        st, mvs, eps_ok, rstd_ok, nrm = (k.sems(ctx, "ff", " ".join(f"{n}{i}" for i in range(4)))
                                         for n in ("stats", "moments", "plus_eps", "rstd", "normal"))
        block = ctx.enter_context(nc.Block())
        NLD = 12
        EQ = 4

        def quarter(bank):
            return banks[bank][:].rearrange("p (b d) -> p b d", b=GRP)

        def seqs(g):
            return slice(g * GRP, (g + 1) * GRP)

        def ticks(stages):
            for tick in range(NGRP + 3):
                for stage, behind in stages:
                    if 0 <= tick - behind < NGRP:
                        stage(tick - behind)

        @block.sync
        def _(sp):
            sp.dma_start(fc1_raw[:], io["fc1_w"]).then_inc(ld_w, 16)
            sp.dma_start(w1_raw[:], io["W1_s"]).then_inc(ld_w, 16)
            sp.dma_start(fc1_b[:], io["fc1_bT"]).then_inc(ld, 16)
            sp.dma_start(fc2[:], io["fc2_w"].rearrange("(c p) n -> p c n", p=128)).then_inc(ld, 16)
            for n, tile in rows3.items():
                row_broadcast(nc, sp, tile[:], io[n]).then_inc(ld, 16)
            sp.dma_start(b1[:], io["b1_s"].rearrange("(p o) -> p o", o=1)).then_inc(ld, 16)
            sp.dma_start(w2[:], io["W2_s"]).then_inc(ld, 16)
            for tile, name in ((gain, "g"), (shift, "b"), (bias2, "b2")):
                sp.dma_start(tile[0:NEXP, :], io[name + "_e"]).then_inc(ld, 16)
                row_broadcast(nc, sp, tile[NEXP:128, :], io[name + "_s"]).then_inc(ld, 16)
            sp.dma_start(w1e[:], io["W1_e"].rearrange("n d h -> d n h")).then_inc(ld_e, 16)
            sp.dma_start(w2e[:], io["W2_e"].rearrange("n d h -> d n h")).then_inc(ld_e, 16)
            sp.dma_start(b1e[:], io["b1_eT"]).then_inc(ld_e, 16)
            for g in range(NGRP):
                sp.wait_ge(x4b, g + 1)
                sp.dma_start(io["scratch"].rearrange("b n d -> n b d")[:, seqs(g), :],
                             X4[0:NEXP, seqs(g), :]).then_inc(parked, 16)
            sp.wait_ge(parked, 16 * NGRP)
            sp.dma_start(xE[:], io["scratch"]).then_inc(xe_in, 16)
            for g in range(NGRP):
                sp.wait_ge(nrm[3], g + 1)
                sp.dma_start(io["out"].rearrange("b p d -> p b d")[NEXP:, seqs(g), :],
                             res[NEXP:, seqs(g), :]).then_inc(stored, 16)
            for q in range(NEXP // EQ):
                sp.wait_ge(ne_ok, q + 1)
                sp.dma_start(io["out"][:, q * EQ:(q + 1) * EQ, :], rE[:, q * EQ:(q + 1) * EQ, :]).then_inc(stored, 16)
            sp.wait_ge(stored, 16 * (NGRP + NEXP // EQ))

        @block.tensor
        def _(pe):
            pe.wait_ge(wlo, 2)
            pe.wait_ge(ld, 16 * NLD)

            def hidden(g):
                for c in range(FF // 128):
                    wait(pe, h_ok, 4 * g + c - 3)
                    mm_split(nc, banks[c][:], fc1, np.s_[:, c * 128:(c + 1) * 128], k.x1T,
                             np.s_[:, g * GCOLS:(g + 1) * GCOLS]).then_inc(fc1_mm, 1)

            def fc2_sum(g):
                pe.wait_ge(h_ok, 4 * (g + 1))
                wait(pe, r_ok, g)
                for b in range(GRP):
                    for c in range(FF // 128):
                        last = nc.tensor.matmul(banks[FC2_BANK][:, b * 128:(b + 1) * 128], hT[:, g % 2, c, b, :],
                                                fc2[:, c, :], start=(c == 0), stop=(c == FF // 128 - 1))
                last.then_inc(fc2_mm, 1)

            def z_transposes(g):
                pe.wait_ge(z_ok, g + 1)
                wait(pe, ze_ok, g)
                for b in range(GRP):
                    last = nc.tensor.transpose(banks[ZT_BANK][:, b * 128:(b + 1) * 128], N5[:, g * GRP + b, :],
                                               k.ident[:])
                last.then_inc(zT_mm, 1)

            def shared_w1(g):
                pe.wait_ge(z_lo, g + 1)
                wait(pe, g_ok, g)
                mm_split(nc, banks[W1_BANK][:], w1, np.s_[:, :], zT, np.s_[:, g % 2]).then_inc(w1_mm, 1)

            def shared_w2(g):
                pe.wait_ge(g_ok, g + 1)
                wait(pe, res_ok, g)
                for b in range(GRP):
                    last = nc.tensor.matmul(banks[W2_BANK][:, b * 128:(b + 1) * 128], gT[:, g % 2, b, :], w2[:],
                                            start=True, stop=True)
                last.then_inc(w2_mm, 1)

            ticks([(hidden, 0), (z_transposes, 2), (fc2_sum, 0), (shared_w1, 2), (shared_w2, 2)])
            pe.wait_ge(ld_e, 48)
            pe.wait_ge(ze_ok, NGRP)
            for q in range(NEXP // EQ):
                for e in range(q * EQ, (q + 1) * EQ):
                    last = nc.tensor.matmul(banks[q][:, (e % EQ) * NSEQ:(e % EQ + 1) * NSEQ], w1e[:, e, :],
                                            zE[:, :, e], start=True, stop=True)
                last.then_inc(e1_mm, 1)
            for q in range(NEXP // EQ):
                pe.wait_ge(e1_g, q + 1)
                for e in range(q * EQ, (q + 1) * EQ):
                    last = nc.tensor.matmul(banks[4 + q][0:NSEQ, (e % EQ) * 128:(e % EQ + 1) * 128], hE[:, e, :],
                                            w2e[:, e, :], start=True, stop=True)
                last.then_inc(e2_mm, 1)

        @block.scalar
        def _(act):
            act.wait_ge(ld_w, 32)
            nc.scalar.activation(fc1.hi[:], fc1_raw[:], ACT.Copy).then_inc(hi_ok, 1)
            nc.scalar.activation(w1.hi[:], w1_raw[:], ACT.Copy).then_inc(hi_ok, 1)
            act.wait_ge(ld, 16 * NLD)
            act.wait_ge(zeroed, 1)

            def gelu_hidden(g):
                for c in range(FF // 128):
                    act.wait_ge(fc1_mm, 4 * g + c + 1)
                    if c == 0:
                        wait(act, fc2_mm, g - 1)
                    nc.scalar.activation(hT[:, g % 2, c], quarter(c), ACT.Gelu,
                                         bias=fc1_b[:, c:c + 1]).then_inc(h_ok, 1)

            def z_high(g):
                act.wait_ge(zT_mm, g + 1)
                wait(act, w1_mm, g - 1)
                nc.scalar.activation(zT.hi[:, g % 2], quarter(ZT_BANK), ACT.Copy).then_inc(z_hi, 1)

            def gelu_shared(g):
                act.wait_ge(w1_mm, g + 1)
                wait(act, w2_mm, g - 1)
                nc.scalar.activation(gT[:, g % 2, :, NEXP:], quarter(W1_BANK)[:, :, NEXP:], ACT.Gelu,
                                     bias=b1[:, 0:1]).then_inc(g_ok, 1)

            ticks([(gelu_hidden, 0), (z_high, 2), (gelu_shared, 2)])
            for q in range(NEXP // EQ):
                act.wait_ge(e1_b, q + 1)
                part = hE[:, q * EQ:(q + 1) * EQ, :]
                nc.scalar.activation(part, part, ACT.Gelu).then_inc(e1_g, 1)

        @block.vector
        def _(vec):
            vec.wait_ge(hi_ok, 2)
            nc.vector.tensor_tensor(fc1.lo[:], fc1_raw[:], f32(fc1.hi[:]), ALU.subtract).then_inc(wlo, 1)
            nc.vector.tensor_tensor(w1.lo[:], w1_raw[:], f32(w1.hi[:]), ALU.subtract).then_inc(wlo, 1)
            vec.wait_ge(ld, 16 * NLD)

            def statistics(g, i, src):
                for b in range(g * GRP, (g + 1) * GRP):
                    last = nc.vector.bn_stats(stats[:, i, b], src[:, b])
                last.then_inc(st[i], 1)
                vec.wait_ge(st[i], g + 1)
                for b in range(g * GRP, (g + 1) * GRP):
                    last = nc.vector.bn_aggr(mv[:, i, b], stats[:, i, b])
                last.then_inc(mvs[i], 1)

            def normalise(g, i, dst, src):
                vec.wait_ge(rstd_ok[i], g + 1)
                for b in range(g * GRP, (g + 1) * GRP):
                    last = nc.vector.tensor_scalar(dst[:, b], src[:, b], mv[:, i, b, 0:1], rstd[:, i, b:b + 1],
                                                   ALU.subtract, ALU.mult)
                last.then_inc(nrm[i], 1)

            def residual3(g):
                vec.wait_ge(fc2_mm, g + 1)
                nc.vector.tensor_tensor(R[:, seqs(g)], quarter(FC2_BANK), k.xres[:, seqs(g), :],
                                        ALU.add).then_inc(r_ok, 1)
                vec.wait_ge(r_ok, g + 1)
                statistics(g, 0, R)

            def normal3(g):
                normalise(g, 0, N3, R)

            def outer_statistics(g):
                vec.wait_ge(x4a, g + 1)
                statistics(g, 1, N3)

            def outer_normal(g):
                normalise(g, 1, X4, N3)
                vec.wait_ge(nrm[1], g + 1)
                statistics(g, 2, X4)

            def z_normal(g):
                normalise(g, 2, N5, X4)

            def z_low(g):
                vec.wait_ge(z_hi, g + 1)
                wait(vec, w1_mm, g - 1)
                nc.vector.tensor_tensor(zT.lo[:, g % 2], quarter(ZT_BANK), f32(zT.hi[:, g % 2]),
                                        ALU.subtract).then_inc(z_lo, 1)
                nc.vector.tensor_copy(zE[:, seqs(g), :], quarter(ZT_BANK)[:, :, 0:NEXP]).then_inc(ze_ok, 1)

            def output_statistics(g):
                vec.wait_ge(w2_mm, g + 1)
                vec.wait_ge(x4b, g + 1)
                nc.vector.tensor_tensor(res[:, seqs(g), :], quarter(W2_BANK), X4[:, seqs(g)],
                                        ALU.add).then_inc(res_ok, 1)
                vec.wait_ge(res_ok, g + 1)
                statistics(g, 3, res)

            def output(g):
                normalise(g, 3, res, res)

            ticks([(normal3, 1), (z_normal, 2), (z_low, 2), (outer_statistics, 1), (residual3, 0),
                   (outer_normal, 1), (output_statistics, 2), (output, 3)])
            vec.wait_ge(ld_e, 48)
            vec.wait_ge(xe_in, 16)
            for q in range(NEXP // EQ):
                vec.wait_ge(e1_mm, q + 1)
                es = slice(q * EQ, (q + 1) * EQ)
                nc.vector.tensor_tensor(hE[:, es, :], banks[q][:, 0:EQ * NSEQ].rearrange("p (e b) -> p e b", e=EQ),
                                        b1e[:, es].unsqueeze(2).to_broadcast([128, EQ, NSEQ]),
                                        ALU.add).then_inc(e1_b, 1)

            def expert_sums(q):
                es = slice(q * EQ, (q + 1) * EQ)
                vec.wait_ge(e2_mm, q + 1)
                nc.vector.tensor_tensor(rE[:, es, :], banks[4 + q][0:NSEQ, :].rearrange("p (e d) -> p e d", e=EQ),
                                        xE[:, es, :], ALU.add).then_inc(re_ok, 1)
                vec.wait_ge(re_ok, q + 1)
                for e in range(q * EQ, (q + 1) * EQ):
                    last = nc.vector.bn_stats(stats_e[:, e], rE[:, e])
                last.then_inc(st_e, 1)
                vec.wait_ge(st_e, q + 1)
                for e in range(q * EQ, (q + 1) * EQ):
                    last = nc.vector.bn_aggr(mv_e[:, e], stats_e[:, e])
                last.then_inc(mv_e_ok, 1)

            def expert_output(q):
                vec.wait_ge(rstd_e_ok, q + 1)
                for e in range(q * EQ, (q + 1) * EQ):
                    last = nc.vector.tensor_scalar(rE[:, e], rE[:, e], mv_e[:, e, 0:1], rstd_e[:, e:e + 1],
                                                   ALU.subtract, ALU.mult)
                last.then_inc(ne_ok, 1)

            for q in range(NEXP // EQ):
                expert_sums(q)
                if q >= 1:
                    expert_output(q - 1)
            expert_output(NEXP // EQ - 1)

        @block.gpsimd
        def _(pool):
            nc.gpsimd.memset(gT[:], 0.0).then_inc(zeroed, 1)
            pool.wait_ge(ld, 16 * NLD)

            def row(r):
                return r[:].unsqueeze(1).to_broadcast([128, GRP, 128])

            def inverse_deviation(g, i):
                pool.wait_ge(mvs[i], g + 1)
                nc.gpsimd.tensor_tensor(rstd[:, i, seqs(g)], mv[:, i, seqs(g), 1], k.eps[:, 0:GRP],
                                        ALU.add).then_inc(eps_ok[i], 1)
                pool.wait_ge(eps_ok[i], g + 1)
                nc.gpsimd.tensor_tensor(rstd[:, i, seqs(g)], rstd[:, i, seqs(g)], k.half_neg[:, 0:GRP],
                                        ALU.pow).then_inc(rstd_ok[i], 1)

            def affine3(g):
                pool.wait_ge(nrm[0], g + 1)
                part = N3[:, seqs(g)]
                nc.gpsimd.tensor_tensor(part, part, row(rows3["ln3_g"]), ALU.mult).then_inc(gain3, 1)
                pool.wait_ge(gain3, g + 1)
                nc.gpsimd.tensor_tensor(part, part, row(rows3["ln3_b"]), ALU.add).then_inc(shift3, 1)
                pool.wait_ge(shift3, g + 1)
                nc.gpsimd.tensor_tensor(part, part, k.x1[:, seqs(g), :], ALU.add).then_inc(x4a, 1)

            def affine5(g):
                pool.wait_ge(nrm[2], g + 1)
                part = N5[:, seqs(g)]
                nc.gpsimd.tensor_tensor(part, part, row(gain), ALU.mult).then_inc(gain5, 1)
                pool.wait_ge(gain5, g + 1)
                nc.gpsimd.tensor_tensor(part, part, row(shift), ALU.add).then_inc(z_ok, 1)
                nc.gpsimd.tensor_tensor(X4[:, seqs(g)], X4[:, seqs(g)], row(bias2), ALU.add).then_inc(x4b, 1)

            ticks([(lambda g: inverse_deviation(g, 2), 2), (lambda g: inverse_deviation(g, 0), 1), (affine5, 2),
                   (affine3, 1), (lambda g: inverse_deviation(g, 1), 1), (lambda g: inverse_deviation(g, 3), 2)])
            for q in range(NEXP // EQ):
                es = slice(q * EQ, (q + 1) * EQ)
                pool.wait_ge(mv_e_ok, q + 1)
                nc.gpsimd.tensor_tensor(rstd_e[:, es], mv_e[:, es, 1], k.eps[0:NSEQ, 0:EQ], ALU.add).then_inc(eps_e, 1)
                pool.wait_ge(eps_e, q + 1)
                nc.gpsimd.tensor_tensor(rstd_e[:, es], rstd_e[:, es], k.half_neg[0:NSEQ, 0:EQ],
                                        ALU.pow).then_inc(rstd_e_ok, 1)


def build(nc, io):
    k = Kernel(nc, io)
    with ExitStack() as ctx:
        allocate(k, ctx)
        with ExitStack() as inner:
            allocate_attention(k, inner)
            setup_and_mixer(k)
            attention(k, "sa", k.x1T, k.x1T, k.m_sa, k.wv_sa, k.wo_sa, k.rows["ln1_g"], k.rows["ln1_b"],
                      k.rows["ca_bo"], k.x2T)
            attention(k, "ca", k.x2T, k.ctxT, k.m_ca, k.wv_ca, k.wo_ca, k.rows["ln2_g"], k.rows["ln2_b"],
                      k.rows["fc2_b"], k.x1T)
        feed_forward(k)


def layouts(a):
    tall = {"x": a["x"], "xT": a["x"].transpose(2, 0, 1).reshape(D, T),
            "ctxT": a["ctx_1024"].transpose(2, 0, 1).reshape(D, T),
            "mask": a["mask_BxS2_bk0"],
            "short_bT": a["L0_attn_short_b"].reshape(3, D).T, "b_inT": a["L0_attn_b_in"].reshape(3, D).T,
            "fc1_bT": a["L0_xattn_fc1_b"].reshape(FF // D, D).T, "b1_eT": a["L0_ffn_b1_e"].T}
    for n in "W_in short_w inner_w inner_b W_out b_out".split():
        tall[n] = a["L0_attn_" + n]
    for s in ("sa", "ca"):
        for n in ("wq", "wk"):
            tall[f"{s}_{n}T"] = a[f"L0_xattn_{s}_{n}"].T
        for n in ("wv", "wo", "bo"):
            tall[f"{s}_{n}"] = a[f"L0_xattn_{s}_{n}"]
    for n in "ln1_g ln1_b ln2_g ln2_b ln3_g ln3_b fc1_w fc2_w fc2_b".split():
        tall[n] = a["L0_xattn_" + n]
    for n in "g_e b_e W1_e W2_e b2_e g_s b_s W1_s b1_s W2_s b2_s".split():
        tall[n] = a["L0_ffn_" + n]
    return {n: np.ascontiguousarray(v) for n, v in tall.items()}


def kernel(**inputs):
    from concourse import bacc
    from concourse.bass_utils import run_bass_kernel_spmd

    nc = bacc.Bacc("TRN2", target_bir_lowering=False, num_devices=1)
    arrays = layouts({n: np.asarray(v) for n, v in inputs.items()})
    io = {n: nc.dram_tensor("in_" + n, v.shape, mybir.dt.from_np(v.dtype), kind="ExternalInput").ap()
          for n, v in arrays.items()}
    io["scratch"] = nc.dram_tensor("experts_out", (NSEQ, NEXP, D), F32, kind="Internal").ap()
    io["out"] = nc.dram_tensor("out", (NSEQ, L, D), F32, kind="ExternalOutput").ap()
    build(nc, io)
    result = run_bass_kernel_spmd(nc, [{"in_" + n: v for n, v in arrays.items()}], core_ids=[0])
    return result.results[0]["out"]
```

```python
from contextlib import ExitStack
from itertools import count

import numpy as np

import concourse.bass as bass
from concourse import mybir

F32 = mybir.dt.float32
F32R = mybir.dt.float32r
BF16 = mybir.dt.bfloat16
U8 = mybir.dt.uint8
ALU = mybir.AluOpType
ACT = mybir.ActivationFunctionType
AX_X = mybir.AxisListType.X

NSEQ, L, D = 16, 128, 128
H, DH = 16, 64
INNER = H * DH
FF = 512
NEXP = 16
EPS = 1e-5
SCALE = DH ** -0.5
MASKED = -(2.0 ** 100)
T = NSEQ * L
PAIR = 2
NPAIR = NSEQ // PAIR
PCOLS = PAIR * L
HQ = 4
QUADS = PAIR * H // HQ
UNITS = H // 2
GRP = 4
NGRP = NSEQ // GRP
GCOLS = GRP * L
Y_AHEAD, T_LAG, PV_LAG = 4, 2, 3
P_RING = 4
EQ, QUADRANT = 4, 32
FC2_BANK = 4
HIDDEN_AHEAD = 2
FF_LOADS = 14


def wait(engine, sem, value):
    if isinstance(value, int) and value <= 0:
        return
    engine.wait_ge(sem, value)


def wait_apart(engine, sem, value, spare):
    wait(engine, sem, value)
    engine.sem_inc(spare, 1)


def f32(ap):
    return ap.bitcast(F32)


class Split:

    def __init__(self, hi, lo):
        self.hi, self.lo = hi, lo


def mm_split(nc, out, w, wsel, x, xsel, first=True):
    nc.tensor.matmul(out, w.hi[wsel], x.hi[xsel], start=first, stop=False)
    nc.tensor.matmul(out, w.hi[wsel], x.lo[xsel], start=False, stop=False)
    return nc.tensor.matmul(out, w.lo[wsel], x.hi[xsel], start=False, stop=True)


class Kernel:
    def __init__(self, nc, io):
        self.nc, self.io = nc, io

    def sb(self, ctx, name, shape, dt=F32):
        return ctx.enter_context(self.nc.sbuf_tensor(name, shape, dt))

    def split(self, ctx, name, shape):
        return Split(self.sb(ctx, name + "_hi", shape, F32R), self.sb(ctx, name + "_lo", shape, F32R))

    def banks(self, ctx, tag):
        return [ctx.enter_context(self.nc.psum_tensor(f"{tag}_bank{i}", [128, 512], F32)) for i in range(8)]

    def sems(self, ctx, tag, names):
        return [ctx.enter_context(self.nc.semaphore(f"{tag}_{n}")) for n in names.split()]


def allocate(k, ctx):
    sb, split = k.sb, k.split
    k.ident = sb(ctx, "ident", [128, 128])
    k.half_neg = sb(ctx, "half_neg", [128, NSEQ])
    k.one = sb(ctx, "one", [128, 1])
    k.rows = {n: sb(ctx, "row_" + n, [128, 128]) for n in
              "sa_bo ca_bo ln1_g ln1_b ln2_g ln2_b fc2_b".split()}
    k.x1 = sb(ctx, "x1", [128, NSEQ, 128])
    k.xres = sb(ctx, "xres", [128, NSEQ, 128])
    k.x1T = split(ctx, "x1T", [128, T])


def allocate_attention(k, ctx):
    sb, split = k.sb, k.split
    k.ones_row0 = sb(ctx, "ones_row0", [128, 128], BF16)
    k.maskb = sb(ctx, "maskb", [128, T], BF16)
    k.m_sa = split(ctx, "m_sa", [128, H, 128])
    k.m_ca = split(ctx, "m_ca", [128, H, 128])
    k.wv_sa = split(ctx, "wv_sa", [128, INNER])
    k.wo_sa = sb(ctx, "wo_sa", [128, H // 2, 128])
    k.wv_ca = split(ctx, "wv_ca", [128, INNER])
    k.wo_ca = sb(ctx, "wo_ca", [128, H // 2, 128])
    k.x2T = split(ctx, "x2T", [128, NSEQ * (L + 2)])
    k.ctxT = split(ctx, "ctxT", [128, T])


def allocate_feed_forward(k, ctx):
    sb = k.sb
    k.fc1 = k.split(ctx, "fc1", [128, FF])
    k.fc1_b = sb(ctx, "fc1_b", [128, FF // 128])
    k.fc2 = sb(ctx, "fc2", [128, FF // 128, 128])
    k.ln3_g = sb(ctx, "ln3_g", [128, 128])
    k.gainT = sb(ctx, "gainT", [128, NEXP + 1])
    k.shiftT = sb(ctx, "shiftT", [128, NEXP + 1])
    k.b1_raw = sb(ctx, "b1_raw", [128, NEXP + 1])
    k.w1 = k.split(ctx, "w1s", [128, 128])
    k.w2 = sb(ctx, "w2", [128, 128])
    k.bias2 = sb(ctx, "bias2", [128, 128])
    k.ff_ld, k.ff_hi, k.ff_lo = k.sems(ctx, "ffw", "ld hi lo")


def load_feed_forward(k, sp, fc1_raw, w1_raw):
    nc, io = k.nc, k.io
    sp.dma_start(fc1_raw[:], io["fc1_w"]).then_inc(k.ff_ld, 16)
    sp.dma_start(w1_raw[:], io["W1_s"]).then_inc(k.ff_ld, 16)
    sp.dma_start(k.fc1_b[:], io["fc1_bT"]).then_inc(k.ff_ld, 16)
    sp.dma_start(k.fc2[:], io["fc2_w"].rearrange("(c p) n -> p c n", p=128)).then_inc(k.ff_ld, 16)
    row_broadcast(nc, sp, k.ln3_g[:], io["ln3_g"]).then_inc(k.ff_ld, 16)
    for tile, name in ((k.gainT, "g"), (k.shiftT, "b"), (k.b1_raw, "b1")):
        sp.dma_start(tile[:, 0:NEXP], io[name + "_eT"]).then_inc(k.ff_ld, 16)
        sp.dma_start(tile[:, NEXP:], io[name + "_s"].rearrange("(p o) -> p o", o=1)).then_inc(k.ff_ld, 16)
    sp.dma_start(k.w2[:], io["W2_s"]).then_inc(k.ff_ld, 16)
    sp.dma_start(k.bias2[0:NEXP, :], io["b2_e"]).then_inc(k.ff_ld, 16)
    row_broadcast(nc, sp, k.bias2[NEXP:128, :], io["b2_s"]).then_inc(k.ff_ld, 16)
    sp.wait_ge(k.ff_ld, 16 * FF_LOADS)


def row_broadcast(nc, engine, dst, src_row):
    return engine.dma_start(dst, src_row.partition_broadcast(dst.shape[0]))


def setup_and_mixer(k):
    nc, io = k.nc, k.io
    with ExitStack() as ctx:
        xT = Split(*(part[:].rearrange("p (b l) -> p b l", b=NSEQ) for part in (k.x2T.hi, k.x2T.lo)))
        zeros = k.sb(ctx, "zeros", [128, NSEQ, 2])
        xT_raw = k.x1
        c_raw = k.sb(ctx, "c_raw", [128, T])
        wv_raw = k.sb(ctx, "wv_raw", [128, 2, INNER])
        w3_raw = k.sb(ctx, "w3_raw", [128, 3, 3 * D])
        w_in = k.sb(ctx, "w_in", [128, 3 * D])
        tap_rows = k.sb(ctx, "tap_rows", [128, 3, 3 * D])
        w3 = k.split(ctx, "w3", [128, 3, 3 * D])
        w_out = k.sb(ctx, "w_out", [128, D])
        qkT = k.sb(ctx, "qkT", [128, 2, H // 2, 128])
        mask_raw = k.sb(ctx, "mask_raw", [1, T], U8)
        taps = k.sb(ctx, "taps", [128, 3, 3])
        short_b = k.sb(ctx, "short_b", [128, 3])
        b_in = k.sb(ctx, "b_in", [128, 3])
        bias = k.sb(ctx, "conv_bias", [128, 3])
        early = k.sb(ctx, "early", [128, 3, 2])
        tap_b = k.sb(ctx, "tap_b", [128, 3, 3])
        inner = k.sb(ctx, "inner", [128, 4])
        inner_b = k.sb(ctx, "inner_b", [128, 1])
        b_out = k.sb(ctx, "b_out", [128, 128])
        ln3_b = k.sb(ctx, "ln3_b", [128, 128])
        C = k.sb(ctx, "C", [128, 2, 3, GRP, L])
        KV = k.sb(ctx, "KV", [128, GRP, L + 3])
        G = k.sb(ctx, "G", [128, GRP, L])
        yT = k.sb(ctx, "yT", [128, GRP, L])
        R = k.sb(ctx, "R", [128, GRP, 128])
        N1 = k.sb(ctx, "N1", [128, GRP, 128])
        stats = k.sb(ctx, "stats", [128, NSEQ, 6])
        mv = k.sb(ctx, "mv", [128, NSEQ, 2])
        rstd = k.sb(ctx, "rstd", [128, NSEQ])
        shift = k.sb(ctx, "mean_shift", [128, NSEQ])
        banks = k.banks(ctx, "mix")
        C_BANKS, OUT_BANK, XT_BANK, M_BANKS = (0, 1, 2), 3, 4, (5, 6)
        (ld_x0, ld_x, ld_win, ld_small, ld_tok, ld_qk, ld_wv, ld_rows, ld_keep, ld_ctx, ld_mask, ident0,
         ident_ok, zeros_ok,
         consts_ok, pads_ok, xhi, xlo, w3_ok, whi, wlo, raw_hi, kept_ok, mm_m, m_hi, m_lo, tapb_ok, early_ok,
         bias_ok, c_mm, c_ok, fix_ok, kv_ok, g_ok, y_ok, link, o_mm, r_ok, mv_ok, rstd_ok, shift_ok,
         n_ok, xT_mm, x1hi, x1lo, xb_ok, res_ok) = k.sems(ctx, "mix", """ld_x0 ld_x ld_win ld_small ld_tok ld_qk ld_wv
            ld_rows ld_keep ld_ctx ld_mask ident0 ident_ok zeros_ok
            consts_ok pads_ok xhi xlo w3_ok whi wlo raw_hi kept_ok mm_m m_hi m_lo tapb_ok early_ok bias_ok
            c_mm c_ok fix_ok kv_ok g_ok y_ok link o_mm r_ok mv_ok rstd_ok shift_ok n_ok xT_mm x1hi
            x1lo xb_ok res_ok""")
        ld_taps = k.sems(ctx, "mix", "ld_tap0 ld_tap1 ld_tap2")
        block = ctx.enter_context(nc.Block())
        ROWS = 1 + len(k.rows)
        MQ = H // HQ
        weights = ((k.m_sa, k.wv_sa), (k.m_ca, k.wv_ca))

        def bank(i):
            return banks[i][:].rearrange("p (b l) -> p b l", b=GRP)

        def heads(i):
            first = i % MQ // 2 * 2 * HQ
            return slice(first + i % 2, first + 2 * HQ, 2)

        def seqs(g):
            return slice(g * GRP, (g + 1) * GRP)

        def cols(g):
            return slice(g * GCOLS, (g + 1) * GCOLS)

        def ticks(stages):
            for tick in range(NGRP + 2):
                for stage, behind in stages:
                    if 0 <= tick - behind < NGRP:
                        stage(tick - behind)

        @block.sync
        def _(sp):
            sp.dma_start(w_in[:], io["W_in"]).then_inc(ld_win, 16)
            for c in range(3):
                part = np.s_[:, c * D:(c + 1) * D]
                row_broadcast(nc, sp, tap_rows[:, :, c * D:(c + 1) * D], io["short_wT"][part]).then_inc(ld_taps[c], 16)
                if c == 0:
                    sp.dma_start(xT_raw[:, seqs(0), :], io["xT"][:, seqs(0), :]).then_inc(ld_x0, 16)
            sp.dma_start(taps[:], io["short_w"].rearrange("(c p) j -> p c j", p=128)).then_inc(ld_small, 16)
            sp.dma_start(short_b[:], io["short_bT"]).then_inc(ld_small, 16)
            sp.dma_start(b_in[:], io["b_inT"]).then_inc(ld_small, 16)
            sp.dma_start(inner[:], io["inner_w"]).then_inc(ld_small, 16)
            sp.dma_start(inner_b[:], io["inner_b"].rearrange("(p o) -> p o", o=1)).then_inc(ld_small, 16)
            sp.dma_start(xT_raw[:, GRP:, :], io["xT"][:, GRP:, :]).then_inc(ld_x, 16)
            row_broadcast(nc, sp, b_out[:], io["b_out"]).then_inc(ld_tok, 16)
            sp.dma_start(w_out[:], io["W_out"]).then_inc(ld_tok, 16)
            sp.dma_start(k.xres[:], io["x"].rearrange("b p d -> p b d")).then_inc(ld_tok, 16)
            row_broadcast(nc, sp, ln3_b[:], io["ln3_b"]).then_inc(ld_rows, 16)
            for n, tile in k.rows.items():
                row_broadcast(nc, sp, tile[:], io[n]).then_inc(ld_rows, 16)
            sp.dma_start(wv_raw[:, 0], io["sa_wv"]).then_inc(ld_wv, 16)
            sp.dma_start(c_raw[:], io["ctxT"]).then_inc(ld_ctx, 16)
            sp.dma_start(wv_raw[:, 1], io["ca_wv"]).then_inc(ld_wv, 16)
            sp.wait_ge(mm_m, MQ)
            sp.dma_start(qkT[:, 0], io["ca_wqT"].rearrange("(c p) d -> p c d", p=128)).then_inc(ld_qk, 16)
            sp.dma_start(qkT[:, 1], io["ca_wkT"].rearrange("(c p) d -> p c d", p=128)).then_inc(ld_qk, 16)
            sp.dma_start(k.wo_sa[:], io["sa_wo"].rearrange("(c p) n -> p c n", p=128)).then_inc(ld_keep, 16)
            sp.dma_start(k.wo_ca[:], io["ca_wo"].rearrange("(c p) n -> p c n", p=128)).then_inc(ld_keep, 16)
            sp.wait_ge(ld_keep, 32)

        @block.scalar
        def _(act):
            act.dma_start(qkT[:, 0], io["sa_wqT"].rearrange("(c p) d -> p c d", p=128)).then_inc(ld_qk, 16)
            act.dma_start(qkT[:, 1], io["sa_wkT"].rearrange("(c p) d -> p c d", p=128)).then_inc(ld_qk, 16)
            act.dma_start(mask_raw[:], io["mask"].rearrange("(o b) p -> o (b p)", o=1)).then_inc(ld_mask, 16)

            def x_high(g):
                act.wait_ge(ld_x if g else ld_x0, 16)
                nc.scalar.activation(xT.hi[:, seqs(g), 2:], xT_raw[:, seqs(g), :], ACT.Copy).then_inc(xhi, 1)

            act.wait_ge(zeros_ok, 1)
            nc.scalar.activation(xT.hi[:, :, 0:2], zeros[:], ACT.Copy).then_inc(pads_ok, 1)
            nc.scalar.activation(xT.lo[:, :, 0:2], zeros[:], ACT.Copy).then_inc(pads_ok, 1)
            for c in range(3):
                act.wait_ge(w3_ok, c + 1)
                part = np.s_[:, :, c * D:(c + 1) * D]
                nc.scalar.activation(w3.hi[part], w3_raw[part], ACT.Copy).then_inc(whi, 1)
                if c == 0:
                    x_high(0)
            act.wait_ge(bias_ok, 1)

            def next_x_high(g):
                if g + 1 < NGRP:
                    x_high(g + 1)

            def projected(g):
                for c in range(3):
                    act.wait_ge(c_mm, 3 * g + c + 1)
                    wait(act, y_ok, g - 1)
                    nc.scalar.activation(C[:, g % 2, c], bank(C_BANKS[c]), ACT.Identity,
                                         bias=bias[:, c:c + 1]).then_inc(c_ok, 1)

            def normal(g):
                act.wait_ge(shift_ok, g + 1)
                wait(act, xT_mm, g)
                wait(act, res_ok, 2 * g)
                for b in range(GRP):
                    s = g * GRP + b
                    last = nc.scalar.activation(N1[:, b], R[:, b], ACT.Identity, bias=shift[:, s:s + 1],
                                                scale=rstd[:, s:s + 1])
                last.then_inc(n_ok, 1)

            def x1_high(g):
                act.wait_ge(xT_mm, g + 1)
                nc.scalar.activation(k.x1T.hi[:, cols(g)], banks[XT_BANK][:], ACT.Copy).then_inc(x1hi, 1)

            def m_high(g):
                for i in (2 * g, 2 * g + 1):
                    act.wait_ge(mm_m, i + 1)
                    m = weights[i // MQ][0]
                    nc.scalar.activation(m.hi[:, heads(i), :], bank(M_BANKS[i % 2]),
                                         ACT.Copy, scale=SCALE).then_inc(m_hi, 1)

            def raw_high(g):
                if g < 2:
                    act.wait_ge(ld_wv, 32)
                    wv = weights[g][1]
                    nc.scalar.activation(wv.hi[:], wv_raw[:, g], ACT.Copy).then_inc(raw_hi, 1)
                else:
                    act.wait_ge(ld_ctx, 16)
                    half = np.s_[:, (g - 2) * T // 2:(g - 1) * T // 2]
                    nc.scalar.activation(k.ctxT.hi[half], c_raw[half], ACT.Copy).then_inc(raw_hi, 1)

            ticks([(next_x_high, 0), (projected, 0), (x1_high, 2), (m_high, 0), (raw_high, 1), (normal, 1)])

        @block.gpsimd
        def _(pool):
            nc.gpsimd.memset(zeros[:], 0.0).then_inc(zeros_ok, 1)
            nc.gpsimd.memset(k.ident[:], 0.0).then_inc(ident0, 1)
            pool.wait_ge(ident0, 1)
            nc.gpsimd.affine_select(out=k.ident[:], in_=k.ident[:], compare_op=ALU.not_equal, fill=1.0, base=0,
                                    pattern=[[-1, 128]], channel_multiplier=1).then_inc(ident_ok, 1)
            nc.gpsimd.memset(KV[:], 0.0).then_inc(consts_ok, 1)
            nc.gpsimd.memset(k.half_neg[:], -0.5).then_inc(consts_ok, 1)
            nc.gpsimd.memset(k.one[:], 1.0).then_inc(consts_ok, 1)
            nc.gpsimd.memset(k.maskb[:], 0.0).then_inc(consts_ok, 1)
            nc.gpsimd.memset(k.ones_row0[:], 0.0).then_inc(consts_ok, 1)
            pool.wait_ge(consts_ok, 5)
            nc.gpsimd.memset(k.ones_row0[0:1, :], 1.0).then_inc(consts_ok, 1)
            pool.wait_ge(early_ok, 2)
            pool.wait_ge(consts_ok, 5)

            def keys_values(g):
                pool.wait_ge(c_ok, 3 * (g + 1))
                part = C[:, g % 2, :, :, 0:2]
                nc.gpsimd.tensor_tensor(part, part, early[:].unsqueeze(2).to_broadcast([128, 3, GRP, 2]),
                                        ALU.add).then_inc(fix_ok, 1)
                pool.wait_ge(fix_ok, g + 1)
                wait(pool, g_ok, g)
                nc.gpsimd.tensor_tensor(KV[:, :, 3:], C[:, g % 2, 1], C[:, g % 2, 2], ALU.mult).then_inc(kv_ok, 1)

            def gate(g):
                pool.wait_ge(g_ok, g + 1)
                wait(pool, o_mm, g)
                nc.gpsimd.tensor_tensor(yT[:], C[:, g % 2, 0], G[:], ALU.mult).then_inc(y_ok, 1)

            def output_bias(g):
                pool.wait_ge(ld_tok, 48)
                nc.gpsimd.tensor_tensor(k.xres[:, seqs(g), :], k.xres[:, seqs(g), :],
                                        b_out[:].unsqueeze(1).to_broadcast([128, GRP, 128]),
                                        ALU.add).then_inc(xb_ok, 1)

            def inverse_deviation(g):
                pool.wait_ge(mv_ok, g + 1)
                nc.gpsimd.tensor_tensor(rstd[:, seqs(g)], mv[:, seqs(g), 1], k.half_neg[:, 0:GRP],
                                        ALU.pow).then_inc(rstd_ok, 1)

            def residuals(g):
                pool.wait_ge(ld_rows, 16 * ROWS)
                pool.wait_ge(n_ok, g + 1)
                pool.wait_ge(xlo, g + 1)
                for dst, row in ((k.xres, k.rows["sa_bo"]), (k.x1, ln3_b)):
                    nc.gpsimd.tensor_tensor(dst[:, seqs(g), :], N1[:], row[:].unsqueeze(1).to_broadcast([128, GRP, 128]),
                                            ALU.add).then_inc(res_ok, 1)

            ticks([(keys_values, 0), (residuals, 2), (inverse_deviation, 1), (gate, 0), (output_bias, 0)])

        @block.vector
        def _(vec):
            def x_low(g):
                vec.wait_ge(xhi, g + 1)
                nc.vector.tensor_tensor(xT.lo[:, seqs(g), 2:], xT_raw[:, seqs(g), :], f32(xT.hi[:, seqs(g), 2:]),
                                        ALU.subtract).then_inc(xlo, 1)

            vec.wait_ge(ld_win, 16)
            for c in range(3):
                vec.wait_ge(ld_taps[c], 16)
                part = np.s_[:, :, c * D:(c + 1) * D]
                nc.vector.tensor_tensor(w3_raw[part], w_in[:, c * D:(c + 1) * D].unsqueeze(1).to_broadcast([128, 3, D]),
                                        tap_rows[part], ALU.mult).then_inc(w3_ok, 1)
                vec.wait_ge(whi, c + 1)
                nc.vector.tensor_tensor(w3.lo[part], w3_raw[part], f32(w3.hi[part]), ALU.subtract).then_inc(wlo, 1)
                if c == 0:
                    x_low(0)
            vec.wait_ge(ld_small, 16 * 5)
            nc.vector.tensor_tensor(tap_b[:], taps[:], b_in[:].unsqueeze(2).to_broadcast([128, 3, 3]),
                                    ALU.mult).then_inc(tapb_ok, 1)
            vec.wait_ge(tapb_ok, 1)
            nc.vector.tensor_scalar(early[:, :, 1], tap_b[:, :, 0], -1.0, None, ALU.mult).then_inc(early_ok, 1)
            vec.wait_ge(early_ok, 1)
            nc.vector.tensor_tensor(early[:, :, 0], early[:, :, 1], tap_b[:, :, 1], ALU.subtract).then_inc(early_ok, 1)
            nc.vector.tensor_tensor(short_b[:], short_b[:], tap_b[:, :, 2], ALU.add).then_inc(tapb_ok, 1)
            vec.wait_ge(early_ok, 2)
            vec.wait_ge(tapb_ok, 2)
            nc.vector.tensor_tensor(bias[:], short_b[:], early[:, :, 0], ALU.subtract).then_inc(bias_ok, 1)

            links = count(1)

            def next_x_low(g):
                if g + 1 < NGRP:
                    x_low(g + 1)

            def inner_convolution(g):
                vec.wait_ge(kv_ok, g + 1)
                wait(vec, y_ok, g)
                nc.vector.tensor_scalar(G[:], KV[:, :, 3:3 + L], inner[:, 3:4], inner_b[:, 0:1],
                                        ALU.mult, ALU.add).then_inc(link, 1)
                for j in range(3):
                    vec.wait_ge(link, next(links))
                    nc.vector.scalar_tensor_tensor(G[:], KV[:, :, j:j + L], inner[:, j:j + 1], G[:],
                                                   ALU.mult, ALU.add).then_inc(link if j < 2 else g_ok, 1)

            def residual(g):
                vec.wait_ge(o_mm, g + 1)
                vec.wait_ge(xb_ok, g + 1)
                wait(vec, n_ok, g)
                nc.vector.tensor_tensor(R[:], bank(OUT_BANK), k.xres[:, seqs(g), :], ALU.add).then_inc(r_ok, 1)
                vec.wait_ge(r_ok, g + 1)
                for b in range(GRP):
                    last = nc.vector.bn_stats(stats[:, g * GRP + b], R[:, b])
                last.then_inc(link, 1)
                vec.wait_ge(link, next(links))
                for b in range(GRP):
                    last = nc.vector.bn_aggr(mv[:, g * GRP + b], stats[:, g * GRP + b])
                last.then_inc(link, 1)
                vec.wait_ge(link, next(links))
                nc.vector.tensor_scalar(mv[:, seqs(g), 1], mv[:, seqs(g), 1], EPS, None, ALU.add).then_inc(mv_ok, 1)

            def mean_shift(g):
                vec.wait_ge(rstd_ok, g + 1)
                nc.vector.scalar_tensor_tensor(shift[:, seqs(g)], mv[:, seqs(g), 0], -1.0, rstd[:, seqs(g)],
                                               ALU.mult, ALU.mult).then_inc(shift_ok, 1)

            def x1_low(g):
                vec.wait_ge(x1hi, g + 1)
                nc.vector.tensor_tensor(k.x1T.lo[:, cols(g)], banks[XT_BANK][:], f32(k.x1T.hi[:, cols(g)]),
                                        ALU.subtract).then_inc(x1lo, 1)

            def m_low(g):
                for i in (2 * g, 2 * g + 1):
                    vec.wait_ge(m_hi, i + 1)
                    m = weights[i // MQ][0]
                    part = np.s_[:, heads(i), :]
                    nc.vector.scalar_tensor_tensor(m.lo[part], bank(M_BANKS[i % 2]), SCALE, f32(m.hi[part]),
                                                   ALU.mult, ALU.subtract).then_inc(m_lo, 1)

            def raw_low(g):
                if g == 0:
                    vec.wait_ge(ld_mask, 16)
                    vec.wait_ge(consts_ok, 6)
                    nc.vector.tensor_scalar(k.maskb[0:1, :], mask_raw[:], MASKED, None,
                                            ALU.mult).then_inc(kept_ok, 1)
                if g < 2:
                    vec.wait_ge(raw_hi, g + 1)
                    wv = weights[g][1]
                    nc.vector.tensor_tensor(wv.lo[:], wv_raw[:, g], f32(wv.hi[:]), ALU.subtract).then_inc(kept_ok, 1)
                else:
                    vec.wait_ge(raw_hi, g + 1)
                    half = np.s_[:, (g - 2) * T // 2:(g - 1) * T // 2]
                    nc.vector.tensor_tensor(k.ctxT.lo[half], c_raw[half], f32(k.ctxT.hi[half]),
                                            ALU.subtract).then_inc(kept_ok, 1)

            ticks([(next_x_low, 0), (residual, 1), (x1_low, 2), (inner_convolution, 0), (mean_shift, 1), (m_low, 0),
                   (raw_low, 1)])

        @block.tensor
        def _(pe):
            pe.wait_ge(ident_ok, 1)
            pe.wait_ge(pads_ok, 2)

            def projections(g):
                pe.wait_ge(xlo, g + 1)
                for c in range(3):
                    if g == 0:
                        pe.wait_ge(wlo, c + 1)
                    wait(pe, c_ok, 3 * g + c - 2)
                    for j in range(3):
                        out = bank(C_BANKS[c])
                        w = np.s_[:, j, c * D:(c + 1) * D]
                        hi, lo = (part[:, seqs(g), j:j + L] for part in (xT.hi, xT.lo))
                        nc.tensor.matmul(out, w3.hi[w], hi, start=(j == 0), stop=False)
                        nc.tensor.matmul(out, w3.hi[w], lo, start=False, stop=False)
                        last = nc.tensor.matmul(out, w3.lo[w], hi, start=False, stop=(j == 2))
                    last.then_inc(c_mm, 1)

            def output(g):
                pe.wait_ge(ld_tok, 48)
                pe.wait_ge(y_ok, g + 1)
                wait(pe, r_ok, g)
                for b in range(GRP):
                    last = nc.tensor.matmul(banks[OUT_BANK][:, b * 128:(b + 1) * 128], yT[:, b, :], w_out[:],
                                            start=True, stop=True)
                last.then_inc(o_mm, 1)

            def x1_transposes(g):
                pe.wait_ge(n_ok, g + 1)
                wait(pe, x1lo, g)
                for b in range(GRP):
                    last = nc.tensor.transpose(banks[XT_BANK][:, b * 128:(b + 1) * 128], N1[:, b, :], k.ident[:])
                last.then_inc(xT_mm, 1)

            def weight_products(g):
                for i in (2 * g, 2 * g + 1):
                    pe.wait_ge(ld_qk, 32 * (i // MQ + 1))
                    wait(pe, m_lo, i - 1)
                    for c in range(HQ):
                        wq, wk = (qkT[i % 2 * DH:(i % 2 + 1) * DH, j, i % MQ // 2 * HQ + c, :] for j in range(2))
                        last = nc.tensor.matmul(banks[M_BANKS[i % 2]][:, c * 128:(c + 1) * 128], wk, wq,
                                                start=True, stop=True)
                    last.then_inc(mm_m, 1)

            ticks([(projections, 0), (output, 1), (x1_transposes, 2), (weight_products, 0)])


def allocate_late(k, ctx):
    k.V = k.sb(ctx, "V", [128, PAIR, INNER])
    k.P = k.sb(ctx, "P", [128, P_RING, HQ, 128])
    k.hT = (k.V[:].rearrange("p b (c l) -> p (b c l)", l=128).rearrange("p (c b l) -> p c b l", b=GRP, l=128),
            k.P[:])
    k.late_banks = k.banks(ctx, "late")
    k.fc1_mm, k.h_ok, k.fc2_mm = k.sems(ctx, "late", "fc1_mm h_ok fc2_mm")


def hidden(k, pe, g, blocks=range(FF // 128)):
    for c in blocks:
        wait(pe, k.h_ok, 4 * g + c - 3)
        mm_split(k.nc, k.late_banks[c][:], k.fc1, np.s_[:, c * 128:(c + 1) * 128], k.x1T,
                 np.s_[:, g * GCOLS:(g + 1) * GCOLS]).then_inc(k.fc1_mm, 1)


def gelu_hidden(k, act, g):
    for c in range(FF // 128):
        act.wait_ge(k.fc1_mm, 4 * g + c + 1)
        if c == 0:
            wait(act, k.fc2_mm, g - 1)
        k.nc.scalar.activation(k.hT[g % 2][:, c], k.late_banks[c][:].rearrange("p (b l) -> p b l", b=GRP), ACT.Gelu,
                               bias=k.fc1_b[:, c:c + 1]).then_inc(k.h_ok, 1)


def fc2_sum(k, pe, g):
    pe.wait_ge(k.h_ok, 4 * (g + 1))
    for b in range(GRP):
        for c in range(FF // 128):
            last = k.nc.tensor.matmul(k.late_banks[FC2_BANK][:, b * 128:(b + 1) * 128], k.hT[g % 2][:, c, b, :],
                                      k.fc2[:, c, :], start=(c == 0), stop=(c == FF // 128 - 1))
    last.then_inc(k.fc2_mm, 1)


def attentions(k):
    nc = k.nc
    with ExitStack() as ctx:
        fc1_raw = k.sb(ctx, "fc1_raw", [128, FF])
        w1_raw = k.sb(ctx, "w1_raw", [128, 128])
        xq = k.split(ctx, "at_xq", [128, PAIR, 128])
        xv = k.split(ctx, "at_xv", [128, PAIR, 128])
        y = k.split(ctx, "at_y", [128, PAIR, H, 128])
        PT = k.sb(ctx, "at_PT", [128, 2, HQ * 128])
        OT = k.sb(ctx, "at_OT", [128, PAIR, H // 2, 128])
        negmax = k.sb(ctx, "at_negmax", [128, 2, HQ])
        total = k.sb(ctx, "at_total", [128, 2, HQ])
        inv = k.sb(ctx, "at_inv", [128, 2, HQ])
        R = k.sb(ctx, "at_R", [128, PAIR, 128])
        N = k.sb(ctx, "at_N", [128, PAIR, 128])
        X = k.sb(ctx, "at_X", [128, PAIR, 128])
        stats = k.sb(ctx, "at_stats", [128, PAIR, 6])
        mv = k.sb(ctx, "at_mv", [128, PAIR, 2])
        rstd = k.sb(ctx, "at_rstd", [128, PAIR])
        V, P, banks = k.V, k.P, k.late_banks
        Y_BANK, S_BANK, PT_BANK, O_BANK, V_BANK, W_BANK = (0, 1), (2, 3), 4, 5, 6, 7
        (y_mm, y_hi, y_lo, s_mm, max_ok, exp_ok, inv_ok, norm_ok, t_mm, pt_ok, pv_mm, o_ok, v_mm, v_ok,
         xq_ok, xv_ok, wo_mm, r_ok, st_ok, mv_ok, rstd_ok, n_ok, gain_ok, x_ok, res_ok, xT_mm, xT_hi,
         xT_lo, spare) = k.sems(ctx, "at", """y_mm y_hi y_lo s_mm max_ok exp_ok inv_ok norm_ok t_mm pt_ok pv_mm o_ok
             v_mm v_ok xq_ok xv_ok wo_mm r_ok st_ok mv_ok rstd_ok n_ok gain_ok x_ok res_ok xT_mm xT_hi
             xT_lo spare""")
        block = ctx.enter_context(nc.Block())
        queries_T, keys_T = (k.x1T, k.x2T), (k.x1T, k.ctxT)
        heads_m, values_w, out_w = (k.m_sa, k.m_ca), (k.wv_sa, k.wv_ca), (k.wo_sa, k.wo_ca)
        gains, shifts = (k.rows["ln1_g"], k.rows["ln2_g"]), (k.rows["ln1_b"], k.rows["ln2_b"])
        next_biases, results = (k.rows["ca_bo"], k.rows["fc2_b"]), (k.x2T, k.x1T)
        V1_STEPS = (3, 4)
        V0_STEPS = (6, 7)
        XV_STEP = 5
        WO_STEP, XT_STEP = 3, 6

        looping = [0]

        def att(t):
            return t // NPAIR if isinstance(t, int) else looping[0]

        def first_seq(t):
            return (t - NPAIR * att(t)) * PAIR

        def cols(t, n=PCOLS, off=0):
            return bass.ds(first_seq(t) * L + off, n)

        def exists(t):
            return not isinstance(t, int) or 0 <= t < 2 * NPAIR

        def iterations(engine, body):
            for a in range(2):
                looping[0] = a
                body(a * NPAIR)
                with engine.Fori(a * NPAIR + 1, (a + 1) * NPAIR - 1) as t:
                    body(t)
                body((a + 1) * NPAIR - 1)

        @block.sync
        def _(sp):
            load_feed_forward(k, sp, fc1_raw, w1_raw)

        @block.tensor
        def _(pe):
            def y_unit(t, u):
                n = UNITS * t + u
                wait(pe, y_lo, n - 1)
                for j in range(2):
                    last = mm_split(nc, banks[Y_BANK[u % 2]][:, j * PCOLS:(j + 1) * PCOLS], heads_m[att(t)],
                                    np.s_[:, 2 * u + j, :], keys_T[att(t)], np.s_[:, cols(t)])
                last.then_inc(y_mm, 1)

            def scores(t, g):
                n, b, hq = QUADS * t + g, g % PAIR, g // PAIR
                wait(pe, y_lo, UNITS * t + 2 * hq + 2)
                if hq == 0:
                    wait(pe, xq_ok, PAIR * t + b + 1)
                wait(pe, exp_ok, n - 1)
                out = banks[S_BANK[g % 2]][:]
                nc.tensor.matmul(out, k.ones_row0[:],
                                 k.maskb[:, cols(t, 128, b * 128)].unsqueeze(1).to_broadcast([128, HQ, 128]),
                                 start=True, stop=False)
                mm_split(nc, out, xq, np.s_[:, b, :], y, np.s_[:, b, HQ * hq:HQ * (hq + 1), :],
                         first=False).then_inc(s_mm, 1)

            def transposes(n, g):
                wait(pe, norm_ok, n + 1)
                wait(pe, pt_ok, n)
                for h in range(HQ):
                    last = nc.tensor.transpose(banks[PT_BANK][:, h * 128:(h + 1) * 128], P[:, g % P_RING, h, :],
                                               k.ident[:])
                last.then_inc(t_mm, 1)

            def p_v(t, n, g):
                b, hq = g % PAIR, g // PAIR
                wait(pe, pt_ok, n + 1)
                wait(pe, v_ok, 4 * t + (2 if hq < 2 else 4))
                wait(pe, o_ok, n)
                for h in range(HQ):
                    part = 64 * (h % 2)
                    last = nc.tensor.matmul(banks[O_BANK][part:part + 64, (h // 2) * 128:(h // 2 + 1) * 128],
                                            V[:, b, (HQ * hq + h) * DH:(HQ * hq + h + 1) * DH],
                                            PT[:, g % 2, h * 128:(h + 1) * 128], start=True, stop=True)
                last.then_inc(pv_mm, 1)

            def v_half(i, t, b, half):
                wait(pe, xv_ok, t + 1)
                wait(pe, v_ok, i)
                mm_split(nc, banks[V_BANK][:], xv, np.s_[:, b, :], values_w[att(t)],
                         np.s_[:, half * 512:(half + 1) * 512]).then_inc(v_mm, 1)

            def out_proj(t):
                wait(pe, o_ok, QUADS * (t + 1))
                wait(pe, xT_lo, t)
                for b in range(PAIR):
                    for c in range(H // 2):
                        last = nc.tensor.matmul(banks[W_BANK][:, b * 128:(b + 1) * 128], OT[:, b, c, :],
                                                out_w[att(t)][:, c, :],
                                                start=(c == 0), stop=(c == H // 2 - 1))
                last.then_inc(wo_mm, 1)

            def x_transposes(t):
                wait(pe, x_ok, t + 1)
                for b in range(PAIR):
                    last = nc.tensor.transpose(banks[W_BANK][:, b * 128:(b + 1) * 128], X[:, b, :], k.ident[:])
                last.then_inc(xT_mm, 1)

            def pair(t):
                for g in range(QUADS):
                    n = QUADS * t + g
                    scores(t, g)
                    if g + Y_AHEAD < UNITS:
                        y_unit(t, g + Y_AHEAD)
                    elif exists(t + 1):
                        y_unit(t + 1, g + Y_AHEAD - UNITS)
                    back = 1 if g < T_LAG else 0
                    if exists(t - back):
                        transposes(n - T_LAG, (g - T_LAG) % QUADS)
                    if g == WO_STEP and exists(t - 1):
                        out_proj(t - 1)
                    back = 1 if g < PV_LAG else 0
                    if exists(t - back):
                        p_v(t - back, n - PV_LAG, (g - PV_LAG) % QUADS)
                    if g in V1_STEPS:
                        b = V1_STEPS.index(g)
                        v_half(4 * t + 2 + b, t, b, 1)
                    if g in V0_STEPS and exists(t + 1):
                        b = V0_STEPS.index(g)
                        v_half(4 * t + 4 + b, t + 1, b, 0)
                    if g == XT_STEP and exists(t - 1):
                        x_transposes(t - 1)

            for u in range(Y_AHEAD):
                y_unit(0, u)
            for b in range(PAIR):
                v_half(b, 0, b, 0)
            iterations(pe, pair)
            N_ALL = QUADS * 2 * NPAIR
            pe.wait_ge(k.ff_lo, 2)
            pe.wait_ge(xT_lo, NPAIR + 2)
            for n in range(N_ALL, N_ALL + PV_LAG):
                if n - T_LAG < N_ALL:
                    transposes(n - T_LAG, (n - T_LAG) % QUADS)
                if n == N_ALL + 1:
                    pe.wait_ge(exp_ok, N_ALL)
                hidden(k, pe, 0, [n - N_ALL])
                p_v(2 * NPAIR - 1, n - PV_LAG, (n - PV_LAG) % QUADS)
            hidden(k, pe, 0, range(PV_LAG, FF // 128))
            out_proj(2 * NPAIR - 1)
            pe.wait_ge(xT_lo, NPAIR + 4)
            hidden(k, pe, 1)
            x_transposes(2 * NPAIR - 1)
            fc2_sum(k, pe, 0)

        @block.scalar
        def _(act):
            def exps(n, g):
                wait(act, max_ok, n + 1)
                for h in range(HQ):
                    last = nc.scalar.activation(P[:, g % P_RING, h, :], banks[S_BANK[g % 2]][:, h * 128:(h + 1) * 128],
                                                ACT.Exp, bias=negmax[:, g % 2, h:h + 1],
                                                accum_out=total[:, g % 2, h:h + 1])
                last.then_inc(exp_ok, 1)

            def y_high(t, u):
                n = UNITS * t + u
                wait(act, y_mm, n + 1)
                wait(act, s_mm, QUADS * (t - 1) + 2 * (u // 2) + 2)
                for b in range(PAIR):
                    last = nc.scalar.activation(
                        y.hi[:, b, 2 * u:2 * u + 2, :],
                        banks[Y_BANK[u % 2]][:].rearrange("p (h b l) -> p b h l", h=2, b=PAIR)[:, b], ACT.Copy)
                last.then_inc(y_hi, 1)

            def v_out(i, t, b, half):
                wait(act, v_mm, i + 1)
                wait(act, pv_mm, QUADS * (t - 1) + (4 if half == 0 else 8))
                nc.scalar.activation(V[:, b, half * 512:(half + 1) * 512], banks[V_BANK][:], ACT.Copy).then_inc(v_ok, 1)

            def xT_high(t):
                wait(act, xT_mm, t + 1)
                nc.scalar.activation(results[att(t)].hi[:, cols(t)], banks[W_BANK][:, 0:PCOLS],
                                     ACT.Copy).then_inc(xT_hi, 1)

            def o_out(n, g):
                b, hq = g % PAIR, g // PAIR
                wait(act, pv_mm, n + 1)
                nc.scalar.activation(OT[:, b, 2 * hq:2 * hq + 2, :],
                                     banks[O_BANK][:, 0:256].rearrange("p (c l) -> p c l", c=2),
                                     ACT.Copy).then_inc(o_ok, 1)

            def behind(t, g):
                n = QUADS * t + g
                if g >= PV_LAG or exists(t - 1):
                    if g == PV_LAG:
                        wait(act, wo_mm, t)
                    o_out(n - PV_LAG, (g - PV_LAG) % QUADS)
                if g + Y_AHEAD < UNITS:
                    y_high(t, g + Y_AHEAD)
                elif exists(t + 1):
                    y_high(t + 1, g + Y_AHEAD - UNITS)
                if g in V1_STEPS:
                    b = V1_STEPS.index(g)
                    v_out(4 * t + 2 + b, t, b, 1)
                if g in V0_STEPS and exists(t + 1):
                    b = V0_STEPS.index(g)
                    v_out(4 * t + 4 + b, t + 1, b, 0)
                if g == XT_STEP and exists(t - 1):
                    xT_high(t - 1)

            def pair(t):
                for g in range(QUADS):
                    if g > 0:
                        behind(t, g - 1)
                    elif exists(t - 1):
                        behind(t - 1, QUADS - 1)
                    exps(QUADS * t + g, g)
                if isinstance(t, int) and t == NPAIR:
                    weights_high()

            def weights_high():
                act.wait_ge(k.ff_ld, 16 * FF_LOADS)
                nc.scalar.activation(k.fc1.hi[:], fc1_raw[:], ACT.Copy).then_inc(k.ff_hi, 1)
                nc.scalar.activation(k.w1.hi[:], w1_raw[:], ACT.Copy, scale=k.gainT[:, NEXP:]).then_inc(k.ff_hi, 1)

            for u in range(Y_AHEAD):
                y_high(0, u)
            for b in range(PAIR):
                v_out(b, 0, b, 0)
            iterations(act, pair)
            behind(2 * NPAIR - 1, QUADS - 1)
            N_ALL = QUADS * 2 * NPAIR
            for n in range(N_ALL - PV_LAG, N_ALL):
                o_out(n, n % QUADS)
            for g in range(HIDDEN_AHEAD):
                gelu_hidden(k, act, g)
            xT_high(2 * NPAIR - 1)

        @block.vector
        def _(vec):
            def reciprocals(n, g):
                wait(vec, exp_ok, n + 1)
                nc.vector.reciprocal(inv[:, g % 2], total[:, g % 2]).then_inc(inv_ok, 1)

            def y_low(t, u):
                n = UNITS * t + u
                wait(vec, y_hi, n + 1)
                for b in range(PAIR):
                    last = nc.vector.tensor_tensor(
                        y.lo[:, b, 2 * u:2 * u + 2, :],
                        banks[Y_BANK[u % 2]][:].rearrange("p (h b l) -> p b h l", h=2, b=PAIR)[:, b],
                        f32(y.hi[:, b, 2 * u:2 * u + 2, :]), ALU.subtract)
                last.then_inc(y_lo, 1)

            def maxima(n, g):
                wait(vec, s_mm, n + 1)
                nc.vector.tensor_reduce(negmax[:, g % 2], banks[S_BANK[g % 2]][:].rearrange("p (h l) -> p h l", h=HQ),
                                        AX_X, ALU.max, negate=True).then_inc(max_ok, 1)

            def pt_out(n, g):
                wait(vec, t_mm, n + 1)
                wait(vec, pv_mm, n - 1)
                nc.vector.tensor_copy(PT[:, g % 2], banks[PT_BANK][:]).then_inc(pt_ok, 1)

            def residual(t):
                wait(vec, wo_mm, t + 1)
                nc.vector.tensor_tensor(R[:], banks[W_BANK][:, 0:PCOLS].rearrange("p (b d) -> p b d", b=PAIR),
                                        k.xres[:, bass.ds(first_seq(t), PAIR), :], ALU.add).then_inc(r_ok, 1)
                wait(vec, r_ok, t + 1)
                for b in range(PAIR):
                    last = nc.vector.bn_stats(stats[:, b], R[:, b])
                last.then_inc(st_ok, 1)
                wait_apart(vec, st_ok, 2 * t + 1, spare)
                for b in range(PAIR):
                    last = nc.vector.bn_aggr(mv[:, b], stats[:, b])
                last.then_inc(st_ok, 1)
                wait_apart(vec, st_ok, 2 * t + 2, spare)
                nc.vector.tensor_scalar(mv[:, :, 1], mv[:, :, 1], EPS, None, ALU.add).then_inc(mv_ok, 1)

            def normalise(t):
                wait(vec, rstd_ok, t + 1)
                for b in range(PAIR):
                    last = nc.vector.tensor_scalar(N[:, b], R[:, b], mv[:, b, 0:1], rstd[:, b:b + 1],
                                                   ALU.subtract, ALU.mult)
                last.then_inc(n_ok, 1)

            def xT_low(t):
                wait(vec, xT_hi, t + 1)
                out = results[att(t)]
                nc.vector.tensor_tensor(out.lo[:, cols(t)], banks[W_BANK][:, 0:PCOLS], f32(out.hi[:, cols(t)]),
                                        ALU.subtract).then_inc(xT_lo, 1)

            def pair(t):
                for g in range(QUADS):
                    n = QUADS * t + g
                    if exists(t - (g < 1)):
                        reciprocals(n - 1, (g - 1) % QUADS)
                    maxima(n, g)
                    u = g - 1 + Y_AHEAD
                    if u < UNITS and (g > 0 or exists(t - 1)):
                        y_low(t, u)
                    elif u >= UNITS and exists(t + 1):
                        y_low(t + 1, u - UNITS)
                    if exists(t - (g < T_LAG)):
                        pt_out(n - T_LAG, (g - T_LAG) % QUADS)
                    if g == WO_STEP and exists(t - 1):
                        residual(t - 1)
                    if g == WO_STEP + 1 and exists(t - 1):
                        normalise(t - 1)
                    if g == XT_STEP and exists(t - 1):
                        xT_low(t - 1)
                if isinstance(t, int) and t == NPAIR:
                    weights_low()

            def weights_low():
                vec.wait_ge(k.ff_hi, 2)
                nc.vector.tensor_tensor(k.fc1.lo[:], fc1_raw[:], f32(k.fc1.hi[:]), ALU.subtract).then_inc(k.ff_lo, 1)
                nc.vector.scalar_tensor_tensor(k.w1.lo[:], w1_raw[:], k.gainT[:, NEXP:], f32(k.w1.hi[:]),
                                               ALU.mult, ALU.subtract).then_inc(k.ff_lo, 1)

            for u in range(Y_AHEAD):
                y_low(0, u)
            iterations(vec, pair)
            N_ALL = QUADS * 2 * NPAIR
            reciprocals(N_ALL - 1, (N_ALL - 1) % QUADS)
            for n in range(N_ALL - T_LAG, N_ALL):
                pt_out(n, n % QUADS)
            residual(2 * NPAIR - 1)
            normalise(2 * NPAIR - 1)
            xT_low(2 * NPAIR - 1)

        @block.gpsimd
        def _(pool):
            def copy(dst, src):
                return nc.gpsimd.tensor_tensor(dst, f32(src), k.one[:].to_broadcast([128, src.shape[1]]), ALU.mult)

            def queries(t, b):
                wait_apart(pool, s_mm, QUADS * (t - 1) + QUADS - PAIR + b + 1, spare)
                src = queries_T[att(t)]
                copy(xq.hi[:, b], src.hi[:, cols(t, 128, b * 128)])
                copy(xq.lo[:, b], src.lo[:, cols(t, 128, b * 128)]).then_inc(xq_ok, 1)

            def keys(t):
                wait_apart(pool, v_mm, 4 * t, spare)
                src = keys_T[att(t)]
                copy(xv.hi[:].rearrange("p b l -> p (b l)"), src.hi[:, cols(t)])
                copy(xv.lo[:].rearrange("p b l -> p (b l)"), src.lo[:, cols(t)]).then_inc(xv_ok, 1)

            def normalise(n, g):
                wait(pool, inv_ok, n + 1)
                tile = P[:, g % P_RING]
                nc.gpsimd.tensor_tensor(tile, tile, inv[:, g % 2].unsqueeze(2).to_broadcast([128, HQ, 128]),
                                        ALU.mult).then_inc(norm_ok, 1)

            def inverse_deviation(t):
                wait(pool, mv_ok, t + 1)
                nc.gpsimd.tensor_tensor(rstd[:], mv[:, :, 1], k.half_neg[:, 0:PAIR], ALU.pow).then_inc(rstd_ok, 1)

            def row(r):
                return r[:].unsqueeze(1).to_broadcast([128, PAIR, 128])

            def affine(t):
                wait(pool, n_ok, t + 1)
                nc.gpsimd.tensor_tensor(N[:], N[:], row(gains[att(t)]), ALU.mult).then_inc(gain_ok, 1)
                wait(pool, gain_ok, t + 1)
                wait(pool, xT_mm, t)
                nc.gpsimd.tensor_tensor(X[:], N[:], row(shifts[att(t)]), ALU.add).then_inc(x_ok, 1)

            def next_residual(t):
                wait_apart(pool, x_ok, t + 1, spare)
                nc.gpsimd.tensor_tensor(k.xres[:, bass.ds(first_seq(t), PAIR), :], X[:], row(next_biases[att(t)]),
                                        ALU.add).then_inc(res_ok, 1)

            def pair(t):
                for g in range(QUADS):
                    n = QUADS * t + g
                    if g == QUADS - 1 and exists(t + 1):
                        queries(t + 1, 0)
                    if g == 0 and exists(t - 1):
                        queries(t, 1)
                    if g == XV_STEP and exists(t + 1):
                        keys(t + 1)
                    if exists(t - (g < 1)):
                        normalise(n - 1, (g - 1) % QUADS)
                    if g == WO_STEP and exists(t - 1):
                        inverse_deviation(t - 1)
                    if g == WO_STEP + 1 and exists(t - 1):
                        affine(t - 1)
                    if g == XT_STEP and exists(t - 1):
                        next_residual(t - 1)

            queries(0, 0)
            queries(0, 1)
            keys(0)
            iterations(pool, pair)
            normalise(2 * QUADS * NPAIR - 1, QUADS - 1)
            inverse_deviation(2 * NPAIR - 1)
            affine(2 * NPAIR - 1)
            next_residual(2 * NPAIR - 1)


def feed_forward(k):
    nc, io = k.nc, k.io
    with ExitStack() as ctx:
        sb = k.sb
        R = sb(ctx, "ffR", [128, 2, GRP, 128])
        N3 = sb(ctx, "N3", [128, 2, GRP, 128])
        N5 = sb(ctx, "N5", [128, 2, GRP, 128])
        X4 = k.x1
        res = k.xres
        zT = k.split(ctx, "zT", [128, 2, GRP, 128])
        gT = sb(ctx, "gT", [128, 2, GRP, 128])
        w1_raw = sb(ctx, "w1_raw_again", [128, 128])
        w1e = sb(ctx, "w1e", [128, NEXP, 128])
        w2e = sb(ctx, "w2e", [128, NEXP, 128])
        b1 = sb(ctx, "b1", [128, NEXP + 1])
        zE = sb(ctx, "zE", [128, NSEQ, NEXP])
        hE = sb(ctx, "hE", [128, NEXP, QUADRANT])
        hE_in = sb(ctx, "hE_in", [128, NEXP, NSEQ])
        xE = sb(ctx, "xE", [128, NEXP // EQ, 128])
        rE = sb(ctx, "rE", [128, NEXP // EQ, 128])
        stats = sb(ctx, "ffstats", [128, 4, NSEQ, 6])
        mv = sb(ctx, "ffmv", [128, 4, NSEQ, 2])
        rstd = sb(ctx, "ffrstd", [128, 4, NSEQ])
        shift = sb(ctx, "ffshift", [128, 4, NSEQ])
        stats_e = sb(ctx, "stats_e", [128, NEXP // EQ, 6])
        mv_e = sb(ctx, "mv_e", [128, NEXP // EQ, 2])
        rstd_e = sb(ctx, "rstd_e", [128, NEXP // EQ])
        banks = k.late_banks
        ZT_BANK, W1_BANK, W2_BANK = 5, 6, 7
        B1_BANK, E1_BANK, E2_BANK = W2_BANK, 0, 1
        (ld_w1e, ld_w2e, r_ok, x4a, x4b, zT_mm, z_hi, z_lo, ze_ok, w1_mm, g_ok, w2_mm, res_ok, b1_mm,
         b1_ok, w1e_ok, parked, xe_in, e1_mm, e1_b, e1_g, e2_mm, re_ok, link, mv_e_ok, rstd_e_ok, ne_ok, stored,
         zeroed) = k.sems(ctx, "ff", """ld_w1e ld_w2e r_ok x4a x4b zT_mm z_hi z_lo ze_ok w1_mm g_ok
            w2_mm res_ok b1_mm b1_ok w1e_ok parked xe_in e1_mm e1_b e1_g e2_mm re_ok link mv_e_ok rstd_e_ok
            ne_ok stored zeroed""")
        mvs, rstd_ok, nrm = (k.sems(ctx, "ff", " ".join(f"{n}{i}" for i in range(4)))
                             for n in ("moments", "rstd", "normal"))
        shift1_ok, shift2_ok, shift3_ok = k.sems(ctx, "ff", "shift1_ok shift2_ok shift3_ok")
        shift_ok = {1: shift1_ok, 2: shift2_ok, 3: shift3_ok}
        block = ctx.enter_context(nc.Block())

        def quarter(bank):
            return banks[bank][:].rearrange("p (b d) -> p b d", b=GRP)

        def seqs(g):
            return slice(g * GRP, (g + 1) * GRP)

        def ticks(stages):
            for tick in range(NGRP + 10):
                for stage, behind in stages:
                    if 0 <= tick - behind < NGRP:
                        stage(tick - behind)

        def first(step):
            return lambda g: step() if g == 0 else None

        def last_group(step):
            return lambda g: step() if g == NGRP - 1 else None

        @block.sync
        def _(sp):
            sp.dma_start(w1_raw[:], io["W1_s"]).then_inc(ld_w1e, 16)
            sp.dma_start(w1e[:], io["W1_e"].rearrange("n d h -> d n h")).then_inc(ld_w1e, 16)
            sp.dma_start(w2e[:], io["W2_e"].rearrange("n d h -> d n h")).then_inc(ld_w2e, 16)
            for g in range(NGRP):
                sp.wait_ge(x4b, g + 1)
                sp.dma_start(io["scratch"].rearrange("b n d -> n b d")[:, seqs(g), :],
                             X4[0:NEXP, seqs(g), :]).then_inc(parked, 16)
            sp.wait_ge(parked, 16 * NGRP)
            sp.wait_ge(zeroed, 3)
            for i in range(EQ):
                sp.dma_start(xE[QUADRANT * i:QUADRANT * i + NSEQ],
                             io["scratch"].rearrange("b (c i) d -> i b c d", i=EQ)[i]).then_inc(xe_in, 16)
            for g in range(NGRP):
                sp.wait_ge(nrm[3], g + 1)
                sp.dma_start(io["out"].rearrange("b p d -> p b d")[NEXP:, seqs(g), :],
                             res[NEXP:, seqs(g), :]).then_inc(stored, 16)
            sp.wait_ge(ne_ok, 1)
            for i in range(EQ):
                sp.dma_start(io["out"][:, 0:NEXP].rearrange("b (c i) d -> i b c d", i=EQ)[i],
                             rE[QUADRANT * i:QUADRANT * i + NSEQ]).then_inc(stored, 16)
            sp.wait_ge(stored, 16 * (NGRP + EQ))

        @block.tensor
        def _(pe):
            def later_hidden(g):
                if g >= HIDDEN_AHEAD:
                    hidden(k, pe, g)

            def shift_products():
                pe.wait_ge(ld_w1e, 32)
                for e in range(NEXP + 1):
                    w = w1e[:, e, :] if e < NEXP else w1_raw[:]
                    last = nc.tensor.matmul(banks[B1_BANK][:, e:e + 1], w, k.shiftT[:, e:e + 1], start=True, stop=True)
                last.then_inc(b1_mm, 1)

            def later_fc2(g):
                if g > 0:
                    pe.wait_ge(r_ok, g)
                    fc2_sum(k, pe, g)

            def z_transposes(g):
                pe.wait_ge(nrm[2], g + 1)
                wait(pe, ze_ok, g)
                for b in range(GRP):
                    last = nc.tensor.transpose(banks[ZT_BANK][:, b * 128:(b + 1) * 128], N5[:, g % 2, b, :],
                                               k.ident[:])
                last.then_inc(zT_mm, 1)

            def shared_w1(g):
                pe.wait_ge(z_lo, g + 1)
                wait(pe, g_ok, g)
                mm_split(nc, banks[W1_BANK][:], k.w1, np.s_[:, :], zT, np.s_[:, g % 2]).then_inc(w1_mm, 1)

            def shared_w2(g):
                pe.wait_ge(g_ok, g + 1)
                if g == 0:
                    pe.wait_ge(b1_ok, 1)
                wait(pe, res_ok, g)
                for b in range(GRP):
                    last = nc.tensor.matmul(banks[W2_BANK][:, b * 128:(b + 1) * 128], gT[:, g % 2, b, :], k.w2[:],
                                            start=True, stop=True)
                last.then_inc(w2_mm, 1)

            def experts_w1():
                pe.wait_ge(ze_ok, NGRP)
                pe.wait_ge(w1e_ok, NEXP // EQ)
                for e in range(NEXP):
                    last = nc.tensor.matmul(banks[E1_BANK][:, e * NSEQ:(e + 1) * NSEQ], w1e[:, e, :], zE[:, :, e],
                                            start=True, stop=True)
                last.then_inc(e1_mm, 1)

            def experts_w2():
                pe.wait_ge(ld_w2e, 16)
                pe.wait_ge(e1_g, 1)
                for c in range(NEXP // EQ):
                    for i in range(EQ):
                        last = nc.tensor.matmul(
                            banks[E2_BANK][QUADRANT * i:QUADRANT * (i + 1), c * 128:(c + 1) * 128],
                            hE[:, c * EQ + i, :], w2e[:, c * EQ + i, :], start=True, stop=True)
                last.then_inc(e2_mm, 1)

            ticks([(last_group(experts_w2), 10), (shared_w2, 6), (later_fc2, 1), (later_hidden, 0),
                   (shared_w1, 5), (z_transposes, 4), (last_group(experts_w1), 5), (first(shift_products), 3)])

        @block.scalar
        def _(act):
            def normal(g, i, dst, src):
                act.wait_ge(shift_ok[i], g + 1)
                for b in range(GRP):
                    s = g * GRP + b
                    last = nc.scalar.activation(dst[:, b], src[:, b], ACT.Identity, bias=shift[:, i, s:s + 1],
                                                scale=rstd[:, i, s:s + 1])
                last.then_inc(nrm[i], 1)

            def outer_normal(g):
                normal(g, 1, X4[:, seqs(g)], N3[:, g % 2])

            def z_normal(g):
                wait(act, zT_mm, g - 1)
                normal(g, 2, N5[:, g % 2], X4[:, seqs(g)])

            def output(g):
                normal(g, 3, res[:, seqs(g)], res[:, seqs(g)])

            def later_gelu(g):
                if g >= HIDDEN_AHEAD:
                    gelu_hidden(k, act, g)

            def z_high(g):
                act.wait_ge(zT_mm, g + 1)
                wait(act, w1_mm, g - 1)
                nc.scalar.activation(zT.hi[:, g % 2], quarter(ZT_BANK), ACT.Copy).then_inc(z_hi, 1)

            def gelu_shared(g):
                if g == 0:
                    act.wait_ge(zeroed, 3)
                    act.wait_ge(b1_ok, 1)
                act.wait_ge(w1_mm, g + 1)
                wait(act, w2_mm, g - 1)
                nc.scalar.activation(gT[:, g % 2, :, NEXP:], quarter(W1_BANK)[:, :, NEXP:], ACT.Gelu,
                                     bias=b1[:, NEXP:NEXP + 1]).then_inc(g_ok, 1)

            def gelu_experts():
                act.wait_ge(e1_b, 1)
                nc.scalar.activation(hE[:, :, 0:NSEQ], hE_in[:], ACT.Gelu).then_inc(e1_g, 1)

            ticks([(later_gelu, 0), (z_normal, 3), (last_group(gelu_experts), 5), (output, 8),
                   (outer_normal, 2), (gelu_shared, 4), (z_high, 3)])

        @block.vector
        def _(vec):
            links = count(1)

            def statistics(g, i, src):
                for b in range(GRP):
                    last = nc.vector.bn_stats(stats[:, i, g * GRP + b], src[:, b])
                last.then_inc(link, 1)
                vec.wait_ge(link, next(links))
                for b in range(g * GRP, (g + 1) * GRP):
                    last = nc.vector.bn_aggr(mv[:, i, b], stats[:, i, b])
                last.then_inc(link, 1)
                vec.wait_ge(link, next(links))
                nc.vector.tensor_scalar(mv[:, i, seqs(g), 1], mv[:, i, seqs(g), 1], EPS, None,
                                        ALU.add).then_inc(mvs[i], 1)

            def mean_shift(g, i):
                vec.wait_ge(rstd_ok[i], g + 1)
                nc.vector.scalar_tensor_tensor(shift[:, i, seqs(g)], mv[:, i, seqs(g), 0], -1.0, rstd[:, i, seqs(g)],
                                               ALU.mult, ALU.mult).then_inc(shift_ok[i], 1)

            def residual3(g):
                vec.wait_ge(k.fc2_mm, g + 1)
                wait(vec, nrm[0], g - 1)
                nc.vector.tensor_tensor(R[:, g % 2], quarter(FC2_BANK), k.xres[:, seqs(g), :],
                                        ALU.add).then_inc(r_ok, 1)
                vec.wait_ge(r_ok, g + 1)
                statistics(g, 0, R[:, g % 2])

            def first_biases():
                vec.wait_ge(b1_mm, 1)
                nc.vector.tensor_tensor(b1[:], banks[B1_BANK][:, 0:NEXP + 1], k.b1_raw[:], ALU.add).then_inc(b1_ok, 1)

            def gained(g):
                vec.wait_ge(mvs[0], g + 1)
                wait(vec, nrm[1], g - 1)
                for b in range(GRP):
                    last = nc.vector.scalar_tensor_tensor(N3[:, g % 2, b], R[:, g % 2, b],
                                                          mv[:, 0, g * GRP + b, 0:1], k.ln3_g[:],
                                                          ALU.subtract, ALU.mult)
                last.then_inc(nrm[0], 1)

            def outer_sums(g):
                vec.wait_ge(nrm[0], g + 1)
                vec.wait_ge(rstd_ok[0], g + 1)
                for b in range(GRP):
                    s = g * GRP + b
                    last = nc.vector.scalar_tensor_tensor(N3[:, g % 2, b], N3[:, g % 2, b], rstd[:, 0, s:s + 1],
                                                          k.x1[:, s, :], ALU.mult, ALU.add)
                last.then_inc(x4a, 1)
                vec.wait_ge(x4a, g + 1)
                statistics(g, 1, N3[:, g % 2])

            def x4_statistics(g):
                vec.wait_ge(nrm[1], g + 1)
                statistics(g, 2, X4[:, seqs(g)])

            def z_low(g):
                vec.wait_ge(z_hi, g + 1)
                wait(vec, w1_mm, g - 1)
                nc.vector.tensor_tensor(zT.lo[:, g % 2], quarter(ZT_BANK), f32(zT.hi[:, g % 2]),
                                        ALU.subtract).then_inc(z_lo, 1)
                nc.vector.tensor_copy(zE[:, seqs(g), :], quarter(ZT_BANK)[:, :, 0:NEXP]).then_inc(ze_ok, 1)

            def output_statistics(g):
                vec.wait_ge(w2_mm, g + 1)
                vec.wait_ge(x4b, g + 1)
                nc.vector.tensor_tensor(res[:, seqs(g), :], quarter(W2_BANK), X4[:, seqs(g)],
                                        ALU.add).then_inc(res_ok, 1)
                vec.wait_ge(res_ok, g + 1)
                statistics(g, 3, res[:, seqs(g)])

            def experts_bias():
                vec.wait_ge(e1_mm, 1)
                nc.vector.tensor_tensor(hE_in[:], banks[E1_BANK][:, 0:NEXP * NSEQ].rearrange("p (e b) -> p e b", e=NEXP),
                                        b1[:, 0:NEXP].unsqueeze(2).to_broadcast([128, NEXP, NSEQ]),
                                        ALU.add).then_inc(e1_b, 1)

            def experts_sums():
                vec.wait_ge(e2_mm, 1)
                vec.wait_ge(xe_in, 16 * EQ)
                nc.vector.tensor_tensor(rE[:], quarter(E2_BANK), xE[:], ALU.add).then_inc(re_ok, 1)
                vec.wait_ge(re_ok, 1)
                for c in range(NEXP // EQ):
                    last = nc.vector.bn_stats(stats_e[:, c], rE[:, c])
                last.then_inc(link, 1)
                vec.wait_ge(link, next(links))
                for c in range(NEXP // EQ):
                    last = nc.vector.bn_aggr(mv_e[:, c], stats_e[:, c])
                last.then_inc(link, 1)
                vec.wait_ge(link, next(links))
                nc.vector.tensor_scalar(mv_e[:, :, 1], mv_e[:, :, 1], EPS, None, ALU.add).then_inc(mv_e_ok, 1)

            def experts_output():
                vec.wait_ge(rstd_e_ok, 1)
                for c in range(NEXP // EQ):
                    last = nc.vector.tensor_scalar(rE[:, c], rE[:, c], mv_e[:, c, 0:1], rstd_e[:, c:c + 1],
                                                   ALU.subtract, ALU.mult)
                last.then_inc(ne_ok, 1)

            ticks([(last_group(experts_bias), 4), (first(first_biases), 4), (x4_statistics, 2),
                   (lambda g: mean_shift(g, 3), 7), (gained, 1), (lambda g: mean_shift(g, 2), 2),
                   (outer_sums, 1), (z_low, 3), (lambda g: mean_shift(g, 1), 1), (output_statistics, 4),
                   (residual3, 0)])
            experts_sums()
            experts_output()

        @block.gpsimd
        def _(pool):
            nc.gpsimd.memset(gT[:], 0.0).then_inc(zeroed, 1)
            nc.gpsimd.memset(hE[:], 0.0).then_inc(zeroed, 1)
            nc.gpsimd.memset(xE[:], 0.0).then_inc(zeroed, 1)

            def row(r):
                return r[:].unsqueeze(1).to_broadcast([128, GRP, 128])

            def inverse_deviation(g, i):
                pool.wait_ge(mvs[i], g + 1)
                nc.gpsimd.tensor_tensor(rstd[:, i, seqs(g)], mv[:, i, seqs(g), 1], k.half_neg[:, 0:GRP],
                                        ALU.pow).then_inc(rstd_ok[i], 1)

            def second_bias(g):
                pool.wait_ge(nrm[2], g + 1)
                nc.gpsimd.tensor_tensor(X4[:, seqs(g)], X4[:, seqs(g)], row(k.bias2), ALU.add).then_inc(x4b, 1)

            def experts_gain(g):
                if g == 0:
                    pool.wait_ge(b1_mm, 1)
                es = slice(g * EQ, (g + 1) * EQ)
                nc.gpsimd.tensor_tensor(w1e[:, es, :], w1e[:, es, :],
                                        k.gainT[:, es].unsqueeze(2).to_broadcast([128, EQ, 128]),
                                        ALU.mult).then_inc(w1e_ok, 1)

            ticks([(lambda g: inverse_deviation(g, 2), 2), (lambda g: inverse_deviation(g, 1), 1),
                   (experts_gain, 3), (second_bias, 3), (lambda g: inverse_deviation(g, 0), 0),
                   (lambda g: inverse_deviation(g, 3), 9)])
            pool.wait_ge(mv_e_ok, 1)
            nc.gpsimd.tensor_tensor(rstd_e[:], mv_e[:, :, 1], k.half_neg[:, 0:NEXP // EQ],
                                    ALU.pow).then_inc(rstd_e_ok, 1)


def build(nc, io):
    k = Kernel(nc, io)
    with ExitStack() as ctx:
        allocate(k, ctx)
        allocate_feed_forward(k, ctx)
        allocate_attention(k, ctx)
        setup_and_mixer(k)
        allocate_late(k, ctx)
        attentions(k)
        feed_forward(k)


def layouts(a):
    tall = {"x": a["x"], "xT": a["x"].transpose(2, 0, 1),
            "ctxT": a["ctx_1024"].transpose(2, 0, 1).reshape(D, T),
            "mask": a["mask_BxS2_bk0"],
            "short_wT": a["L0_attn_short_w"].T, "short_bT": a["L0_attn_short_b"].reshape(3, D).T,
            "b_inT": a["L0_attn_b_in"].reshape(3, D).T,
            "fc1_bT": a["L0_xattn_fc1_b"].reshape(FF // D, D).T, "b1_eT": a["L0_ffn_b1_e"].T,
            "g_eT": a["L0_ffn_g_e"].T, "b_eT": a["L0_ffn_b_e"].T}
    for n in "W_in short_w inner_w inner_b W_out b_out".split():
        tall[n] = a["L0_attn_" + n]
    for s in ("sa", "ca"):
        for n in ("wq", "wk"):
            tall[f"{s}_{n}T"] = a[f"L0_xattn_{s}_{n}"].T
        for n in ("wv", "wo", "bo"):
            tall[f"{s}_{n}"] = a[f"L0_xattn_{s}_{n}"]
    for n in "ln1_g ln1_b ln2_g ln2_b ln3_g ln3_b fc1_w fc2_w fc2_b".split():
        tall[n] = a["L0_xattn_" + n]
    for n in "W1_e W2_e b2_e g_s b_s W1_s b1_s W2_s b2_s".split():
        tall[n] = a["L0_ffn_" + n]
    return {n: np.ascontiguousarray(v) for n, v in tall.items()}


def kernel(**inputs):
    from concourse import bacc
    from concourse.bass_utils import run_bass_kernel_spmd

    nc = bacc.Bacc("TRN2", target_bir_lowering=False, num_devices=1)
    arrays = layouts({n: np.asarray(v) for n, v in inputs.items()})
    io = {n: nc.dram_tensor("in_" + n, v.shape, mybir.dt.from_np(v.dtype), kind="ExternalInput").ap()
          for n, v in arrays.items()}
    io["scratch"] = nc.dram_tensor("experts_out", (NSEQ, NEXP, D), F32, kind="Internal").ap()
    io["out"] = nc.dram_tensor("out", (NSEQ, L, D), F32, kind="ExternalOutput").ap()
    build(nc, io)
    result = run_bass_kernel_spmd(nc, [{"in_" + n: v for n, v in arrays.items()}], core_ids=[0])
    return result.results[0]["out"]
```
